# Optimizing a Trainium2 kernel written in Bass

```python
import numpy as np
import jax
import jax.numpy as jnp

def _softmax(x, axis=-1):
    return jax.nn.softmax(x, axis=axis)

def _gelu(x):
    return jax.nn.gelu(x, approximate=True)

def _silu(x):
    return jax.nn.silu(x)

def _sigmoid(x):
    return jax.nn.sigmoid(x)

def _layernorm(x, axis=-1, eps=1e-05):
    m = jnp.mean(x, axis=axis, keepdims=True)
    v = jnp.var(x, axis=axis, keepdims=True)
    return (x - m) / jnp.sqrt(v + eps)

def _scatter_add(tgt, idx, src, axis=0):
    return tgt.at[idx].add(src)

def _segment_sum(src, seg, n):
    return jax.ops.segment_sum(src, seg, n)
kernel_name = 'mk_hybrid_d2_jaxref_r8_b82ba6'

def setup_inputs(seed: int=0):
    np.random.seed(seed)
    _w = jnp.asarray

    def _L0_attn_a_setup():
        import jax, jax.numpy as jnp
        import numpy as np
        H = 16
        DN = 128
        DR = 64
        DV = 128
        R = 64
        DIM = 256
        THETA = 10000.0
        EPS = 1e-06
        SCALE = (DN + DR) ** (-0.5)

        def rms_norm(x, w):
            var = jnp.mean(x * x, axis=-1, keepdims=True)
            return x * jax.lax.rsqrt(var + EPS) * w

        def rope_cos_sin(seqlen):
            inv = 1.0 / THETA ** (jnp.arange(0, DR, 2, dtype=jnp.float32) / DR)
            ang = jnp.arange(seqlen, dtype=jnp.float32)[:, None] * inv
            return (jnp.cos(ang), jnp.sin(ang))

        def apply_rope(t, cos, sin):
            b, s, h, d = t.shape
            t = t.reshape(b, s, h, d // 2, 2)
            x0, x1 = (t[..., 0], t[..., 1])
            c = cos[None, :, None, :]
            sn = sin[None, :, None, :]
            out = jnp.stack([x0 * c - x1 * sn, x0 * sn + x1 * c], axis=-1)
            return out.reshape(b, s, h, d)
        key = jax.random.key(seed)
        ks = jax.random.split(key, 6)
        b, s = (2, 256)
        sc = lambda n: n ** (-0.5)
        return {'x': jax.random.normal(ks[0], (b, s, DIM), jnp.float32), 'wq': jax.random.normal(ks[1], (DIM, H * (DN + DR)), jnp.float32) * sc(DIM), 'wkv_a': jax.random.normal(ks[2], (DIM, R + DR), jnp.float32) * sc(DIM), 'kv_norm_w': jnp.ones((R,), jnp.float32), 'wkv_b': jax.random.normal(ks[3], (R, H * (DN + DV)), jnp.float32) * sc(R), 'wo': jax.random.normal(ks[4], (H * DV, DIM), jnp.float32) * sc(H * DV)}
    _L0_attn_a_in = _L0_attn_a_setup()

    def _L0_attn_b_setup():
        import jax, jax.numpy as jnp
        import numpy as np
        HEADS = 16
        DIM_HEAD = 128
        SCALE = 16.0
        EPS = 1e-05

        def _layernorm(x, g):
            mu = jnp.mean(x, axis=-1, keepdims=True)
            var = jnp.mean((x - mu) ** 2, axis=-1, keepdims=True)
            return (x - mu) * jax.lax.rsqrt(var + EPS) * g

        def _l2norm(t):
            return t * jax.lax.rsqrt(jnp.sum(t * t, axis=-1, keepdims=True) + 1e-12)
        key = jax.random.key(seed)
        ks = jax.random.split(key, 5)
        B, N, dim = (2, 256, 256)
        hidden = HEADS * DIM_HEAD
        x = jax.random.normal(ks[0], (B, N, dim), dtype=jnp.float32)
        g_norm = jnp.ones((dim,), dtype=jnp.float32)
        Wq = jax.random.normal(ks[1], (dim, hidden), dtype=jnp.float32) * dim ** (-0.5)
        Wkv = jax.random.normal(ks[2], (dim, 2 * DIM_HEAD), dtype=jnp.float32) * dim ** (-0.5)
        Wout = jax.random.normal(ks[3], (hidden, dim), dtype=jnp.float32) * hidden ** (-0.5)
        g_out = jnp.ones((dim,), dtype=jnp.float32)
        return {'x': x, 'g_norm': g_norm, 'Wq': Wq, 'Wkv': Wkv, 'Wout': Wout, 'g_out': g_out}
    _L0_attn_b_in = _L0_attn_b_setup()

    def _L0_ffn_setup():
        import jax, jax.numpy as jnp
        import numpy as np
        EPS = 1e-07
        CURVATURE = 1.0
        MAX_NORM_RATIO = 0.99
        B, L, N, K = (4, 256, 256, 256)

        def _ternary_init(key, n, k):
            rand = jax.random.normal(key, (n, k), dtype=jnp.float32)
            threshold = 0.5 * jnp.mean(jnp.abs(rand))
            return jnp.where(rand > threshold, 1.0, jnp.where(rand < -threshold, -1.0, 0.0)).astype(jnp.float32)
        key = jax.random.key(seed)
        kx, kw = jax.random.split(key)
        x = jax.random.normal(kx, (B, L, N), dtype=jnp.float32)
        weight = _ternary_init(kw, N, K)
        scale = jnp.full((K,), 1.0 / np.sqrt(N), dtype=jnp.float32)
        return {'x': x, 'weight': weight, 'scale': scale}
    _L0_ffn_in = _L0_ffn_setup()

    def _L1_attn_a_setup():
        import jax, jax.numpy as jnp
        import numpy as np
        B, T, D = (4, 256, 256)
        H = 16
        KD = D // 2
        VD = D
        DK = KD // H
        DV = VD // H
        LR = 16
        EPS = 1e-05
        GATE_LOGIT_NORMALIZER = 16.0
        key = jax.random.key(seed)
        ks = jax.random.split(key, 9)

        def w(k, shape):
            fan_in = shape[0]
            return (jax.random.normal(k, shape, jnp.float32) * fan_in ** (-0.5)).astype(jnp.float32)
        return {'x': jax.random.normal(ks[0], (B, T, D), jnp.float32), 'Wq': w(ks[1], (D, KD)), 'Wk': w(ks[2], (D, KD)), 'Wv': w(ks[3], (D, VD)), 'Wg': w(ks[4], (D, VD)), 'Wgk1': w(ks[5], (D, LR)), 'Wgk2': w(ks[6], (LR, KD)), 'bgk2': jnp.zeros((KD,), jnp.float32), 'norm_w': jnp.ones((DV,), jnp.float32), 'Wo': w(ks[7], (VD, D))}
    _L1_attn_a_in = _L1_attn_a_setup()

    def _L1_attn_b_setup():
        import jax, jax.numpy as jnp
        import numpy as np
        D_MODEL = 256
        NUM_HEADS = 16
        D_KV = D_MODEL // NUM_HEADS
        THETA = 10000.0
        N_LORA = 4
        RANK = 16
        BATCH = 2
        SEQ = 256

        def _adapter_ids(starts, batch):
            ids = jnp.searchsorted(starts, jnp.arange(batch), side='right') - 1
            return jnp.clip(ids, 0, starts.shape[0] - 1)

        def _multilora(x, ids, W, A, B):
            base = jnp.einsum('bsd,od->bso', x, W)
            Ai, Bi = (A[ids], B[ids])
            low = jnp.einsum('bsd,brd->bsr', x, Ai)
            return base + jnp.einsum('bsr,bor->bso', low, Bi)

        def _rope(x):
            d = x.shape[-1]
            pos = jnp.arange(x.shape[-2], dtype=jnp.float32)
            inv_freq = THETA ** (-jnp.arange(0, d, 2, dtype=jnp.float32) / d)
            ang = pos[:, None] * inv_freq[None, :]
            cos, sin = (jnp.cos(ang), jnp.sin(ang))
            x1, x2 = (x[..., 0::2], x[..., 1::2])
            o1 = x1 * cos - x2 * sin
            o2 = x1 * sin + x2 * cos
            return jnp.stack([o1, o2], axis=-1).reshape(x.shape)
        key = jax.random.key(seed)
        ks = jax.random.split(key, 16)
        s = 0.02
        inp = {'x': jax.random.normal(ks[0], (BATCH, SEQ, D_MODEL), jnp.float32), 'lora_start_indices': jnp.sort(jax.random.randint(ks[1], (N_LORA,), 0, BATCH)), 'Wq': jax.random.normal(ks[2], (D_MODEL, D_MODEL), jnp.float32) * s, 'Aq': jax.random.normal(ks[3], (N_LORA, RANK, D_MODEL), jnp.float32) * s, 'Bq': jax.random.normal(ks[4], (N_LORA, D_MODEL, RANK), jnp.float32) * s, 'Wk': jax.random.normal(ks[5], (D_MODEL, D_MODEL), jnp.float32) * s, 'Ak': jax.random.normal(ks[6], (N_LORA, RANK, D_MODEL), jnp.float32) * s, 'Bk': jax.random.normal(ks[7], (N_LORA, D_MODEL, RANK), jnp.float32) * s, 'Wv': jax.random.normal(ks[8], (D_MODEL, D_MODEL), jnp.float32) * s, 'Av': jax.random.normal(ks[9], (N_LORA, RANK, D_MODEL), jnp.float32) * s, 'Bv': jax.random.normal(ks[10], (N_LORA, D_MODEL, RANK), jnp.float32) * s, 'Wo': jax.random.normal(ks[11], (D_MODEL, D_MODEL), jnp.float32) * s, 'Ao': jax.random.normal(ks[12], (N_LORA, RANK, D_MODEL), jnp.float32) * s, 'Bo': jax.random.normal(ks[13], (N_LORA, D_MODEL, RANK), jnp.float32) * s}
        return inp
    _L1_attn_b_in = _L1_attn_b_setup()

    def _L1_ffn_setup():
        import jax, jax.numpy as jnp
        import numpy as np
        B, L, D = (4, 256, 256)
        S, K, NB = (16, 4, 2)
        H = D // 64
        EPS = 1e-06

        def _rms(x, w):
            return x * jax.lax.rsqrt(jnp.mean(x * x, axis=-1, keepdims=True) + EPS) * w
        key = jax.random.key(seed)
        ks = jax.random.split(key, 8)
        g = lambda k, shape, s: jax.random.normal(k, shape, dtype=jnp.float32) * s
        return {'x': g(ks[0], (B, L, D), 1.0), 'workspace': g(ks[1], (S, D), 0.02), 'compete_w': g(ks[2], (S, D), 0.02), 'compete_b': jnp.zeros((S,), jnp.float32), 'write_w': g(ks[3], (D, D), 0.02), 'write_b': jnp.zeros((D,), jnp.float32), 'in_proj_w': g(ks[4], (3 * D, D), 0.02), 'in_proj_b': jnp.zeros((3 * D,), jnp.float32), 'out_proj_w': g(ks[5], (D, D), 0.02), 'out_proj_b': jnp.zeros((D,), jnp.float32), 'ig_w': g(ks[6], (1, D), 0.02), 'ig_b': jnp.zeros((1,), jnp.float32), 'norm_pre_w': jnp.ones((D,), jnp.float32), 'norm_post_w': jnp.ones((D,), jnp.float32)}
    _L1_ffn_in = _L1_ffn_setup()
    _d = {'L0_attn_a_x': _L0_attn_a_in['x'], 'L0_attn_a_wq': _L0_attn_a_in['wq'], 'L0_attn_a_wkv_a': _L0_attn_a_in['wkv_a'], 'L0_attn_a_kv_norm_w': _L0_attn_a_in['kv_norm_w'], 'L0_attn_a_wkv_b': _L0_attn_a_in['wkv_b'], 'L0_attn_a_wo': _L0_attn_a_in['wo'], 'L0_attn_b_g_norm': _L0_attn_b_in['g_norm'], 'L0_attn_b_Wq': _L0_attn_b_in['Wq'], 'L0_attn_b_Wkv': _L0_attn_b_in['Wkv'], 'L0_attn_b_Wout': _L0_attn_b_in['Wout'], 'L0_attn_b_g_out': _L0_attn_b_in['g_out'], 'L0_ffn_weight': _L0_ffn_in['weight'], 'L0_ffn_scale': _L0_ffn_in['scale'], 'L1_attn_a_Wq': _L1_attn_a_in['Wq'], 'L1_attn_a_Wk': _L1_attn_a_in['Wk'], 'L1_attn_a_Wv': _L1_attn_a_in['Wv'], 'L1_attn_a_Wg': _L1_attn_a_in['Wg'], 'L1_attn_a_Wgk1': _L1_attn_a_in['Wgk1'], 'L1_attn_a_Wgk2': _L1_attn_a_in['Wgk2'], 'L1_attn_a_bgk2': _L1_attn_a_in['bgk2'], 'L1_attn_a_norm_w': _L1_attn_a_in['norm_w'], 'L1_attn_a_Wo': _L1_attn_a_in['Wo'], 'L1_attn_b_lora_start_indices': _L1_attn_b_in['lora_start_indices'], 'L1_attn_b_Wq': _L1_attn_b_in['Wq'], 'L1_attn_b_Aq': _L1_attn_b_in['Aq'], 'L1_attn_b_Bq': _L1_attn_b_in['Bq'], 'L1_attn_b_Wk': _L1_attn_b_in['Wk'], 'L1_attn_b_Ak': _L1_attn_b_in['Ak'], 'L1_attn_b_Bk': _L1_attn_b_in['Bk'], 'L1_attn_b_Wv': _L1_attn_b_in['Wv'], 'L1_attn_b_Av': _L1_attn_b_in['Av'], 'L1_attn_b_Bv': _L1_attn_b_in['Bv'], 'L1_attn_b_Wo': _L1_attn_b_in['Wo'], 'L1_attn_b_Ao': _L1_attn_b_in['Ao'], 'L1_attn_b_Bo': _L1_attn_b_in['Bo'], 'L1_ffn_workspace': _L1_ffn_in['workspace'], 'L1_ffn_compete_w': _L1_ffn_in['compete_w'], 'L1_ffn_compete_b': _L1_ffn_in['compete_b'], 'L1_ffn_write_w': _L1_ffn_in['write_w'], 'L1_ffn_write_b': _L1_ffn_in['write_b'], 'L1_ffn_in_proj_w': _L1_ffn_in['in_proj_w'], 'L1_ffn_in_proj_b': _L1_ffn_in['in_proj_b'], 'L1_ffn_out_proj_w': _L1_ffn_in['out_proj_w'], 'L1_ffn_out_proj_b': _L1_ffn_in['out_proj_b'], 'L1_ffn_ig_w': _L1_ffn_in['ig_w'], 'L1_ffn_ig_b': _L1_ffn_in['ig_b'], 'L1_ffn_norm_pre_w': _L1_ffn_in['norm_pre_w'], 'L1_ffn_norm_post_w': _L1_ffn_in['norm_post_w']}
    _x0 = _d['L0_attn_a_x']
    _d['L0_attn_a_x'] = jax.random.normal(jax.random.fold_in(jax.random.key(seed), 1), (4, 512, 256), dtype=_x0.dtype)
    del _x0
    return _d

def reference(L0_attn_a_x, L0_attn_a_wq, L0_attn_a_wkv_a, L0_attn_a_kv_norm_w, L0_attn_a_wkv_b, L0_attn_a_wo, L0_attn_b_g_norm, L0_attn_b_Wq, L0_attn_b_Wkv, L0_attn_b_Wout, L0_attn_b_g_out, L0_ffn_weight, L0_ffn_scale, L1_attn_a_Wq, L1_attn_a_Wk, L1_attn_a_Wv, L1_attn_a_Wg, L1_attn_a_Wgk1, L1_attn_a_Wgk2, L1_attn_a_bgk2, L1_attn_a_norm_w, L1_attn_a_Wo, L1_attn_b_lora_start_indices, L1_attn_b_Wq, L1_attn_b_Aq, L1_attn_b_Bq, L1_attn_b_Wk, L1_attn_b_Ak, L1_attn_b_Bk, L1_attn_b_Wv, L1_attn_b_Av, L1_attn_b_Bv, L1_attn_b_Wo, L1_attn_b_Ao, L1_attn_b_Bo, L1_ffn_workspace, L1_ffn_compete_w, L1_ffn_compete_b, L1_ffn_write_w, L1_ffn_write_b, L1_ffn_in_proj_w, L1_ffn_in_proj_b, L1_ffn_out_proj_w, L1_ffn_out_proj_b, L1_ffn_ig_w, L1_ffn_ig_b, L1_ffn_norm_pre_w, L1_ffn_norm_post_w):

    def _L0_attn_a_ref(x, wq, wkv_a, kv_norm_w, wkv_b, wo):
        import jax, jax.numpy as jnp
        import numpy as np
        H = 16
        DN = 128
        DR = 64
        DV = 128
        R = 64
        DIM = 256
        THETA = 10000.0
        EPS = 1e-06
        SCALE = (DN + DR) ** (-0.5)

        def rms_norm(x, w):
            var = jnp.mean(x * x, axis=-1, keepdims=True)
            return x * jax.lax.rsqrt(var + EPS) * w

        def rope_cos_sin(seqlen):
            inv = 1.0 / THETA ** (jnp.arange(0, DR, 2, dtype=jnp.float32) / DR)
            ang = jnp.arange(seqlen, dtype=jnp.float32)[:, None] * inv
            return (jnp.cos(ang), jnp.sin(ang))

        def apply_rope(t, cos, sin):
            b, s, h, d = t.shape
            t = t.reshape(b, s, h, d // 2, 2)
            x0, x1 = (t[..., 0], t[..., 1])
            c = cos[None, :, None, :]
            sn = sin[None, :, None, :]
            out = jnp.stack([x0 * c - x1 * sn, x0 * sn + x1 * c], axis=-1)
            return out.reshape(b, s, h, d)
        b, s, _ = x.shape
        cos, sin = rope_cos_sin(s)
        q = (x @ wq).reshape(b, s, H, DN + DR)
        q_nope, q_pe = (q[..., :DN], q[..., DN:])
        q_pe = apply_rope(q_pe, cos, sin)
        kv_a = x @ wkv_a
        kv, k_pe = (kv_a[..., :R], kv_a[..., R:])
        k_pe = apply_rope(k_pe[:, :, None, :], cos, sin)
        kv = rms_norm(kv, kv_norm_w)
        kvb = (kv @ wkv_b).reshape(b, s, H, DN + DV)
        k_nope, v = (kvb[..., :DN], kvb[..., DN:])
        qf = jnp.concatenate([q_nope, q_pe], axis=-1)
        kf = jnp.concatenate([k_nope, jnp.broadcast_to(k_pe, (b, s, H, DR))], axis=-1)
        scores = jnp.einsum('bshd,bthd->bhst', qf, kf) * SCALE
        mask = jnp.tril(jnp.ones((s, s), bool))
        scores = jnp.where(mask[None, None], scores, jnp.finfo(scores.dtype).min)
        p = jax.nn.softmax(scores, axis=-1)
        out = jnp.einsum('bhst,bthd->bshd', p, v).reshape(b, s, H * DV)
        return out @ wo

    def _L0_attn_b_ref(x, g_norm, Wq, Wkv, Wout, g_out):
        import jax, jax.numpy as jnp
        import numpy as np
        HEADS = 16
        DIM_HEAD = 128
        SCALE = 16.0
        EPS = 1e-05

        def _layernorm(x, g):
            mu = jnp.mean(x, axis=-1, keepdims=True)
            var = jnp.mean((x - mu) ** 2, axis=-1, keepdims=True)
            return (x - mu) * jax.lax.rsqrt(var + EPS) * g

        def _l2norm(t):
            return t * jax.lax.rsqrt(jnp.sum(t * t, axis=-1, keepdims=True) + 1e-12)
        B, N, dim = x.shape
        xn = _layernorm(x, g_norm)
        q = xn @ Wq
        kv = xn @ Wkv
        k, v = (kv[..., :DIM_HEAD], kv[..., DIM_HEAD:])
        q = q.reshape(B, N, HEADS, DIM_HEAD).transpose(0, 2, 1, 3)
        q = q * SCALE
        q = _l2norm(q)
        k = _l2norm(k)
        s = jnp.sqrt(SCALE).astype(x.dtype)
        q = q * s
        k = k * s
        sim = jnp.einsum('bhid,bjd->bhij', q, k)
        attn = jax.nn.softmax(sim.astype(jnp.float32), axis=-1).astype(sim.dtype)
        out = jnp.einsum('bhij,bjd->bhid', attn, v)
        out = out.transpose(0, 2, 1, 3).reshape(B, N, HEADS * DIM_HEAD)
        out = out @ Wout
        return _layernorm(out, g_out)

    def _L0_ffn_ref(x, weight, scale):
        import jax, jax.numpy as jnp
        import numpy as np
        EPS = 1e-07
        CURVATURE = 1.0
        MAX_NORM_RATIO = 0.99
        B, L, N, K = (4, 256, 256, 256)

        def _ternary_init(key, n, k):
            rand = jax.random.normal(key, (n, k), dtype=jnp.float32)
            threshold = 0.5 * jnp.mean(jnp.abs(rand))
            return jnp.where(rand > threshold, 1.0, jnp.where(rand < -threshold, -1.0, 0.0)).astype(jnp.float32)
        sqrt_c = jnp.sqrt(jnp.float32(CURVATURE))
        out = jnp.einsum('bln,nk->blk', x, weight) * scale
        v_norm = jnp.maximum(jnp.linalg.norm(out, axis=-1, keepdims=True), EPS)
        scaled_norm = sqrt_c * v_norm
        out = out * (jnp.tanh(scaled_norm) / (scaled_norm + EPS))
        max_norm = MAX_NORM_RATIO / sqrt_c
        o_norm = jnp.maximum(jnp.linalg.norm(out, axis=-1, keepdims=True), EPS)
        out = out * jnp.minimum(max_norm / o_norm, 1.0)
        return out.astype(x.dtype)

    def _L1_attn_a_ref(x, Wq, Wk, Wv, Wg, Wgk1, Wgk2, bgk2, norm_w, Wo):
        import jax, jax.numpy as jnp
        import numpy as np
        B, T, D = (4, 256, 256)
        H = 16
        KD = D // 2
        VD = D
        DK = KD // H
        DV = VD // H
        LR = 16
        EPS = 1e-05
        GATE_LOGIT_NORMALIZER = 16.0
        b, t, _ = x.shape
        dv = norm_w.shape[0]
        vd = Wv.shape[1]
        h = vd // dv
        dk = Wq.shape[1] // h
        scale = dk ** (-0.5)
        q = (x @ Wq).reshape(b, t, h, dk) * scale
        k = (x @ Wk).reshape(b, t, h, dk)
        v = (x @ Wv).reshape(b, t, h, dv)
        gk = jax.nn.log_sigmoid(x @ Wgk1 @ Wgk2 + bgk2) / GATE_LOGIT_NORMALIZER
        gk = gk.reshape(b, t, h, dk)
        qT = jnp.moveaxis(q, 1, 0)
        kT = jnp.moveaxis(k, 1, 0)
        vT = jnp.moveaxis(v, 1, 0)
        gT = jnp.moveaxis(gk, 1, 0)

        def step(S, inp):
            qt, kt, vt, gt = inp
            S = S * jnp.exp(gt)[..., None] + kt[..., None] * vt[..., None, :]
            ot = jnp.einsum('bhk,bhkv->bhv', qt, S)
            return (S, ot)
        S0 = jnp.zeros((b, h, dk, dv), x.dtype)
        _, o = jax.lax.scan(step, S0, (qT, kT, vT, gT))
        o = jnp.moveaxis(o, 0, 1)
        g = (x @ Wg).reshape(b, t, h, dv)
        o = o * jax.lax.rsqrt(jnp.mean(o * o, axis=-1, keepdims=True) + EPS) * norm_w
        o = o * (g * jax.nn.sigmoid(g))
        return o.reshape(b, t, vd) @ Wo

    def _L1_attn_b_ref(x, lora_start_indices, Wq, Aq, Bq, Wk, Ak, Bk, Wv, Av, Bv, Wo, Ao, Bo):
        import jax, jax.numpy as jnp
        import numpy as np
        D_MODEL = 256
        NUM_HEADS = 16
        D_KV = D_MODEL // NUM_HEADS
        THETA = 10000.0
        N_LORA = 4
        RANK = 16
        BATCH = 2
        SEQ = 256

        def _adapter_ids(starts, batch):
            ids = jnp.searchsorted(starts, jnp.arange(batch), side='right') - 1
            return jnp.clip(ids, 0, starts.shape[0] - 1)

        def _multilora(x, ids, W, A, B):
            base = jnp.einsum('bsd,od->bso', x, W)
            Ai, Bi = (A[ids], B[ids])
            low = jnp.einsum('bsd,brd->bsr', x, Ai)
            return base + jnp.einsum('bsr,bor->bso', low, Bi)

        def _rope(x):
            d = x.shape[-1]
            pos = jnp.arange(x.shape[-2], dtype=jnp.float32)
            inv_freq = THETA ** (-jnp.arange(0, d, 2, dtype=jnp.float32) / d)
            ang = pos[:, None] * inv_freq[None, :]
            cos, sin = (jnp.cos(ang), jnp.sin(ang))
            x1, x2 = (x[..., 0::2], x[..., 1::2])
            o1 = x1 * cos - x2 * sin
            o2 = x1 * sin + x2 * cos
            return jnp.stack([o1, o2], axis=-1).reshape(x.shape)
        b, s, _ = x.shape
        ids = _adapter_ids(lora_start_indices, b)
        Q = _multilora(x, ids, Wq, Aq, Bq)
        K = _multilora(x, ids, Wk, Ak, Bk)
        V = _multilora(x, ids, Wv, Av, Bv)
        split = lambda t: t.reshape(b, s, NUM_HEADS, D_KV).transpose(0, 2, 1, 3)
        Q, K, V = (split(Q), split(K), split(V))
        Q, K = (_rope(Q), _rope(K))
        scores = jnp.einsum('bhqd,bhkd->bhqk', Q, K) / jnp.sqrt(jnp.asarray(D_KV, x.dtype))
        causal = jnp.tril(jnp.ones((s, s), bool))
        scores = jnp.where(causal, scores, jnp.asarray(-jnp.inf, scores.dtype))
        attn = jax.nn.softmax(scores, axis=-1)
        out = jnp.einsum('bhqk,bhkd->bhqd', attn, V)
        out = out.transpose(0, 2, 1, 3).reshape(b, s, D_MODEL)
        return _multilora(out, ids, Wo, Ao, Bo)

    def _L1_ffn_ref(x, workspace, compete_w, compete_b, write_w, write_b, in_proj_w, in_proj_b, out_proj_w, out_proj_b, ig_w, ig_b, norm_pre_w, norm_post_w):
        import jax, jax.numpy as jnp
        import numpy as np
        B, L, D = (4, 256, 256)
        S, K, NB = (16, 4, 2)
        H = D // 64
        EPS = 1e-06

        def _rms(x, w):
            return x * jax.lax.rsqrt(jnp.mean(x * x, axis=-1, keepdims=True) + EPS) * w
        Bq, Lq, Dd = x.shape
        hd = Dd // H
        scale = 1.0 / np.sqrt(hd).astype(np.float32)
        ws = jnp.broadcast_to(workspace[None], (Bq, S, Dd))
        wq, wk, wv = (in_proj_w[:Dd], in_proj_w[Dd:2 * Dd], in_proj_w[2 * Dd:])
        bq, bk, bv = (in_proj_b[:Dd], in_proj_b[Dd:2 * Dd], in_proj_b[2 * Dd:])
        k_eff = min(K, Lq)
        for _ in range(NB):
            logits = _rms(x, norm_pre_w) @ compete_w.T + compete_b
            slot_logits = jnp.swapaxes(logits, 1, 2)
            vals, idx = jax.lax.top_k(slot_logits, k_eff)
            wgt = jax.nn.softmax(vals, axis=-1)
            wx = x @ write_w.T + write_b
            gathered = jnp.take_along_axis(wx[:, None], idx[..., None], axis=2)
            written = jnp.einsum('bsk,bskd->bsd', wgt, gathered)
            ws = _rms(ws + written, norm_post_w)
            q = (x @ wq.T + bq).reshape(Bq, Lq, H, hd)
            kk = (ws @ wk.T + bk).reshape(Bq, S, H, hd)
            vv = (ws @ wv.T + bv).reshape(Bq, S, H, hd)
            att = jax.nn.softmax(jnp.einsum('blhd,bshd->bhls', q, kk) * scale, axis=-1)
            ctx = jnp.einsum('bhls,bshd->blhd', att, vv).reshape(Bq, Lq, Dd)
            x_b = ctx @ out_proj_w.T + out_proj_b
            x = _rms(x + x_b, norm_post_w)
            ignition = jax.nn.sigmoid(x @ ig_w.T + ig_b)
        return x
    x = L0_attn_a_x
    x = x + _L0_attn_a_ref(_layernorm(x, axis=-1), L0_attn_a_wq, L0_attn_a_wkv_a, L0_attn_a_kv_norm_w, L0_attn_a_wkv_b, L0_attn_a_wo)
    x = x + _L0_ffn_ref(_layernorm(x, axis=-1), L0_ffn_weight, L0_ffn_scale)
    x = x + _L0_attn_b_ref(_layernorm(x, axis=-1), L0_attn_b_g_norm, L0_attn_b_Wq, L0_attn_b_Wkv, L0_attn_b_Wout, L0_attn_b_g_out)
    x = x + _L0_ffn_ref(_layernorm(x, axis=-1), L0_ffn_weight, L0_ffn_scale)
    x = x + _L1_attn_a_ref(_layernorm(x, axis=-1), L1_attn_a_Wq, L1_attn_a_Wk, L1_attn_a_Wv, L1_attn_a_Wg, L1_attn_a_Wgk1, L1_attn_a_Wgk2, L1_attn_a_bgk2, L1_attn_a_norm_w, L1_attn_a_Wo)
    x = x + _L1_ffn_ref(_layernorm(x, axis=-1), L1_ffn_workspace, L1_ffn_compete_w, L1_ffn_compete_b, L1_ffn_write_w, L1_ffn_write_b, L1_ffn_in_proj_w, L1_ffn_in_proj_b, L1_ffn_out_proj_w, L1_ffn_out_proj_b, L1_ffn_ig_w, L1_ffn_ig_b, L1_ffn_norm_pre_w, L1_ffn_norm_post_w)
    x = x + _L1_attn_b_ref(_layernorm(x, axis=-1), L1_attn_b_lora_start_indices, L1_attn_b_Wq, L1_attn_b_Aq, L1_attn_b_Bq, L1_attn_b_Wk, L1_attn_b_Ak, L1_attn_b_Bk, L1_attn_b_Wv, L1_attn_b_Av, L1_attn_b_Bv, L1_attn_b_Wo, L1_attn_b_Ao, L1_attn_b_Bo)
    x = x + _L1_ffn_ref(_layernorm(x, axis=-1), L1_ffn_workspace, L1_ffn_compete_w, L1_ffn_compete_b, L1_ffn_write_w, L1_ffn_write_b, L1_ffn_in_proj_w, L1_ffn_in_proj_b, L1_ffn_out_proj_w, L1_ffn_out_proj_b, L1_ffn_ig_w, L1_ffn_ig_b, L1_ffn_norm_pre_w, L1_ffn_norm_post_w)
    return x

_drawn_inputs = setup_inputs


def setup_inputs(seed=0):
    import zlib

    import numpy as np

    out = dict(_drawn_inputs(seed))
    spreads = {'L0_attn_a_kv_norm_w': (1.0, 0.2),
     'L0_attn_b_g_norm': (1.0, 0.2),
     'L0_attn_b_g_out': (1.0, 0.2),
     'L0_ffn_scale': (0.0625, 0.574),
     'L1_attn_a_bgk2': (0.0, 0.418),
     'L1_attn_a_norm_w': (1.0, 0.2),
     'L1_ffn_compete_b': (0.0, 0.8),
     'L1_ffn_write_b': (0.0, 0.1),
     'L1_ffn_in_proj_b': (0.0, 0.1),
     'L1_ffn_out_proj_b': (0.0, 0.1),
     'L1_ffn_norm_pre_w': (1.0, 0.6),
     'L1_ffn_norm_post_w': (1.0, 0.2)}
    factors = {'L1_attn_b_Wq': 8.0,
     'L1_attn_b_Aq': 8.0,
     'L1_attn_b_Bq': 8.0,
     'L1_attn_b_Wk': 8.0,
     'L1_attn_b_Ak': 8.0,
     'L1_attn_b_Bk': 8.0,
     'L1_attn_b_Wv': 4.222,
     'L1_attn_b_Av': 8.0,
     'L1_attn_b_Bv': 8.0,
     'L1_attn_b_Wo': 4.248,
     'L1_attn_b_Ao': 8.0,
     'L1_attn_b_Bo': 8.0,
     'L1_ffn_workspace': 8.0}
    for name, (base, spread) in spreads.items():
        noise = np.random.default_rng([zlib.crc32(name.encode()), seed]).standard_normal(out[name].shape)
        drawn = base * np.exp(spread * noise) if base else spread * noise
        out[name] = jnp.asarray(drawn.astype(out[name].dtype))
    for name, factor in factors.items():
        out[name] = (out[name] * factor).astype(out[name].dtype)
    return out
```

```python
from contextlib import ExitStack

import numpy as np

import concourse.bass as bass
from concourse import mybir

F32 = mybir.dt.float32
BF16 = mybir.dt.bfloat16
ALU = mybir.AluOpType
ACT = mybir.ActivationFunctionType
AX = mybir.AxisListType

P = 128
B, S, D = 4, 512, 256
TI = S // P
NT = B * TI
DC = D // P
LN_EPS = 1e-5
NEG = -1e30

CAUSAL_ORDER = (3, 2, 0, 1)
CAUSAL_COL = {3: 0, 2: S, 0: S + 3 * P, 1: 2 * S}
CAUSAL_COLS = 2 * S + 2 * P
CAUSAL_BANK = {3: 0, 2: 1, 0: 1, 1: 2}


class Kit:

    def __init__(self, nc, ctx):
        self.nc, self.ctx = nc, ctx
        self.sems = []

    def sb(self, name, shape, dtype=F32):
        return self.ctx.enter_context(self.nc.sbuf_tensor(name, shape, dtype))

    def ps(self, name, shape, dtype=F32):
        return self.ctx.enter_context(self.nc.psum_tensor(name, shape, dtype))

    def sem(self, name):
        self.sems.append(self.ctx.enter_context(self.nc.semaphore(name)))
        return self.sems[-1]

    def clear_sems(self):
        with self.nc.Block() as block:
            @block.gpsimd
            def _(pool):
                for s in self.sems:
                    pool.sem_clear(s)


def layer_norm_stats(dve, stats, mv, var_eps, tiles, eps, var_ready):
    n = len(tiles)
    for i, x in enumerate(tiles):
        dve.bn_stats(stats[:, i, :], x)
    dve.drain()
    for i in range(n):
        dve.bn_aggr(mv[:, i, :], stats[:, i, :])
    dve.drain()
    dve.tensor_scalar(var_eps, mv[:, 0:n, 1], eps, None, ALU.add).then_inc(var_ready, 1)


MLA_H, MLA_DN, MLA_DR, MLA_R = 16, 128, 64, 64
MLA_SCALE = float((MLA_DN + MLA_DR) ** -0.5)
MLA_PAIRS = MLA_H // 2
MLA_EPS = 1e-6


def mla_fold_weights(nc, g, w):
    with ExitStack() as ctx:
        k = Kit(nc, ctx)
        wqT = k.sb("mla_wqT", [P, MLA_H, D])
        wkT = k.sb("mla_wkT", [P, MLA_H, MLA_R])
        wvT = k.sb("mla_wvT", [P, MLA_H, MLA_R])
        wo = k.sb("mla_wo", [P, MLA_H, D])
        fold = k.ps("mla_fold", [P, 8, 512])
        loaded = k.sem("mla_fold_loaded")
        loaded_v = k.sem("mla_fold_loaded_v")
        pe_loaded = k.sem("mla_fold_pe_loaded")
        q_folded = k.sem("mla_q_folded")
        v_folded = k.sem("mla_v_folded")
        wap, wvo = g["wap"], g["wvo"]

        with nc.Block() as block:
            @block.sync
            def _(sp):
                sp.dma_start(wqT[:, :, :], w["mla_wqT"]).then_inc(loaded, 16)
                sp.dma_start(g["x"][:, :, :], w["x"]).then_inc(g["x_loaded"], 16)
                sp.dma_start(wo[:, :, :], w["mla_wo"]).then_inc(loaded_v, 16)
                for dst, src, done in g["early_loads"]:
                    sp.dma_start(dst, src).then_inc(done, 16)

            @block.tensor
            def _(pe):
                pe.wait_ge(loaded, 32)
                for c in range(DC):
                    for h in range(MLA_H):
                        last = pe.matmul(fold[:, 2 * c + h // 8, (h % 8) * 64:(h % 8 + 1) * 64],
                                         wqT[:, h, c * P:(c + 1) * P], wkT[:, h, :], start=True, stop=True)
                        if h % 8 == 7:
                            last.then_inc(q_folded, 1)
                pe.wait_ge(loaded_v, 32)
                for h in range(MLA_H):
                    last = pe.matmul(fold[64 * (h % 2):64 * (h % 2) + 64, 4 + h // 4,
                                          (h // 2 % 2) * D:(h // 2 % 2 + 1) * D],
                                     wvT[:, h, :], wo[:, h, :], start=True, stop=True)
                    if h % 4 == 3:
                        last.then_inc(v_folded, 1)

            @block.vector
            def _(dve):
                dve.wait_ge(pe_loaded, 16)
                for c in range(DC):
                    dve.tensor_scalar(wap[:, c, :, 1, :], g["wq_pe"][:, c, :, :], MLA_SCALE, None, ALU.mult)
                for n in range(2 * DC):
                    dve.wait_ge(q_folded, n + 1)
                    dve.tensor_scalar(wap[:, n // 2, 4 * (n % 2):4 * (n % 2) + 4, 0, :],
                                      fold[:, n, :].rearrange("p (a b) -> p a b", a=4), MLA_SCALE, None, ALU.mult)

            @block.scalar
            def _(act):
                act.dma_start(wkT[:, :, :], w["mla_wkT"]).then_inc(loaded, 16)
                act.dma_start(g["wq_pe"][:, :, :, :], w["mla_wq_pe"]).then_inc(pe_loaded, 16)
                act.dma_start(wvT[:, :, :], w["mla_wvT"]).then_inc(loaded_v, 16)
                for dst, name in g["first_loads"]:
                    act.dma_start(dst, w[name]).then_inc(g["consts_loaded"], 16)
                for n in range(4):
                    act.wait_ge(v_folded, n + 1)
                    act.activation(wvo[:, 2 * n:2 * n + 2, :].rearrange("p a b -> p (a b)"), fold[:, 4 + n, :],
                                   ACT.Copy)
        k.clear_sems()


def mla_attention(nc, g):
    with ExitStack() as ctx:
        k = Kit(nc, ctx)
        x, wap, wvo, ident, ident_b, mask_b = (g[n] for n in ("x", "wap", "wvo", "ident", "ident_b", "mask_b"))
        wkva, kvw, ropeT, ropeN = (g[n] for n in ("wkva", "kvw", "ropeT", "ropeN"))
        stats = k.sb("stats", [P, TI, 6])
        mv = k.sb("mv", [P, TI, 2])
        ve = k.sb("ve", [P, 2, TI])
        rstd = k.sb("rstd", [P, 2, TI])
        xn = k.sb("xn", [P, TI, D])
        xnT = k.sb("xnT", [P, DC, S])
        kva = k.sb("kva", [P, TI, P])
        sq = k.sb("sq", [P, TI, MLA_R])
        ss = k.sb("ss", [P, TI])
        kr1 = k.sb("kr1", [P, TI, MLA_DR])
        kr2 = k.sb("kr2", [P, TI, MLA_DR])
        kc = k.sb("kc", [P, TI, 2, P])
        kT = k.sb("kT", [P, 2, S])
        wst = k.sb("wst", [P, DC, 2, P])
        qT = k.sb("qT", [P, 2, S])
        swp = k.sb("swp", [P, S])
        rot1 = k.sb("rot1", [P, S])
        rot2 = k.sb("rot2", [P, S])
        nmax = k.sb("nmax", [P, 2, TI])
        lsum = k.sb("lsum", [P, 2, TI])
        rl = k.sb("rl", [P, 2, TI])
        probs = k.sb("probs", [P, 2, CAUSAL_COLS])
        probsT = k.sb("probsT", [P, 2, CAUSAL_COLS])
        on = k.sb("on", [P, TI, MLA_PAIRS, 2, MLA_R])
        onT = k.sb("onT", [P, 2, MLA_PAIRS, P])
        sc = k.ps("sc", [P, 2, 3 * 512])
        po = k.ps("po", [P, 2, TI, MLA_R])
        pq = k.ps("pq", [P, 512])

        def bank(n):
            return sc[:, n // 3, (n % 3) * 512:(n % 3 + 1) * 512]

        names = ("var_ready", "rstd_ready", "xn_ready", "xt_ready", "xnT_ready", "kva_ready", "kvar_ready",
                 "krstd_ready", "kc_ready", "kt_ready", "kT_ready", "staged", "qb_ready", "rope_in", "rope_done",
                 "qa_ready", "qa_copied", "s_ready", "max_ready", "e_ready", "t_ready", "pt_a", "pt_b", "o_ready",
                 "o_done", "ot_ready", "onT_a", "onT_b", "y_ready", "x_done")
        s = {n: k.sem("mla_" + n) for n in names}

        with nc.Block() as block:
            @block.vector
            def _(dve):
                dve.nop().then_inc(s["x_done"], 1)
                dve.nop().then_inc(s["x_done"], 1)
                dve.nop().then_inc(s["o_done"], 1)
                dve.wait_ge(g["x_loaded"], 16)
                dve.wait_ge(g["consts_loaded"], 16 * len(g["first_loads"]))
                with dve.Fori(0, B) as b:
                    dve.wait_ge(s["xt_ready"], b + 1)
                    layer_norm_stats(dve, stats, mv, ve[:, 0, :], [x[:, b * TI + i, :] for i in range(TI)],
                                     LN_EPS, s["var_ready"])
                    dve.wait_ge(s["rstd_ready"], b + 1)
                    for i in range(TI):
                        last = dve.tensor_scalar(xn[:, i, :], x[:, b * TI + i, :], mv[:, i, 0:1], rstd[:, 0, i:i + 1],
                                                 ALU.subtract, ALU.mult)
                    last.then_inc(s["xn_ready"], 1)

                    def rope_queries(n):
                        dve.wait_ge(s["qb_ready"], n + 1)
                        dve.wait_ge(s["rope_done"], n + 1)
                        dve.tensor_tensor(rot1[:, :], pq[:, :], ropeT[:, 0, :], ALU.mult)
                        dve.stream_shuffle(swp[:, :], pq[:, :],
                                           [(r + 16) % 32 for r in range(32)]).then_inc(s["rope_in"], 1)

                    dve.wait_ge(s["kva_ready"], b + 1)
                    dve.tensor_copy(kva[:, :, :], bank(2).rearrange("p (i c) -> p i c", i=TI))
                    dve.drain()
                    kv, pe4 = kva[:, :, 0:MLA_R], kva[:, :, MLA_R:].rearrange("p i (q e r) -> p i q e r", q=2, e=2)
                    dve.tensor_tensor(sq[:, :, :], kv, kv, ALU.mult)
                    dve.tensor_tensor(kr1[:, :, :], kva[:, :, MLA_R:], ropeN[:, :, 0, :], ALU.mult)
                    for e in range(2):
                        for q in range(2):
                            lo = q * 32 + e * 16
                            dve.tensor_tensor(kr2[:, :, lo:lo + 16], pe4[:, :, q, 1 - e, :],
                                              ropeN[:, :, 1, lo:lo + 16], ALU.mult)
                    dve.drain()
                    dve.tensor_reduce(ss[:, :], sq[:, :, :], AX.X, ALU.add)
                    dve.tensor_tensor(kc[:, :, 0, MLA_R:], kr1[:, :, :], kr2[:, :, :], ALU.add)
                    dve.tensor_tensor(kc[:, :, 1, 0:MLA_R], kr1[:, :, :], kr2[:, :, :], ALU.add)
                    dve.drain()
                    dve.tensor_scalar(ve[:, 1, :], ss[:, :], 1.0 / MLA_R, MLA_EPS, ALU.mult,
                                      ALU.add).then_inc(s["kvar_ready"], 1)
                    dve.wait_ge(s["krstd_ready"], b + 1)
                    dve.tensor_tensor(sq[:, :, :], kv, rstd[:, 1, :].unsqueeze(2).to_broadcast([P, TI, MLA_R]),
                                      ALU.mult)
                    dve.drain()
                    kvw_b = kvw[:, :].unsqueeze(1).to_broadcast([P, TI, MLA_R])
                    dve.tensor_tensor(kc[:, :, 0, 0:MLA_R], sq[:, :, :], kvw_b, ALU.mult)
                    dve.tensor_tensor(kc[:, :, 1, MLA_R:], sq[:, :, :], kvw_b, ALU.mult).then_inc(s["kc_ready"], 1)
                    rope_queries(b * MLA_PAIRS)

                    def pair(p, last_pair):
                        n = b * MLA_PAIRS + p
                        for j in range(2):
                            for qi in CAUSAL_ORDER:
                                if qi != 0:
                                    dve.wait_ge(s["s_ready"], 6 * n + 3 * j + CAUSAL_BANK[qi] + 1)
                                at = CAUSAL_COL[qi]
                                red = dve.tensor_reduce(nmax[:, j, qi:qi + 1], sc[:, j, at:at + (qi + 1) * P],
                                                        AX.X, ALU.max, negate=True)
                                if qi != 2:
                                    red.then_inc(s["max_ready"], 1)
                        if not last_pair:
                            rope_queries(n + 1)
                        for j in range(2):
                            dve.wait_ge(s["t_ready"], 6 * n + 3 * j + 2)
                            dve.tensor_copy(probsT[:, j, S:2 * S], sc[:, j, S:2 * S])
                            dve.wait_ge(s["t_ready"], 6 * n + 3 * j + 3)
                            dve.tensor_copy(probsT[:, j, 2 * S:CAUSAL_COLS],
                                            sc[:, j, 2 * S:CAUSAL_COLS]).then_inc(s["pt_b"], 1)
                        dve.reciprocal(rl[:, :, :], lsum[:, :, :])
                        dve.drain()
                        dve.wait_ge(s["o_ready"], n + 1)
                        dve.tensor_tensor(on[:, :, p, :, :].rearrange("p q j r -> p j q r"), po[:, :, :, :],
                                          rl[:, :, :].unsqueeze(3).to_broadcast([P, 2, TI, MLA_R]),
                                          ALU.mult).then_inc(s["o_done"], 1)

                    with dve.Fori(0, MLA_PAIRS - 1) as p:
                        pair(p, False)
                    pair(MLA_PAIRS - 1, True)
                    for i in range(TI):
                        dve.wait_ge(s["ot_ready"], 2 * (b * TI + i) + 2)
                        dve.tensor_copy(onT[:, i % 2, 4:8, :].rearrange("p a t -> p (a t)"),
                                        bank(2 * (i % 2) + 1)).then_inc(s["onT_b"], 1)
                        if i:
                            dve.wait_ge(s["y_ready"], b * TI + i)
                            xi = x[:, b * TI + i - 1, :]
                            dve.tensor_tensor(xi, bank(4 + (i - 1) % 2)[:, 0:D], xi, ALU.add).then_inc(s["x_done"], 1)
                    dve.wait_ge(s["y_ready"], b * TI + TI)
                    xi = x[:, b * TI + TI - 1, :]
                    dve.tensor_tensor(xi, bank(4 + (TI - 1) % 2)[:, 0:D], xi, ALU.add).then_inc(s["x_done"], 1)

            @block.gpsimd
            def _(pool):
                pool.nop().then_inc(s["rope_done"], 1)
                with pool.Fori(0, B) as b:
                    def stage(p):
                        pool.tensor_copy(wst[:, :, :, :], wap[:, :, p, :, :]).then_inc(s["staged"], 1)

                    pool.wait_ge(s["qa_ready"], b * MLA_PAIRS + 1)
                    for which, (var, std) in enumerate((("var_ready", "rstd_ready"), ("kvar_ready", "krstd_ready"))):
                        pool.wait_ge(s[var], b + 1)
                        pool.tensor_tensor(rstd[:, which, :], ve[:, which, :], g["neg_half"][:, 0:TI],
                                           ALU.pow).then_inc(s[std], 1)
                        if which == 0:
                            stage(0)

                    def rope(n):
                        pool.wait_ge(s["rope_in"], n + 1)
                        pool.tensor_tensor(rot2[:, :], swp[:, :], ropeT[:, 1, :], ALU.mult)
                        pool.drain()
                        pool.tensor_tensor(qT[0:64, 1, :], rot1[0:64, :], rot2[0:64, :], ALU.add)
                        pool.drain()
                        pool.tensor_tensor(qT[64:P, 0, :], rot1[64:P, :], rot2[64:P, :],
                                           ALU.add).then_inc(s["rope_done"], 1)
                        pool.drain()

                    with pool.Fori(0, MLA_PAIRS - 1) as p:
                        rope(b * MLA_PAIRS + p)
                        pool.wait_ge(s["qa_ready"], b * MLA_PAIRS + p + 2)
                        stage(p + 1)
                    rope(b * MLA_PAIRS + MLA_PAIRS - 1)

            @block.scalar
            def _(act):
                act.nop().then_inc(s["qa_copied"], 1)
                with act.Fori(0, B) as b:
                    def copy_latent_queries(n):
                        act.wait_ge(s["qa_ready"], n + 2)
                        act.activation(qT[0:64, 0, :], pq[0:64, :], ACT.Copy)
                        act.activation(qT[64:P, 1, :], pq[64:P, :], ACT.Copy).then_inc(s["qa_copied"], 1)

                    act.wait_ge(s["xt_ready"], b + 2)
                    for c in range(DC):
                        last = act.activation(xnT[:, c, :], bank(c), ACT.Copy)
                    last.then_inc(s["xnT_ready"], 1)
                    copy_latent_queries(b * MLA_PAIRS)
                    act.wait_ge(s["kt_ready"], b + 1)
                    for v in range(2):
                        last = act.activation(kT[:, v, :], bank(v), ACT.Copy)
                    last.then_inc(s["kT_ready"], 1)

                    def pair(p, last_pair):
                        n = b * MLA_PAIRS + p
                        for j in range(2):
                            for qi in CAUSAL_ORDER:
                                if qi != 0:
                                    act.wait_ge(s["max_ready"], 6 * n + 3 * j + CAUSAL_BANK[qi] + 1)
                                at = CAUSAL_COL[qi]
                                ex = act.activation(probs[:, j, at:at + (qi + 1) * P], sc[:, j, at:at + (qi + 1) * P],
                                                    ACT.Exp, bias=nmax[:, j, qi:qi + 1],
                                                    accum_out=lsum[:, j, qi:qi + 1])
                                if qi != 2:
                                    ex.then_inc(s["e_ready"], 1)
                        for j in range(2):
                            act.wait_ge(s["t_ready"], 6 * n + 3 * j + 1)
                            act.activation(probsT[:, j, 0:S], sc[:, j, 0:S], ACT.Copy).then_inc(s["pt_a"], 1)
                            if j == 0 and not last_pair:
                                copy_latent_queries(n + 1)

                    with act.Fori(0, MLA_PAIRS - 1) as p:
                        pair(p, False)
                    pair(MLA_PAIRS - 1, True)
                    for i in range(TI):
                        act.wait_ge(s["ot_ready"], 2 * (b * TI + i) + 1)
                        act.activation(onT[:, i % 2, 0:4, :].rearrange("p a t -> p (a t)"), bank(2 * (i % 2)),
                                       ACT.Copy).then_inc(s["onT_a"], 1)

            @block.tensor
            def _(pe):
                pe.nop().then_inc(s["xt_ready"], 1)
                pe.nop().then_inc(s["qa_ready"], 1)
                with pe.Fori(0, B) as b:
                    pe.wait_ge(s["xn_ready"], b + 1)
                    for c in range(DC):
                        for i in range(TI):
                            last = pe.transpose(bank(c)[:, i * P:(i + 1) * P], xn[:, i, c * P:(c + 1) * P],
                                                ident[:, :])
                    last.then_inc(s["xt_ready"], 1)
                    pe.wait_ge(s["xnT_ready"], b + 1)
                    for i in range(TI):
                        for c in range(DC):
                            last = pe.matmul(bank(2)[:, i * P:(i + 1) * P], xnT[:, c, i * P:(i + 1) * P],
                                             wkva[:, c, :], start=(c == 0), stop=(c == DC - 1))
                    last.then_inc(s["kva_ready"], 1)

                    def project(n, kind):
                        if kind == 1:
                            pe.wait_ge(s["staged"], n + 1)
                            pe.wait_ge(s["qa_copied"], n + 1)
                        else:
                            pe.wait_ge(s["rope_in"], n + 1)
                        for c in range(DC):
                            last = pe.matmul(pq[:, :], wst[:, c, kind, :], xnT[:, c, :], start=(c == 0),
                                             stop=(c == DC - 1))
                        last.then_inc(s["qb_ready" if kind == 1 else "qa_ready"], 1)

                    project(b * MLA_PAIRS, 1)
                    pe.wait_ge(s["kc_ready"], b + 1)
                    for v in range(2):
                        for i in range(TI):
                            last = pe.transpose(bank(v)[:, i * P:(i + 1) * P], kc[:, i, v, :], ident[:, :])
                    last.then_inc(s["kt_ready"], 1)
                    project(b * MLA_PAIRS, 0)

                    def pair(p, last_pair):
                        n = b * MLA_PAIRS + p
                        pe.wait_ge(s["kT_ready"], b + 1)
                        pe.wait_ge(s["rope_done"], n + 2)
                        pe.wait_ge(s["qa_copied"], n + 2)
                        for j in range(2):
                            for qi in CAUSAL_ORDER:
                                at = CAUSAL_COL[qi]
                                pe.matmul(sc[:, j, at:at + (qi + 1) * P], qT[:, j, qi * P:(qi + 1) * P],
                                          kT[:, j, 0:(qi + 1) * P], start=True, stop=False)
                                last = pe.matmul(sc[:, j, at + qi * P:at + (qi + 1) * P], ident_b[:, :], mask_b[:, :],
                                                 start=False, stop=True)
                                if qi != 2:
                                    last.then_inc(s["s_ready"], 1)
                        for j in range(2):
                            if not last_pair:
                                project(n + 1, 1 - j)
                            for qi in CAUSAL_ORDER:
                                if qi != 0:
                                    pe.wait_ge(s["e_ready"], 6 * n + 3 * j + CAUSAL_BANK[qi] + 1)
                                for kj in range(qi + 1):
                                    at = CAUSAL_COL[qi] + kj * P
                                    last = pe.transpose(sc[:, j, at:at + P], probs[:, j, at:at + P], ident[:, :])
                                if qi != 2:
                                    last.then_inc(s["t_ready"], 1)
                        pe.wait_ge(s["o_done"], n + 1)
                        for j in range(2):
                            pe.wait_ge(s["pt_a"], 2 * n + j + 1)
                            pe.wait_ge(s["pt_b"], 2 * n + j + 1)
                            for qi in range(TI):
                                for kj in range(qi + 1):
                                    at = CAUSAL_COL[qi] + kj * P
                                    last = pe.matmul(po[:, j, qi, :], probsT[:, j, at:at + P], kc[:, kj, 0, 0:MLA_R],
                                                     start=(kj == 0), stop=(kj == qi))
                        last.then_inc(s["o_ready"], 1)

                    with pe.Fori(0, MLA_PAIRS - 1) as p:
                        pair(p, False)
                    pair(MLA_PAIRS - 1, True)

                    def turn(i):
                        for hp in range(MLA_PAIRS):
                            last = pe.transpose(bank(2 * (i % 2) + hp // 4)[:, (hp % 4) * P:(hp % 4 + 1) * P],
                                                on[:, i, hp, :, :].rearrange("p j r -> p (j r)"), ident[:, :])
                            if hp % 4 == 3:
                                last.then_inc(s["ot_ready"], 1)

                    pe.wait_ge(s["o_done"], b * MLA_PAIRS + MLA_PAIRS + 1)
                    turn(0)
                    for i in range(TI):
                        if i + 1 < TI:
                            turn(i + 1)
                        pe.wait_ge(s["onT_a"], b * TI + i + 1)
                        pe.wait_ge(s["onT_b"], b * TI + i + 1)
                        pe.wait_ge(s["x_done"], b * TI + i + 1)
                        for hp in range(MLA_PAIRS):
                            last = pe.matmul(bank(4 + i % 2)[:, 0:D], onT[:, i % 2, hp, :], wvo[:, hp, :],
                                             start=(hp == 0), stop=(hp == MLA_PAIRS - 1))
                        last.then_inc(s["y_ready"], 1)
        k.clear_sems()


class Normed:

    def __init__(self, k, tag):
        self.stats = k.sb(tag + "_stats", [P, TI, 6])
        self.mv = k.sb(tag + "_mv", [P, TI, 2])
        self.ve = k.sb(tag + "_ve", [P, TI])
        self.rstd = k.sb(tag + "_rstd", [P, TI])
        self.xn = k.sb(tag + "_xn", [P, TI, D])
        self.xnT = k.sb(tag + "_xnT", [P, DC, S])
        self.var_ready = k.sem(tag + "_var_ready")
        self.rstd_ready = k.sem(tag + "_rstd_ready")
        self.xn_ready = k.sem(tag + "_xn_ready")
        self.xt_ready = k.sem(tag + "_xt_ready")
        self.xnT_ready = k.sem(tag + "_xnT_ready")

    def scale_rows(self, dve, x, b):
        for i in range(TI):
            last = dve.tensor_scalar(self.xn[:, i, :], x[:, b * TI + i, :], self.mv[:, i, 0:1], self.rstd[:, i:i + 1],
                                     ALU.subtract, ALU.mult)
        return last

    def norm(self, dve, x, b):
        dve.wait_ge(self.xt_ready, b + 1)
        layer_norm_stats(dve, self.stats, self.mv, self.ve[:, :], [x[:, b * TI + i, :] for i in range(TI)],
                         LN_EPS, self.var_ready)
        dve.wait_ge(self.rstd_ready, b + 1)
        self.scale_rows(dve, x, b).then_inc(self.xn_ready, 1)

    def invert(self, pool, g, b):
        pool.wait_ge(self.var_ready, b + 1)
        pool.tensor_tensor(self.rstd[:, :], self.ve[:, :], g["neg_half"][:, 0:TI], ALU.pow).then_inc(self.rstd_ready, 1)

    def turn(self, pe, g, banks, b):
        pe.wait_ge(self.xn_ready, b + 1)
        for c in range(DC):
            for i in range(TI):
                last = pe.transpose(banks[c][:, i * P:(i + 1) * P], self.xn[:, i, c * P:(c + 1) * P], g["ident"][:, :])
        last.then_inc(self.xt_ready, 1)

    def first_free(self, pe):
        pe.nop().then_inc(self.xt_ready, 1)

    def copy(self, act, banks, b):
        act.wait_ge(self.xt_ready, b + 2)
        for c in range(DC):
            last = act.activation(self.xnT[:, c, :], banks[c], ACT.Copy)
        last.then_inc(self.xnT_ready, 1)


FFN_EPS = 1e-7


def ternary_ffn(nc, g, tag, loads):
    with ExitStack() as ctx:
        k = Kit(nc, ctx)
        x = g["x"]
        ln = Normed(k, tag)
        y = k.sb(tag + "_y", [P, NT, D])
        sq = k.sb(tag + "_sq", [P, TI, D])
        n2 = k.sb(tag + "_n2", [P, NT])
        norm = k.sb(tag + "_norm", [P, NT])
        t = k.sb(tag + "_t", [P, 8, NT])
        ps = k.ps(tag + "_ps", [P, 8, 512])
        y_ready = k.sem(tag + "_y_ready")
        y_scaled = k.sem(tag + "_y_scaled")
        norms_ready = k.sem(tag + "_norms_ready")
        root_ready = k.sem(tag + "_root_ready")
        clipped = k.sem(tag + "_clipped")
        tanh_ready = k.sem(tag + "_tanh_ready")
        banks = [ps[:, 0, :], ps[:, 1, :]]

        with nc.Block() as block:
            @block.sync
            def _(sp):
                for dst, src, done in loads:
                    sp.dma_start(dst, src).then_inc(done, 16)

            @block.vector
            def _(dve):
                dve.nop().then_inc(y_scaled, 1)
                with dve.Fori(0, B) as b:
                    ln.norm(dve, x, b)
                    dve.wait_ge(y_ready, b + 1)
                    for h in range(2):
                        dve.tensor_tensor(y[:, b * TI + 2 * h, :], ps[:, 2 + h, 0:D], g["ffn_scale"][:, :], ALU.mult)
                        last = dve.tensor_tensor(y[:, b * TI + 2 * h + 1, :], ps[:, 2 + h, D:2 * D],
                                                 g["ffn_scale"][:, :], ALU.mult)
                    last.then_inc(y_scaled, 1)
                    dve.drain()
                    for i in range(TI):
                        dve.tensor_tensor(sq[:, i, :], y[:, b * TI + i, :], y[:, b * TI + i, :], ALU.mult)
                    dve.drain()
                    for i in range(TI):
                        last = dve.tensor_reduce(n2[:, bass.ds(b * TI + i, 1)], sq[:, i, :], AX.X, ALU.add)
                    last.then_inc(norms_ready, 1)
                    dve.drain()
                dve.wait_ge(root_ready, 1)
                dve.tensor_scalar(t[:, 0, :], norm[:, :], FFN_EPS, None, ALU.max).then_inc(clipped, 1)
                dve.drain()
                dve.tensor_scalar(t[:, 2, :], t[:, 0, :], FFN_EPS, None, ALU.add)
                dve.drain()
                dve.reciprocal(t[:, 3, :], t[:, 2, :])
                dve.drain()
                dve.wait_ge(tanh_ready, 1)
                dve.tensor_tensor(t[:, 4, :], t[:, 1, :], t[:, 3, :], ALU.mult)
                dve.drain()
                dve.tensor_tensor(t[:, 5, :], norm[:, :], t[:, 4, :], ALU.mult)
                dve.drain()
                dve.tensor_scalar(t[:, 6, :], t[:, 5, :], FFN_EPS, None, ALU.max)
                dve.drain()
                dve.reciprocal(t[:, 7, :], t[:, 6, :])
                dve.drain()
                dve.tensor_scalar(t[:, 0, :], t[:, 7, :], 0.99, 1.0, ALU.mult, ALU.min)
                dve.drain()
                dve.tensor_tensor(t[:, 2, :], t[:, 0, :], t[:, 4, :], ALU.mult)
                dve.drain()
                with dve.Fori(0, NT) as i:
                    dve.scalar_tensor_tensor(x[:, i, :], y[:, i, :], t[:, 2, bass.ds(i, 1)], x[:, i, :],
                                             ALU.mult, ALU.add)

            @block.gpsimd
            def _(pool):
                with pool.Fori(0, B) as b:
                    ln.invert(pool, g, b)
                pool.wait_ge(norms_ready, B)
                pool.tensor_tensor(norm[:, :], n2[:, :], g["pos_half"][:, 0:NT], ALU.pow).then_inc(root_ready, 1)

            @block.scalar
            def _(act):
                with act.Fori(0, B) as b:
                    ln.copy(act, banks, b)
                act.wait_ge(clipped, 1)
                act.activation(t[:, 1, :], t[:, 0, :], ACT.Tanh).then_inc(tanh_ready, 1)

            @block.tensor
            def _(pe):
                ln.first_free(pe)
                with pe.Fori(0, B) as b:
                    ln.turn(pe, g, banks, b)
                    pe.wait_ge(ln.xnT_ready, b + 1)
                    pe.wait_ge(y_scaled, b + 1)
                    for i in range(TI):
                        for c in range(DC):
                            last = pe.matmul(ps[:, 2 + i // 2, (i % 2) * D:(i % 2 + 1) * D],
                                             ln.xnT[:, c, i * P:(i + 1) * P], g["ffn_w"][:, c, :],
                                             start=(c == 0), stop=(c == DC - 1))
                    last.then_inc(y_ready, 1)
        k.clear_sems()


COS_H, COS_D = 16, 128
COS_SCALE = 16.0


def cosine_attention(nc, g):
    with ExitStack() as ctx:
        k = Kit(nc, ctx)
        x, ident, wq, wkv, wout, gout = (g[n] for n in ("x", "ident", "cos_wq", "cos_wkv", "cos_wout", "cos_gout"))
        ln = Normed(k, "cos")
        var2 = k.sb("cos_var2", [P, 2, TI])
        rstd2 = k.sb("cos_rstd2", [P, TI])
        kk = k.sb("cos_kk", [P, TI, P])
        ksum = k.sb("cos_ksum", [P, 3, TI])
        kn = k.sb("cos_kn", [P, TI, P])
        kT = k.sb("cos_kT", [P, S])
        vx = k.sb("cos_vx", [P, TI, COS_D + 1])
        qsq = k.sb("cos_qsq", [P, 2, 4, P])
        qss = k.sb("cos_qss", [P, 2, 4])
        qse = k.sb("cos_qse", [P, 2, 4])
        qrs = k.sb("cos_qrs", [P, 2, 4])
        qn = k.sb("cos_qn", [P, 2, 4, P])
        qT = k.sb("cos_qT", [P, COS_H, S])
        probs = k.sb("cos_probs", [P, 2, TI, S])
        rl = k.sb("cos_rl", [P, 2, TI])
        on = qT[:, :, :].rearrange("p h (i c) -> p i h c", i=TI)
        onT = k.sb("cos_onT", [P, 2, COS_H, P])
        yn = k.sb("cos_yn", [P, TI, D])
        ps = k.ps("cos_ps", [P, 8, 512])
        po = ps[:, 4:8, 0:2 * (COS_D + 1)].rearrange("p (j a) (q c) -> p j a q c", j=2, c=COS_D + 1)
        names = ("scaled_w", "var2_ready", "rstd2_ready", "kv_ready", "k_var", "k_rstd", "kn_ready", "kt_ready",
                 "kT_ready", "q_ready", "q_sq", "q_var", "q_rstd", "qn_ready", "qt_ready", "qT_ready", "s_ready",
                 "e_ready", "o_ready", "o_done", "ot_ready", "onT_a", "onT_d", "y_ready", "y_var", "y_rstd",
                 "batch_done")
        s = {n: k.sem("cos_" + n) for n in names}
        banks = [ps[:, 0, :], ps[:, 1, :]]
        QU = COS_H // 4 * TI

        with nc.Block() as block:
            @block.vector
            def _(dve):
                for _ in range(2):
                    dve.nop().then_inc(s["o_done"], 1)
                    dve.nop().then_inc(s["qn_ready"], 1)
                for c in range(DC):
                    dve.tensor_scalar(wq[:, c, :], wq[:, c, :], g["cos_g"][:, c:c + 1], None, ALU.mult)
                    dve.tensor_scalar(wkv[:, c, :], wkv[:, c, :], g["cos_g"][:, c:c + 1], None, ALU.mult)
                dve.memset(vx[:, :, COS_D:], 1.0).then_inc(s["scaled_w"], 1)
                with dve.Fori(0, B) as b:
                    dve.wait_ge(ln.xt_ready, b + 1)
                    layer_norm_stats(dve, ln.stats, ln.mv, ln.ve[:, :], [x[:, b * TI + i, :] for i in range(TI)],
                                     LN_EPS, ln.var_ready)
                    dve.wait_ge(ln.rstd_ready, b + 1)
                    dve.tensor_tensor(var2[:, 0, :], ln.mv[:, :, 1], ln.rstd[:, :], ALU.mult)
                    dve.drain()
                    dve.tensor_tensor(var2[:, 0, :], var2[:, 0, :], ln.rstd[:, :], ALU.mult)
                    dve.drain()
                    dve.tensor_scalar(var2[:, 1, :], var2[:, 0, :], LN_EPS, None, ALU.add).then_inc(s["var2_ready"], 1)
                    dve.wait_ge(s["rstd2_ready"], b + 1)
                    dve.tensor_tensor(ln.rstd[:, :], rstd2[:, :], ln.rstd[:, :], ALU.mult)
                    dve.drain()
                    ln.scale_rows(dve, x, b).then_inc(ln.xn_ready, 1)
                    dve.wait_ge(s["kv_ready"], b + 1)
                    kv = ps[:, 2:4, :].rearrange("p a (i c) -> p a i c", i=2)
                    dve.tensor_copy(kk.rearrange("p (a i) c -> p a i c", a=2), kv[:, :, :, 0:P])
                    dve.tensor_copy(vx[:, :, 0:COS_D].rearrange("p (a i) c -> p a i c", a=2), kv[:, :, :, P:])
                    dve.drain()
                    dve.tensor_tensor(kn[:, :, :], kk[:, :, :], kk[:, :, :], ALU.mult)
                    dve.drain()
                    dve.tensor_reduce(ksum[:, 0, :], kn[:, :, :], AX.X, ALU.add)
                    dve.drain()
                    dve.tensor_scalar(ksum[:, 1, :], ksum[:, 0, :], 1e-12, None, ALU.add).then_inc(s["k_var"], 1)
                    dve.wait_ge(s["k_rstd"], b + 1)
                    for i in range(TI):
                        last = dve.tensor_scalar(kn[:, i, :], kk[:, i, :], ksum[:, 2, i:i + 1], COS_SCALE,
                                                 ALU.mult, ALU.mult)
                    last.then_inc(s["kn_ready"], 1)

                    with dve.Fori(0, COS_H // 4) as hq:
                        def sums(i):
                            u = b * QU + hq * TI + i
                            dve.wait_ge(s["q_sq"], u + 1)
                            dve.tensor_reduce(qss[:, i % 2, :], qsq[:, i % 2, :, :], AX.X, ALU.add)
                            dve.drain()
                            dve.tensor_scalar(qse[:, i % 2, :], qss[:, i % 2, :], 1e-12 / 256, None,
                                              ALU.add).then_inc(s["q_var"], 1)

                        def scale(i):
                            u = b * QU + hq * TI + i
                            dve.wait_ge(s["q_rstd"], u + 1)
                            dve.wait_ge(s["qt_ready"], u + 1)
                            dve.tensor_tensor(qn[:, i % 2, :, :],
                                              ps[:, i % 2, :].rearrange("p (h c) -> p h c", h=4),
                                              qrs[:, i % 2, :].unsqueeze(2).to_broadcast([P, 4, P]),
                                              ALU.mult).then_inc(s["qn_ready"], 1)

                        sums(0)
                        for i in range(TI):
                            if i + 1 < TI:
                                sums(i + 1)
                            scale(i)

                    with dve.Fori(0, COS_H // 2) as p:
                        for j in range(2):
                            h = b * COS_H + 2 * p + j
                            dve.wait_ge(s["o_ready"], h + 1)
                            dve.reciprocal(rl[:, j, :].rearrange("p (a q) -> p a q", a=2), po[:, j, :, :, COS_D])
                            dve.drain()
                            dve.tensor_tensor(on[:, :, 2 * p + j, :].rearrange("p (a q) c -> p a q c", a=2),
                                              po[:, j, :, :, 0:COS_D],
                                              rl[:, j, :].rearrange("p (a q) -> p a q", a=2).unsqueeze(3)
                                              .to_broadcast([P, 2, 2, COS_D]), ALU.mult).then_inc(s["o_done"], 1)
                    for i in range(TI):
                        for n in (1, 3):
                            dve.wait_ge(s["ot_ready"], 4 * (b * TI + i) + n + 1)
                            last = dve.tensor_copy(onT[:, i % 2, 4 * n:4 * n + 4, :].rearrange("p a t -> p (a t)"),
                                                   ps[:, n, :])
                        last.then_inc(s["onT_d"], 1)
                    dve.wait_ge(s["y_ready"], b + 1)
                    layer_norm_stats(dve, ln.stats, ln.mv, ln.ve[:, :], [ps[:, 4 + i, 0:D] for i in range(TI)],
                                     LN_EPS, s["y_var"])
                    dve.wait_ge(s["y_rstd"], b + 1)
                    for i in range(TI):
                        dve.tensor_scalar(yn[:, i, :], ps[:, 4 + i, 0:D], ln.mv[:, i, 0:1], ln.rstd[:, i:i + 1],
                                          ALU.subtract, ALU.mult)
                    dve.drain()
                    for i in range(TI):
                        dve.tensor_tensor(yn[:, i, :], yn[:, i, :], gout[:, :], ALU.mult)
                    dve.drain()
                    for i in range(TI):
                        xi = x[:, b * TI + i, :]
                        last = dve.tensor_tensor(xi, yn[:, i, :], xi, ALU.add)
                    last.then_inc(s["batch_done"], 1)

            @block.gpsimd
            def _(pool):
                nh = g["neg_half"]
                with pool.Fori(0, B) as b:
                    ln.invert(pool, g, b)
                    pool.wait_ge(s["var2_ready"], b + 1)
                    pool.tensor_tensor(rstd2[:, :], var2[:, 1, :], nh[:, 0:TI], ALU.pow).then_inc(s["rstd2_ready"], 1)
                    pool.wait_ge(s["k_var"], b + 1)
                    pool.tensor_tensor(ksum[:, 2, :], ksum[:, 1, :], nh[:, 0:TI], ALU.pow).then_inc(s["k_rstd"], 1)
                    with pool.Fori(0, COS_H // 4) as hq:
                        for i in range(TI):
                            pool.wait_ge(s["q_var"], b * QU + hq * TI + i + 1)
                            pool.tensor_tensor(qrs[:, i % 2, :], qse[:, i % 2, :], nh[:, 0:4],
                                               ALU.pow).then_inc(s["q_rstd"], 1)
                    pool.wait_ge(s["y_var"], b + 1)
                    pool.tensor_tensor(ln.rstd[:, :], ln.ve[:, :], nh[:, 0:TI], ALU.pow).then_inc(s["y_rstd"], 1)

            @block.scalar
            def _(act):
                for _ in range(TI):
                    act.nop().then_inc(s["e_ready"], 1)
                for _ in range(2):
                    act.nop().then_inc(s["qT_ready"], 1)
                with act.Fori(0, B) as b:
                    ln.copy(act, banks, b)
                    act.wait_ge(s["kt_ready"], b + 1)
                    act.activation(kT[:, :], ps[:, 4, :], ACT.Copy).then_inc(s["kT_ready"], 1)
                    with act.Fori(0, COS_H // 4) as hq:
                        def square(i):
                            u = b * QU + hq * TI + i
                            act.wait_ge(s["q_ready"], u + 1)
                            act.wait_ge(s["qn_ready"], u + 1)
                            act.activation(qsq[:, i % 2, :, :].rearrange("p h c -> p (h c)"), ps[:, i % 2, :],
                                           ACT.Square).then_inc(s["q_sq"], 1)

                        square(0)
                        for i in range(TI):
                            if i + 1 < TI:
                                square(i + 1)
                            act.wait_ge(s["qt_ready"], b * QU + hq * TI + i + 3)
                            act.activation(qT[:, bass.ts(hq, 4), i * P:(i + 1) * P],
                                           ps[:, 2 + i % 2, :].rearrange("p (h t) -> p h t", h=4),
                                           ACT.Copy).then_inc(s["qT_ready"], 1)
                    with act.Fori(0, COS_H // 2) as p:
                        for j in range(2):
                            for kj in range(TI):
                                act.wait_ge(s["s_ready"], TI * (b * COS_H + 2 * p + j) + kj + 1)
                                act.activation(probs[:, j, kj, :], ps[:, kj, :], ACT.Exp).then_inc(s["e_ready"], 1)
                    for i in range(TI):
                        for n in (0, 2):
                            act.wait_ge(s["ot_ready"], 4 * (b * TI + i) + n + 1)
                            last = act.activation(onT[:, i % 2, 4 * n:4 * n + 4, :].rearrange("p a t -> p (a t)"),
                                                  ps[:, n, :], ACT.Copy)
                        last.then_inc(s["onT_a"], 1)

            @block.tensor
            def _(pe):
                ln.first_free(pe)
                for _ in range(2):
                    pe.nop().then_inc(s["qt_ready"], 1)
                pe.wait_ge(s["scaled_w"], 1)
                with pe.Fori(0, B) as b:
                    ln.turn(pe, g, banks, b)
                    pe.wait_ge(ln.xnT_ready, b + 1)
                    for i in range(TI):
                        for c in range(DC):
                            last = pe.matmul(ps[:, 2 + i // 2, (i % 2) * D:(i % 2 + 1) * D],
                                             ln.xnT[:, c, i * P:(i + 1) * P], wkv[:, c, :],
                                             start=(c == 0), stop=(c == DC - 1))
                    last.then_inc(s["kv_ready"], 1)
                    pe.wait_ge(s["kn_ready"], b + 1)
                    for i in range(TI):
                        last = pe.transpose(ps[:, 4, i * P:(i + 1) * P], kn[:, i, :], ident[:, :])
                    last.then_inc(s["kt_ready"], 1)

                    with pe.Fori(0, COS_H // 4) as hq:
                        def project(i):
                            u = b * QU + hq * TI + i
                            pe.wait_ge(s["qn_ready"], u + 1)
                            for c in range(DC):
                                last = pe.matmul(ps[:, i % 2, :], ln.xnT[:, c, i * P:(i + 1) * P],
                                                 wq[:, c, bass.ts(hq, 512)], start=(c == 0), stop=(c == DC - 1))
                            last.then_inc(s["q_ready"], 1)

                        project(0)
                        for i in range(TI):
                            if i + 1 < TI:
                                project(i + 1)
                            u = b * QU + hq * TI + i
                            pe.wait_ge(s["qn_ready"], u + 3)
                            pe.wait_ge(s["qT_ready"], u + 1)
                            for h in range(4):
                                last = pe.transpose(ps[:, 2 + i % 2, h * P:(h + 1) * P], qn[:, i % 2, h, :],
                                                    ident[:, :])
                            last.then_inc(s["qt_ready"], 1)

                    with pe.Fori(0, COS_H // 2) as p:
                        pe.wait_ge(s["kT_ready"], b + 1)
                        pe.wait_ge(s["qT_ready"], b * QU + QU + 2)
                        for j in range(2):
                            h = b * COS_H + 2 * p + j
                            for kj in range(TI):
                                pe.wait_ge(s["e_ready"], TI * h + kj + 1)
                                pe.matmul(ps[:, kj, :], kT[:, kj * P:(kj + 1) * P], qT[:, 2 * p + j, :],
                                          start=True, stop=True).then_inc(s["s_ready"], 1)
                        for j in range(2):
                            h = b * COS_H + 2 * p + j
                            pe.wait_ge(s["e_ready"], TI * h + 2 * TI)
                            pe.wait_ge(s["o_done"], h + 1)
                            for qi in range(TI):
                                for kj in range(TI):
                                    last = pe.matmul(po[:, j, qi // 2, qi % 2, :],
                                                     probs[:, j, kj, qi * P:(qi + 1) * P], vx[:, kj, :],
                                                     start=(kj == 0), stop=(kj == TI - 1))
                            last.then_inc(s["o_ready"], 1)

                    def turn(i):
                        for h in range(COS_H):
                            last = pe.transpose(ps[:, h // 4, (h % 4) * P:(h % 4 + 1) * P], on[:, i, h, :],
                                                ident[:, :])
                            if h % 4 == 3:
                                last.then_inc(s["ot_ready"], 1)

                    pe.wait_ge(s["o_done"], b * COS_H + COS_H + 2)
                    turn(0)
                    for i in range(TI):
                        pe.wait_ge(s["onT_a"], b * TI + i + 1)
                        pe.wait_ge(s["onT_d"], b * TI + i + 1)
                        if i + 1 < TI:
                            turn(i + 1)
                        for h in range(COS_H):
                            last = pe.matmul(ps[:, 4 + i, 0:D], onT[:, i % 2, h, :], wout[:, h, :],
                                             start=(h == 0), stop=(h == COS_H - 1))
                    last.then_inc(s["y_ready"], 1)
        k.clear_sems()


GLA_H, GLA_DK, GLA_DV, GLA_LR = 16, 8, 16, 16
GLA_SCALE = float(GLA_DK ** -0.5)
GLA_EPS = 1e-5
GATE_NORMALIZER = 16.0


def gated_linear_attention(nc, g):
    with ExitStack() as ctx:
        k = Kit(nc, ctx)
        x, ident = g["x"], g["ident"]
        ln = Normed(k, "gla")
        qT = k.sb("gla_qT", [P, S])
        kT = k.sb("gla_kT", [P, S])
        vT = k.sb("gla_vT", [P, 2, S])
        z1 = k.sb("gla_z1", [GLA_LR, S])
        z = k.sb("gla_z", [P, S])
        za = k.sb("gla_za", [P, S])
        ze = k.sb("gla_ze", [P, S])
        decay = k.sb("gla_decay", [P, S])
        ge = k.sb("gla_ge", [P, TI, D])
        gr = k.sb("gla_gr", [P, TI, D])
        gate = k.sb("gla_gate", [P, TI, D])
        kv = k.sb("gla_kv", [P, 2, S])
        st = k.sb("gla_st", [P, 2, S])
        qs = k.sb("gla_qs", [P, 2, S])
        osq = k.sb("gla_osq", [P, TI, GLA_DV, GLA_H])
        oss = k.sb("gla_oss", [P, TI, GLA_H])
        ove = k.sb("gla_ove", [P, TI, GLA_H])
        orstd = k.sb("gla_orstd", [P, TI, GLA_H])
        og = k.sb("gla_og", [P, TI, GLA_DV, GLA_H])
        ogT = k.sb("gla_ogT", [P, DC, S])
        ps = k.ps("gla_ps", [P, 8, 512])
        names = ("q_ready", "k_ready", "v_ready", "z1_ready", "z1_copied", "z_ready", "g_ready", "qT_ready",
                 "kT_ready", "vT_ready", "za_ready", "zl_ready", "lg_ready", "decay_ready", "ge_ready", "gate_ready",
                 "vrep_ready", "kv_ready", "st_ready", "qs_ready", "qs_read", "osq_ready", "ove_ready",
                 "orstd_ready", "og_ready", "ot_ready", "ogT_ready", "y_ready", "batch_done")
        s = {n: k.sem("gla_" + n) for n in names}
        banks = [ps[:, 0, :], ps[:, 1, :]]
        gps = ps[:, 6:8, :].rearrange("p a (i c) -> p a i c", i=2)
        ops = ps[:, 2:4, :].rearrange("p a (i j h) -> p (a i) j h", i=2, h=GLA_H)

        with nc.Block() as block:
            @block.vector
            def _(dve):
                for _ in range(2):
                    dve.nop().then_inc(s["kv_ready"], 1)
                with dve.Fori(0, B) as b:
                    ln.norm(dve, x, b)
                    dve.wait_ge(s["z_ready"], b + 1)
                    dve.tensor_scalar(z[:, :], ps[:, 5, :], g["gla_bgk2"][:, 0:1], None, ALU.add)
                    dve.drain()
                    dve.scalar_tensor_tensor(za[:, :], z[:, :], -1.0, z[:, :], ALU.mult,
                                             ALU.min).then_inc(s["za_ready"], 1)
                    dve.wait_ge(s["zl_ready"], b + 1)
                    dve.scalar_tensor_tensor(za[:, :], z[:, :], 0.0, ze[:, :], ALU.min,
                                             ALU.subtract).then_inc(s["lg_ready"], 1)
                    dve.wait_ge(s["ge_ready"], b + 1)
                    dve.tensor_scalar(gr[:, :, :], ge[:, :, :], 1.0, None, ALU.add)
                    dve.drain()
                    dve.reciprocal(ge[:, :, :], gr[:, :, :])
                    dve.tensor_tensor(gate[:, :, :].rearrange("p (a i) c -> p a i c", a=2), gps,
                                      g["gla_normw"][:, :].unsqueeze(1).unsqueeze(1).to_broadcast([P, 2, 2, D]),
                                      ALU.mult)
                    dve.drain()
                    dve.tensor_tensor(gate[:, :, :], gate[:, :, :], ge[:, :, :], ALU.mult).then_inc(s["gate_ready"], 1)

                    with dve.Fori(0, 2) as half:
                        for j in range(8):
                            n = b * GLA_DV + half * 8 + j
                            if j == 0:
                                dve.wait_ge(s["kT_ready"], b + 1)
                                dve.wait_ge(s["decay_ready"], b + 1)
                            dve.wait_ge(s["vrep_ready"], n + 1)
                            dve.tensor_tensor(kv[:, j % 2, :], ps[:, j % 2, :], kT[:, :],
                                              ALU.mult).then_inc(s["kv_ready"], 1)
                            dve.drain()
                            dve.wait_ge(s["qs_ready"], n + 1)
                            dve.tensor_tensor_scan(st[:, j % 2, :], decay[:, :], kv[:, j % 2, :], 0.0, ALU.mult,
                                                   ALU.add).then_inc(s["st_ready"], 1)
                    dve.wait_ge(s["osq_ready"], b + 1)
                    dve.tensor_reduce(oss[:, :, :], osq[:, :, :, :].rearrange("p i j h -> p i h j"), AX.X, ALU.add)
                    dve.drain()
                    dve.tensor_scalar(ove[:, :, :], oss[:, :, :], 1.0 / GLA_DV, GLA_EPS, ALU.mult,
                                      ALU.add).then_inc(s["ove_ready"], 1)
                    dve.wait_ge(s["orstd_ready"], b + 1)
                    for i in range(TI):
                        dve.tensor_tensor(og[:, i, :, :], ops[:, i, :, :],
                                          orstd[:, i, :].unsqueeze(1).to_broadcast([P, GLA_DV, GLA_H]), ALU.mult)
                    dve.drain()
                    dve.tensor_tensor(og[:, :, :, :].rearrange("p i j h -> p i (j h)"),
                                      og[:, :, :, :].rearrange("p i j h -> p i (j h)"), gate[:, :, :],
                                      ALU.mult).then_inc(s["og_ready"], 1)
                    dve.wait_ge(s["y_ready"], b + 1)
                    for i in range(TI):
                        xi = x[:, b * TI + i, :]
                        last = dve.tensor_tensor(xi, ps[:, 6 + i // 2, (i % 2) * D:(i % 2 + 1) * D], xi, ALU.add)
                    last.then_inc(s["batch_done"], 1)

            @block.gpsimd
            def _(pool):
                for _ in range(2):
                    pool.nop().then_inc(s["qs_ready"], 1)
                with pool.Fori(0, B) as b:
                    ln.invert(pool, g, b)
                    with pool.Fori(0, 2) as half:
                        for j in range(8):
                            if j == 0:
                                pool.wait_ge(s["qT_ready"], b + 1)
                            n = b * GLA_DV + half * 8 + j
                            pool.wait_ge(s["qs_read"], n + 1)
                            pool.wait_ge(s["st_ready"], n + 1)
                            pool.tensor_tensor(qs[:, j % 2, :], st[:, j % 2, :], qT[:, :],
                                               ALU.mult).then_inc(s["qs_ready"], 1)
                    pool.wait_ge(s["ove_ready"], b + 1)
                    pool.tensor_tensor(orstd[:, :, :].rearrange("p i h -> p (i h)"), ove[:, :, :].rearrange("p i h -> p (i h)"),
                                       g["neg_half"][:, :], ALU.pow).then_inc(s["orstd_ready"], 1)

            @block.scalar
            def _(act):
                with act.Fori(0, B) as b:
                    ln.copy(act, banks, b)
                    act.wait_ge(s["z1_ready"], b + 1)
                    act.activation(z1[:, :], ps[0:GLA_LR, 4, :], ACT.Copy).then_inc(s["z1_copied"], 1)
                    act.wait_ge(s["k_ready"], b + 1)
                    act.activation(kT[:, :], ps[:, 1, :], ACT.Copy).then_inc(s["kT_ready"], 1)
                    act.wait_ge(s["v_ready"], b + 1)
                    for c in range(2):
                        last = act.activation(vT[:, c, :], ps[:, 2 + c, :], ACT.Copy)
                    last.then_inc(s["vT_ready"], 1)
                    act.wait_ge(s["za_ready"], b + 1)
                    act.activation(ze[:, :], za[:, :], ACT.Exp)
                    act.wait_ge(s["g_ready"], b + 1)
                    act.activation(ge[:, :, :].rearrange("p (a i) c -> p a i c", a=2), gps, ACT.Exp,
                                   scale=-1.0).then_inc(s["ge_ready"], 1)
                    act.drain()
                    act.activation(ze[:, :], ze[:, :], ACT.Ln, bias=1.0).then_inc(s["zl_ready"], 1)
                    act.activation(qT[:, :], ps[:, 0, :], ACT.Copy, scale=GLA_SCALE).then_inc(s["qT_ready"], 1)
                    act.wait_ge(s["lg_ready"], b + 1)
                    act.activation(decay[:, :], za[:, :], ACT.Exp,
                                   scale=1.0 / GATE_NORMALIZER).then_inc(s["decay_ready"], 1)
                    act.wait_ge(s["qs_read"], b * GLA_DV + GLA_DV + 2)
                    act.activation(osq[:, :, :, :].rearrange("p (a i) j h -> p a (i j h)", a=2), ps[:, 2:4, :],
                                   ACT.Square).then_inc(s["osq_ready"], 1)
                    act.wait_ge(s["ot_ready"], b + 1)
                    for c in range(DC):
                        last = act.activation(ogT[:, c, :], ps[:, 4 + c, :], ACT.Copy)
                    last.then_inc(s["ogT_ready"], 1)

            @block.tensor
            def _(pe):
                ln.first_free(pe)
                for _ in range(2):
                    pe.nop().then_inc(s["qs_read"], 1)
                with pe.Fori(0, B) as b:
                    ln.turn(pe, g, banks, b)
                    pe.wait_ge(ln.xnT_ready, b + 1)

                    def turned(bank, weights, rows, ready):
                        for c in range(DC):
                            last = pe.matmul(ps[0:rows, bank, :], weights[:, c, :], ln.xnT[:, c, :],
                                             start=(c == 0), stop=(c == DC - 1))
                        last.then_inc(s[ready], 1)

                    turned(4, g["gla_wgk1"], GLA_LR, "z1_ready")
                    turned(0, g["gla_wq"], P, "q_ready")
                    pe.wait_ge(s["z1_copied"], b + 1)
                    pe.matmul(ps[:, 5, :], g["gla_wgk2"][:, :], z1[:, :], start=True,
                              stop=True).then_inc(s["z_ready"], 1)
                    for i in range(TI):
                        for c in range(DC):
                            last = pe.matmul(ps[:, 6 + i // 2, (i % 2) * D:(i % 2 + 1) * D],
                                             ln.xnT[:, c, i * P:(i + 1) * P], g["gla_wg"][:, c, :],
                                             start=(c == 0), stop=(c == DC - 1))
                    last.then_inc(s["g_ready"], 1)
                    turned(1, g["gla_wk"], P, "k_ready")
                    turned(2, g["gla_wv"][:, :, 0:P], P, "q_ready")
                    turned(3, g["gla_wv"][:, :, P:D], P, "v_ready")
                    with pe.Fori(0, 2) as half:
                        pe.wait_ge(s["kT_ready"], b + 1)
                        pe.wait_ge(s["vT_ready"], b + 1)
                        pe.wait_ge(s["qT_ready"], b + 1)
                        def repeat(j):
                            pe.wait_ge(s["kv_ready"], b * GLA_DV + half * 8 + j + 1)
                            pe.matmul(ps[:, j % 2, :], g["gla_sel"][:, j, :], vT[:, half, :], start=True,
                                      stop=True).then_inc(s["vrep_ready"], 1)

                        repeat(0)
                        for j in range(8):
                            if j < 7:
                                repeat(j + 1)
                            pe.wait_ge(s["qs_ready"], b * GLA_DV + half * 8 + j + 3)
                            for i in range(TI):
                                last = pe.matmul(ps[:, 2 + i // 2, bass.ds((i % 2) * D + half * P + j * GLA_H, GLA_H)],
                                                 qs[:, j % 2, i * P:(i + 1) * P], g["gla_hsum"][:, :],
                                                 start=True, stop=True)
                            last.then_inc(s["qs_read"], 1)
                    pe.wait_ge(s["og_ready"], b + 1)
                    for c in range(DC):
                        for i in range(TI):
                            last = pe.transpose(ps[:, 4 + c, i * P:(i + 1) * P],
                                                og[:, i, c * 8:(c + 1) * 8, :].rearrange("p j h -> p (j h)"),
                                                ident[:, :])
                    last.then_inc(s["ot_ready"], 1)
                    pe.wait_ge(s["ogT_ready"], b + 1)
                    for i in range(TI):
                        for c in range(DC):
                            last = pe.matmul(ps[:, 6 + i // 2, (i % 2) * D:(i % 2 + 1) * D],
                                             ogT[:, c, i * P:(i + 1) * P], g["gla_wo"][:, c, :],
                                             start=(c == 0), stop=(c == DC - 1))
                    last.then_inc(s["y_ready"], 1)
        k.clear_sems()


WS_S, WS_K, WS_NB, WS_H = 16, 4, 2, 4
WS_HD = D // WS_H
WS_ROWS = B * WS_S
WS_EPS = 1e-6
SENTINEL = -3e38


def workspace_ffn(nc, g, tag):
    with ExitStack() as ctx:
        k = Kit(nc, ctx)
        x, ident = g["x"], g["ident"]

        def sb(name, shape):
            return k.sb(f"{tag}_{name}", shape)

        stats, mv = sb("stats", [P, TI, 6]), sb("mv", [P, TI, 2])
        ve, rstd = sb("ve", [P, TI]), sb("rstd", [P, TI])
        cw = sb("cw", [P, DC, WS_S])
        xf = sb("xf", [P, NT, D])
        xs = sb("xs", [P, TI, D])
        xsT = sb("xsT", [P, DC, S])
        xfT = sb("xfT", [P, DC, NT * P])
        junk = sb("junk", [P, D])
        msq, mse = sb("msq", [P, TI]), sb("mse", [P, TI])
        lg = sb("lg", [P, TI, WS_ROWS])
        lt = sb("lt", [WS_ROWS, S + 8])
        top, match = sb("top", [WS_ROWS, 8]), sb("match", [WS_ROWS, 8])
        ntop = sb("ntop", [WS_ROWS, 1])
        etop = sb("etop", [WS_ROWS, WS_K])
        zsum, rz = sb("zsum", [WS_ROWS, 1]), sb("rz", [WS_ROWS, 1])
        elt = sb("elt", [WS_ROWS, S])
        marked = sb("marked", [WS_ROWS, S + 8])
        chosen = sb("chosen", [WS_ROWS, S])
        selw = sb("selw", [WS_ROWS, S])
        selT = sb("selT", [P, TI, WS_ROWS])
        xselT = sb("xselT", [P, DC, WS_ROWS])
        ws = sb("ws", [WS_ROWS, D])
        wsum, wsq = sb("wsum", [WS_ROWS, D]), sb("wsq", [WS_ROWS, D])
        wss, wse, wsr = sb("wss", [WS_ROWS, 1]), sb("wse", [WS_ROWS, 1]), sb("wsr", [WS_ROWS, 1])
        wsT = sb("wsT", [P, DC, WS_ROWS])
        kbd = sb("kbd", [P, 2, B, 2, WS_S])
        vbd = sb("vbd", [P, 2, B, 2, WS_S])
        m = sb("m", [P, DC, 2, B, 2 * WS_S])
        cb = sb("cb", [1, 2, B, 2 * WS_S])
        nb_w = sb("nb", [65, B, D])
        ones = sb("ones", [1, P])
        amax, al = sb("amax", [P, TI * WS_H]), sb("al", [P, TI * WS_H])
        ar = sb("ar", [P, TI * WS_H])
        ash = sb("ash", [P, TI * WS_H, WS_S])
        att = sb("att", [P, TI, WS_H * WS_S])
        attT = sb("attT", [65, S])
        ps = k.ps(tag + "_ps", [P, 8, 512])
        names = ("setup", "bias_loaded", "var_ready", "rstd_ready", "xs_ready", "xt_ready", "xsT_ready", "xfT_ready",
                 "msq_ready", "r_ready", "lg_ready", "lg_done", "lt_ready", "ntop_ready", "exp_ready", "selw_ready",
                 "st_ready", "selT_ready", "xsel_ready", "xselT_ready", "written", "wss_ready", "wsr_ready",
                 "ws_ready", "wt_ready", "wsT_ready", "kv_ready", "bd_ready", "m_ready", "cb_ready", "nb_ready",
                 "fold_v", "fold_a", "xr_ready", "a_ready", "ash_ready", "ae_ready", "att_ready", "at_ready",
                 "attT_ready", "xb_ready", "xsum_ready", "m2_ready", "r2_ready")
        s = {n: k.sem(f"{tag}_{n}") for n in names}
        bias = g["ws_in_b"]

        with nc.Block() as block:
            @block.sync
            def _(sp):
                sp.dma_start(nb_w[64:65, :, :], g["ws_out_b"][:, :, :]).then_inc(s["bias_loaded"], 16)
                sp.dma_start(ws[:, :], g["ws_start"][:, :]).then_inc(s["bias_loaded"], 16)

            @block.vector
            def _(dve):
                dve.memset(kbd[:, :, :, :, :], 0.0)
                dve.memset(vbd[:, :, :, :, :], 0.0)
                dve.memset(ones[:, :], 1.0)
                dve.memset(attT[64:65, :], 1.0)
                dve.memset(lt[:, S:], SENTINEL)
                dve.memset(match[:, WS_K:], SENTINEL)
                for c in range(DC):
                    last = dve.tensor_scalar(cw[:, c, :], g["ws_cw"][:, c, :], g["ws_pre"][:, c:c + 1], None, ALU.mult)
                last.then_inc(s["setup"], 1)
                with dve.Fori(0, B) as b:
                    layer_norm_stats(dve, stats, mv, ve[:, :], [x[:, b * TI + i, :] for i in range(TI)], LN_EPS,
                                     s["var_ready"])
                    dve.wait_ge(s["rstd_ready"], b + 1)
                    for i in range(TI):
                        dve.tensor_scalar(xf[:, b * TI + i, :], x[:, b * TI + i, :], mv[:, i, 0:1], rstd[:, i:i + 1],
                                          ALU.subtract, ALU.mult)
                dve.nop().then_inc(s["xt_ready"], 1)
                dve.drain()
                with dve.Fori(0, WS_NB) as r:
                    with dve.Fori(0, B) as b:
                        n = r * B + b
                        dve.wait_ge(s["xt_ready"], n + 1)
                        dve.wait_ge(s["msq_ready"], n + 1)
                        dve.tensor_copy(xs[:, :, :], xf[:, bass.ts(b, TI), :]).then_inc(s["xs_ready"], 1)
                        dve.wait_ge(s["lg_ready"], n + 1)
                        dve.wait_ge(s["r_ready"], n + 1)
                        dve.tensor_tensor(lg[:, :, bass.ts(b, WS_S)],
                                          ps[:, 2, 0:TI * WS_S].rearrange("p (i s) -> p i s", i=TI),
                                          rstd[:, :].unsqueeze(2).to_broadcast([P, TI, WS_S]),
                                          ALU.mult).then_inc(s["lg_done"], 1)
                    dve.wait_ge(s["lt_ready"], r + 1)
                    dve.tensor_scalar(lt[:, 0:S], ps[0:WS_ROWS, 3, :], g["ws_cb"][:, 0:1], None, ALU.add)
                    dve.drain()
                    dve.max(top[:, :], lt[:, 0:S])
                    dve.drain()
                    dve.tensor_scalar(ntop[:, :], top[:, 0:1], -1.0, None, ALU.mult).then_inc(s["ntop_ready"], 1)
                    dve.tensor_copy(match[:, 0:WS_K], top[:, 0:WS_K])
                    dve.drain()
                    dve.match_replace(marked[:, :], match[:, :], lt[:, :], -SENTINEL)
                    dve.drain()
                    dve.tensor_tensor(chosen[:, :], marked[:, 0:S], lt[:, 0:S], ALU.not_equal)
                    dve.wait_ge(s["exp_ready"], r + 1)
                    dve.tensor_reduce(zsum[:, :], etop[:, :], AX.X, ALU.add)
                    dve.drain()
                    dve.reciprocal(rz[:, :], zsum[:, :])
                    dve.drain()
                    dve.scalar_tensor_tensor(selw[:, :], elt[:, :], rz[:, 0:1], chosen[:, :], ALU.mult,
                                             ALU.mult).then_inc(s["selw_ready"], 1)
                    dve.wait_ge(s["st_ready"], r + 1)
                    dve.tensor_copy(selT[:, :, :], ps[:, 4, 0:TI * WS_ROWS].rearrange("p (i s) -> p i s", i=TI))\
                       .then_inc(s["selT_ready"], 1)
                    dve.wait_ge(s["xsel_ready"], r + 1)
                    dve.tensor_copy(xselT[:, :, :], ps[:, 5, 0:DC * WS_ROWS].rearrange("p (c s) -> p c s", c=DC))\
                       .then_inc(s["xselT_ready"], 1)
                    dve.wait_ge(s["written"], r + 1)
                    dve.wait_ge(s["bias_loaded"], 32)
                    dve.tensor_tensor(wsum[:, :], ps[0:WS_ROWS, 6, 0:D], ws[:, :], ALU.add)
                    dve.drain()
                    dve.tensor_tensor(wsq[:, :], wsum[:, :], wsum[:, :], ALU.mult)
                    dve.drain()
                    dve.tensor_reduce(wss[:, :], wsq[:, :], AX.X, ALU.add)
                    dve.drain()
                    dve.tensor_scalar(wse[:, :], wss[:, :], 1.0 / D, WS_EPS, ALU.mult, ALU.add)\
                       .then_inc(s["wss_ready"], 1)
                    dve.wait_ge(s["wsr_ready"], r + 1)
                    dve.scalar_tensor_tensor(ws[:, :], wsum[:, :], wsr[:, 0:1], g["ws_post"][0:WS_ROWS, :],
                                             ALU.mult, ALU.mult).then_inc(s["ws_ready"], 1)
                    dve.wait_ge(s["wt_ready"], r + 1)
                    dve.tensor_copy(wsT[:, :, :], ps[:, 7, 0:DC * WS_ROWS].rearrange("p (c s) -> p c s", c=DC))\
                       .then_inc(s["wsT_ready"], 1)
                    dve.wait_ge(s["kv_ready"], r + 1)
                    for oc in range(2):
                        for hh in range(2):
                            rows = slice(64 * hh, 64 * hh + 64)
                            kv = ps[rows, 3, :].rearrange("p (v o b s) -> p v o b s", v=4, o=2, b=B)
                            dve.tensor_scalar(kbd[rows, oc, :, hh, :], kv[:, 0, oc], bias[rows, 2 + oc:3 + oc],
                                              float(WS_HD ** -0.5), ALU.add, ALU.mult)
                            last = dve.tensor_scalar(vbd[rows, oc, :, hh, :], kv[:, 1, oc], bias[rows, 4 + oc:5 + oc],
                                                     None, ALU.add)
                    last.then_inc(s["bd_ready"], 1)
                    dve.wait_ge(s["m_ready"], r + 1)
                    dve.tensor_copy(m[:, :, :, :, :].rearrange("p c o b s -> p (c o b s)"), ps[:, 4, :])
                    dve.wait_ge(s["cb_ready"], r + 1)
                    dve.tensor_copy(cb[:, :, :, :].rearrange("p o b s -> p (o b s)"), ps[0:1, 5, 0:2 * P])\
                       .then_inc(s["fold_v"], 1)
                    with dve.Fori(0, B) as b:
                        n = r * B + b
                        dve.wait_ge(s["a_ready"], n + 2)
                        sc = ps[:, 0, 0:TI * WS_H * WS_S].rearrange("p (a s) -> p a s", s=WS_S)
                        dve.tensor_reduce(amax[:, :], sc, AX.X, ALU.max)
                        dve.drain()
                        dve.tensor_tensor(ash[:, :, :], sc, amax[:, :].unsqueeze(2).to_broadcast(
                            [P, TI * WS_H, WS_S]), ALU.subtract).then_inc(s["ash_ready"], 1)
                        dve.wait_ge(s["ae_ready"], n + 1)
                        dve.tensor_reduce(al[:, :], ash[:, :, :], AX.X, ALU.add)
                        dve.drain()
                        dve.reciprocal(ar[:, :], al[:, :])
                        dve.drain()
                        dve.tensor_tensor(att[:, :, :].rearrange("p i (h s) -> p (i h) s", s=WS_S), ash[:, :, :],
                                          ar[:, :].unsqueeze(2).to_broadcast([P, TI * WS_H, WS_S]),
                                          ALU.mult).then_inc(s["att_ready"], 1)
                        dve.wait_ge(s["xb_ready"], n + 1)
                        for i in range(TI):
                            xi = xf[:, b * TI + i, :]
                            last = dve.tensor_tensor(xs[:, i, :], ps[:, 2 + i // 2, (i % 2) * D:(i % 2 + 1) * D],
                                                     xi, ALU.add)
                        last.then_inc(s["xsum_ready"], 1)
                        dve.wait_ge(s["r2_ready"], n + 1)
                        for i in range(TI):
                            dve.scalar_tensor_tensor(xf[:, b * TI + i, :], xs[:, i, :], rstd[:, i:i + 1],
                                                     g["ws_post"][:, :], ALU.mult, ALU.mult)
                        dve.drain()
                with dve.Fori(0, NT) as i:
                    dve.tensor_tensor(x[:, i, :], xf[:, i, :], x[:, i, :], ALU.add)

            @block.gpsimd
            def _(pool):
                nh = g["neg_half"]
                with pool.Fori(0, B) as b:
                    pool.wait_ge(s["var_ready"], b + 1)
                    pool.tensor_tensor(rstd[:, :], ve[:, :], nh[:, 0:TI], ALU.pow).then_inc(s["rstd_ready"], 1)
                pool.nop().then_inc(s["xfT_ready"], 1)

                def row_scales():
                    pool.tensor_tensor(mse[:, :], msq[:, :], g["ws_eps"][:, 0:TI], ALU.add)
                    pool.drain()
                    return pool.tensor_tensor(rstd[:, :], mse[:, :], nh[:, 0:TI], ALU.pow)

                with pool.Fori(0, WS_NB) as r:
                    with pool.Fori(0, B) as b:
                        n = r * B + b
                        pool.wait_ge(s["msq_ready"], n + 2)
                        row_scales().then_inc(s["r_ready"], 1)
                        pool.drain()
                        pool.wait_ge(s["xsT_ready"], n + 1)
                        pool.tensor_copy(xfT[:, :, bass.ts(b, S)], xsT[:, :, :]).then_inc(s["xfT_ready"], 1)
                        pool.drain()
                    pool.wait_ge(s["wss_ready"], r + 1)
                    pool.tensor_tensor(wsr[:, :], wse[:, :], nh[0:WS_ROWS, 0:1], ALU.pow).then_inc(s["wsr_ready"], 1)
                    with pool.Fori(0, B) as b:
                        n = r * B + b
                        pool.wait_ge(s["m2_ready"], n + 1)
                        row_scales().then_inc(s["r2_ready"], 1)
                        pool.drain()

            @block.scalar
            def _(act):
                act.nop().then_inc(s["msq_ready"], 1)

                def mean_squares():
                    for i in range(TI):
                        last = act.activation(junk[:, :], xs[:, i, :], ACT.Square, scale=float(D ** -0.5),
                                              accum_out=msq[:, i:i + 1])
                        if i + 1 < TI:
                            act.drain()
                    return last

                with act.Fori(0, WS_NB) as r:
                    with act.Fori(0, B) as b:
                        n = r * B + b
                        act.wait_ge(s["xs_ready"], n + 1)
                        mean_squares().then_inc(s["msq_ready"], 1)
                        act.wait_ge(s["xt_ready"], n + 2)
                        act.wait_ge(s["xfT_ready"], n + 1)
                        for c in range(DC):
                            last = act.activation(xsT[:, c, :], ps[:, c, :], ACT.Copy)
                        last.then_inc(s["xsT_ready"], 1)
                    act.wait_ge(s["ntop_ready"], r + 1)
                    act.activation(etop[:, :], top[:, 0:WS_K], ACT.Exp, bias=ntop[:, 0:1])
                    act.activation(elt[:, :], lt[:, 0:S], ACT.Exp, bias=ntop[:, 0:1]).then_inc(s["exp_ready"], 1)
                    act.wait_ge(s["nb_ready"], r + 1)
                    act.activation(nb_w[0:64, :, :].rearrange("p (a b) d -> p a (b d)", a=2), ps[0:64, 6:8, :],
                                   ACT.Copy).then_inc(s["fold_a"], 1)
                    with act.Fori(0, B) as b:
                        n = r * B + b
                        act.wait_ge(s["xfT_ready"], r * B + B + 1)
                        act.wait_ge(s["a_ready"], n + 1)
                        act.activation(xsT[:, :, :], xfT[:, :, bass.ts(b, S)], ACT.Copy).then_inc(s["xr_ready"], 1)
                        act.wait_ge(s["ash_ready"], n + 1)
                        act.activation(ash[:, :, :], ash[:, :, :], ACT.Exp).then_inc(s["ae_ready"], 1)
                        act.wait_ge(s["at_ready"], n + 1)
                        act.activation(attT[0:64, :], ps[0:64, 1, :], ACT.Copy).then_inc(s["attT_ready"], 1)
                        act.wait_ge(s["xsum_ready"], n + 1)
                        mean_squares().then_inc(s["m2_ready"], 1)

            @block.tensor
            def _(pe):
                def turn_small(out, tile, rows):
                    return pe.matmul(out, tile, ident[0:rows, 0:rows], start=True, stop=True)

                pe.nop().then_inc(s["a_ready"], 1)
                pe.wait_ge(s["setup"], 1)
                with pe.Fori(0, WS_NB) as r:
                    with pe.Fori(0, B) as b:
                        n = r * B + b
                        pe.wait_ge(s["xs_ready"], n + 1)
                        for c in range(DC):
                            for i in range(TI):
                                last = pe.transpose(ps[:, c, i * P:(i + 1) * P], xs[:, i, c * P:(c + 1) * P],
                                                    ident[:, :])
                        last.then_inc(s["xt_ready"], 1)
                        pe.wait_ge(s["xsT_ready"], n + 1)
                        for i in range(TI):
                            for c in range(DC):
                                last = pe.matmul(ps[:, 2, i * WS_S:(i + 1) * WS_S], xsT[:, c, i * P:(i + 1) * P],
                                                 cw[:, c, :], start=(c == 0), stop=(c == DC - 1))
                        last.then_inc(s["lg_ready"], 1)
                    pe.wait_ge(s["lg_done"], r * B + B)
                    for i in range(TI):
                        last = turn_small(ps[0:WS_ROWS, 3, i * P:(i + 1) * P], lg[:, i, :], P)
                    last.then_inc(s["lt_ready"], 1)
                    pe.wait_ge(s["selw_ready"], r + 1)
                    for i in range(TI):
                        last = turn_small(ps[:, 4, i * WS_ROWS:(i + 1) * WS_ROWS], selw[:, i * P:(i + 1) * P], WS_ROWS)
                    last.then_inc(s["st_ready"], 1)
                    pe.wait_ge(s["selT_ready"], r + 1)
                    for c in range(DC):
                        for b in range(B):
                            for i in range(TI):
                                at = c * WS_ROWS + b * WS_S
                                last = pe.matmul(ps[:, 5, at:at + WS_S], xf[:, b * TI + i, c * P:(c + 1) * P],
                                                 selT[:, i, b * WS_S:(b + 1) * WS_S],
                                                 start=(i == 0), stop=(i == TI - 1))
                    last.then_inc(s["xsel_ready"], 1)
                    pe.wait_ge(s["xselT_ready"], r + 1)
                    for c in range(DC):
                        pe.matmul(ps[0:WS_ROWS, 6, 0:D], xselT[:, c, :], g["ws_write"][:, c, :], start=(c == 0),
                                  stop=False)
                    pe.matmul(ps[0:WS_ROWS, 6, 0:D], ones[:, 0:WS_ROWS], g["ws_write_b"][:, :], start=False,
                              stop=True).then_inc(s["written"], 1)
                    pe.wait_ge(s["ws_ready"], r + 1)
                    for c in range(DC):
                        last = turn_small(ps[:, 7, c * WS_ROWS:(c + 1) * WS_ROWS], ws[:, c * P:(c + 1) * P], WS_ROWS)
                    last.then_inc(s["wt_ready"], 1)
                    pe.wait_ge(s["wsT_ready"], r + 1)
                    for v, name in enumerate(("ws_wk", "ws_wv")):
                        for oc in range(2):
                            at = v * 2 * WS_ROWS + oc * WS_ROWS
                            for c in range(DC):
                                last = pe.matmul(ps[:, 3, at:at + WS_ROWS], g[name][:, c, oc * P:(oc + 1) * P],
                                                 wsT[:, c, :], start=(c == 0), stop=(c == DC - 1))
                    last.then_inc(s["kv_ready"], 1)
                    pe.wait_ge(s["bd_ready"], r + 1)
                    for c in range(DC):
                        for oc in range(2):
                            at = (c * 2 + oc) * P
                            last = pe.matmul(ps[:, 4, at:at + P], g["ws_wq"][:, oc, c * P:(c + 1) * P],
                                             kbd[:, oc, :, :, :].rearrange("p b h s -> p (b h s)"),
                                             start=True, stop=True)
                    last.then_inc(s["m_ready"], 1)
                    for oc in range(2):
                        last = pe.matmul(ps[0:1, 5, oc * P:(oc + 1) * P], bias[:, oc:oc + 1],
                                         kbd[:, oc, :, :, :].rearrange("p b h s -> p (b h s)"),
                                         start=True, stop=True)
                    last.then_inc(s["cb_ready"], 1)
                    for b in range(B):
                        for oc in range(2):
                            last = pe.matmul(ps[32 * oc:32 * oc + 32, 6 + b // 2, (b % 2) * D:(b % 2 + 1) * D],
                                             vbd[:, oc, b, :, :].rearrange("p h s -> p (h s)"),
                                             g["ws_out"][:, oc, :], start=True, stop=True)
                    last.then_inc(s["nb_ready"], 1)
                    with pe.Fori(0, B) as b:
                        n = r * B + b
                        pe.wait_ge(s["fold_v"], r + 1)
                        pe.wait_ge(s["fold_a"], r + 1)
                        pe.wait_ge(s["xr_ready"], n + 1)
                        for i in range(TI):
                            out = ps[:, 0, i * 64:(i + 1) * 64].rearrange("p (o s) -> p o s", o=2)
                            for c in range(DC):
                                last = pe.matmul(out, xsT[:, c, i * P:(i + 1) * P], m[:, c, :, b, :],
                                                 start=(c == 0), stop=False)
                            last = pe.matmul(out, ones[:, :], cb[:, :, b, :], start=False, stop=True)
                        last.then_inc(s["a_ready"], 1)
                        pe.wait_ge(s["att_ready"], n + 1)
                        for i in range(TI):
                            last = turn_small(ps[0:64, 1, i * P:(i + 1) * P], att[:, i, :], P)
                        last.then_inc(s["at_ready"], 1)
                        pe.wait_ge(s["attT_ready"], n + 1)
                        for i in range(TI):
                            last = pe.matmul(ps[:, 2 + i // 2, (i % 2) * D:(i % 2 + 1) * D],
                                             attT[:, i * P:(i + 1) * P], nb_w[:, b, :], start=True, stop=True)
                        last.then_inc(s["xb_ready"], 1)
        k.clear_sems()


LORA_N, LORA_RANK = 4, 16
LORA_ROWS = LORA_N * LORA_RANK
LORA_H = 16
LORA_HD = D // LORA_H
LORA_SCALE = float(LORA_HD ** -0.5)
LORA_G = LORA_H // 4


def lora_attention(nc, g):
    with ExitStack() as ctx:
        k = Kit(nc, ctx)
        x, ident, ident_b, mask_b, rope = (g[n] for n in ("x", "ident", "ident_b", "mask_b", "lora_rope"))
        ln = Normed(k, "lora")
        starts = k.sb("lora_startf", [LORA_ROWS, LORA_N])
        begun = k.sb("lora_begun", [LORA_ROWS, B, LORA_N])
        which = k.sb("lora_which", [LORA_ROWS, B])
        mine = k.sb("lora_mine", [LORA_ROWS, B])
        am = k.sb("lora_am", [LORA_ROWS, 4, D])
        wqk = k.sb("lora_wqk", [P, DC, 2, LORA_H, 32])
        wvo = k.sb("lora_wvo", [P, 2, DC, D])
        wst = k.sb("lora_wst", [P, DC, 2, P])
        qkT = k.sb("lora_qkT", [P, 2, S])
        swp = k.sb("lora_swp", [P, S])
        rot1 = k.sb("lora_rot1", [P, S])
        rot2 = k.sb("lora_rot2", [P, S])
        v = k.sb("lora_v", [P, TI, D])
        nmax = k.sb("lora_nmax", [P, 2, TI])
        lsum = k.sb("lora_lsum", [P, 2, TI])
        rl = k.sb("lora_rl", [P, 2, TI])
        probs = k.sb("lora_probs", [P, 2, CAUSAL_COLS])
        probsT = k.sb("lora_probsT", [P, 2, CAUSAL_COLS])
        on = k.sb("lora_on", [P, TI, LORA_H, LORA_HD])
        onT = k.sb("lora_onT", [P, DC, S])
        sc = k.ps("lora_sc", [P, 2, 3 * 512])
        po = k.ps("lora_po", [P, 512])
        pq = k.ps("lora_pq", [P, 512])
        out2 = po[:, 0:2 * TI * LORA_HD].rearrange("p (j q c) -> p j q c", j=2, q=TI)

        def bank(n):
            return sc[:, n // 3, (n % 3) * 512:(n % 3 + 1) * 512]

        names = ("setup", "am_ready", "fold_ready", "w_ready", "v_ready", "v_copied", "staged", "pj_ready",
                 "rope_in", "rope_done", "s_ready", "max_ready", "e_ready", "t_ready", "pt_a", "pt_b", "o_ready",
                 "o_done", "ot_ready", "onT_ready", "y_ready", "x_done")
        s = {n: k.sem("lora_" + n) for n in names}
        PAIRS = LORA_H // 2

        with nc.Block() as block:
            @block.vector
            def _(dve):
                dve.nop().then_inc(s["rope_in"], 1)
                dve.nop().then_inc(s["o_done"], 1)
                dve.tensor_copy(starts[:, :], g["lora_starts"][:, :])
                dve.memset(wqk[:, :, :, :, 16:32], 0.0)
                dve.tensor_scalar(g["lora_wq"][:, :, :], g["lora_wq"][:, :, :], LORA_SCALE, None, ALU.mult)
                dve.drain()
                dve.tensor_tensor(begun[:, :, :], starts[:, :].unsqueeze(1).to_broadcast([LORA_ROWS, B, LORA_N]),
                                  g["lora_batch"][:, :].unsqueeze(2).to_broadcast([LORA_ROWS, B, LORA_N]), ALU.is_le)
                dve.drain()
                dve.tensor_reduce(which[:, :], begun[:, :, :], AX.X, ALU.add)
                dve.drain()
                dve.tensor_scalar(mine[:, :], which[:, :], -1.0, 0.0, ALU.add, ALU.max)
                dve.drain()
                dve.tensor_scalar(which[:, :], mine[:, :], float(LORA_N - 1), None, ALU.min)
                dve.drain()
                dve.tensor_scalar(mine[:, :], which[:, :], g["lora_row"][:, 0:1], None, ALU.is_equal)
                dve.drain()
                with dve.Fori(0, B) as b:
                    for n, name in enumerate("qkvo"):
                        last = dve.tensor_scalar(am[:, n, :], g["lora_a" + name][:, :], mine[:, bass.ds(b, 1)],
                                                 LORA_SCALE if name == "q" else 1.0, ALU.mult, ALU.mult)
                    last.then_inc(s["am_ready"], 1)
                    ln.norm(dve, x, b)
                    dve.wait_ge(s["fold_ready"], b + 1)
                    for n, name in enumerate("qkvo"):
                        for c in range(DC):
                            folded = bank(n)[:, c * D:(c + 1) * D]
                            if n < 2:
                                last = dve.tensor_tensor(wqk[:, c, n, :, 0:16],
                                                         folded.rearrange("p (h e) -> p h e", e=16),
                                                         g["lora_w" + name][:, c, :].rearrange("p (h e) -> p h e", e=16),
                                                         ALU.add)
                            else:
                                last = dve.tensor_tensor(wvo[:, n - 2, c, :], folded, g["lora_w" + name][:, c, :],
                                                         ALU.add)
                    last.then_inc(s["w_ready"], 1)

                    def rope_half(u, kind):
                        dve.wait_ge(s["pj_ready"], 2 * u + kind + 2)
                        dve.wait_ge(s["rope_done"], 2 * u + kind + 1)
                        dve.tensor_tensor(rot1[:, :], pq[:, :], rope[:, 0, :], ALU.mult)
                        dve.stream_shuffle(swp[:, :], pq[:, :], [*range(8, 16), *range(8), *range(16, 32)])\
                           .then_inc(s["rope_in"], 1)

                    rope_half(b * LORA_G, 0)
                    rope_half(b * LORA_G, 1)

                    def pair(u, gi, pr, last_group):
                        n = 2 * u + pr
                        for j in range(2):
                            for qi in CAUSAL_ORDER:
                                if qi != 0:
                                    dve.wait_ge(s["s_ready"], 6 * n + 3 * j + CAUSAL_BANK[qi] + 1)
                                at = CAUSAL_COL[qi]
                                red = dve.tensor_reduce(nmax[:, j, qi:qi + 1], sc[:, j, at:at + (qi + 1) * P],
                                                        AX.X, ALU.max, negate=True)
                                if qi != 2:
                                    red.then_inc(s["max_ready"], 1)
                        for j in range(2):
                            if pr == 1 and not last_group:
                                rope_half(u + 1, j)
                            dve.wait_ge(s["t_ready"], 6 * n + 3 * j + 2)
                            dve.tensor_copy(probsT[:, j, S:2 * S], sc[:, j, S:2 * S])
                            dve.wait_ge(s["t_ready"], 6 * n + 3 * j + 3)
                            dve.tensor_copy(probsT[:, j, 2 * S:CAUSAL_COLS],
                                            sc[:, j, 2 * S:CAUSAL_COLS]).then_inc(s["pt_b"], 1)
                        dve.reciprocal(rl[:, :, :], lsum[:, :, :])
                        dve.drain()
                        dve.wait_ge(s["o_ready"], n + 1)
                        dve.tensor_tensor(on[:, :, bass.ds(4 * gi + 2 * pr, 2), :].rearrange("p q j r -> p j q r"),
                                          out2, rl[:, :, :].unsqueeze(3).to_broadcast([P, 2, TI, LORA_HD]),
                                          ALU.mult).then_inc(s["o_done"], 1)

                    with dve.Fori(0, LORA_G - 1) as gi:
                        for pr in range(2):
                            pair(b * LORA_G + gi, gi, pr, False)
                    for pr in range(2):
                        pair(b * LORA_G + LORA_G - 1, LORA_G - 1, pr, True)
                    dve.wait_ge(s["y_ready"], b + 1)
                    for i in range(TI):
                        xi = x[:, b * TI + i, :]
                        last = dve.tensor_tensor(xi, bank(2 + i // 2)[:, (i % 2) * D:(i % 2 + 1) * D], xi, ALU.add)
                    last.then_inc(s["x_done"], 1)

            @block.gpsimd
            def _(pool):
                pool.nop().then_inc(s["rope_done"], 1)
                with pool.Fori(0, B) as b:
                    ln.invert(pool, g, b)

                    def stage(gi):
                        pool.tensor_copy(wst[:, :, :, :].rearrange("p c k (h e) -> p (c k) h e", h=4),
                                         wqk[:, :, :, bass.ds(4 * gi, 4), :].rearrange("p c k h e -> p (c k) h e"))\
                            .then_inc(s["staged"], 1)

                    def rotate(u, kind):
                        pool.wait_ge(s["rope_in"], 2 * u + kind + 2)
                        pool.tensor_tensor(rot2[:, :], swp[:, :], rope[:, 1, :], ALU.mult)
                        pool.drain()
                        pool.tensor_tensor(qkT[:, kind, :], rot1[:, :], rot2[:, :], ALU.add)\
                            .then_inc(s["rope_done"], 1)
                        pool.drain()

                    with pool.Fori(0, LORA_G) as gi:
                        u = b * LORA_G + gi
                        pool.wait_ge(s["w_ready"], b + 1)
                        pool.wait_ge(s["pj_ready"], 2 * u + 1)
                        stage(gi)
                        rotate(u, 0)
                        rotate(u, 1)

            @block.scalar
            def _(act):
                with act.Fori(0, B) as b:
                    ln.copy(act, [bank(4), bank(5)], b)
                    act.wait_ge(s["v_ready"], b + 1)
                    for h in range(2):
                        last = act.activation(v[:, 2 * h:2 * h + 2, :].rearrange("p i d -> p (i d)"), bank(h),
                                              ACT.Copy)
                    last.then_inc(s["v_copied"], 1)

                    with act.Fori(0, PAIRS) as p:
                        n = b * PAIRS + p
                        for j in range(2):
                            for qi in CAUSAL_ORDER:
                                if qi != 0:
                                    act.wait_ge(s["max_ready"], 6 * n + 3 * j + CAUSAL_BANK[qi] + 1)
                                at = CAUSAL_COL[qi]
                                ex = act.activation(probs[:, j, at:at + (qi + 1) * P], sc[:, j, at:at + (qi + 1) * P],
                                                    ACT.Exp, bias=nmax[:, j, qi:qi + 1],
                                                    accum_out=lsum[:, j, qi:qi + 1])
                                if qi != 2:
                                    ex.then_inc(s["e_ready"], 1)
                        for j in range(2):
                            act.wait_ge(s["t_ready"], 6 * n + 3 * j + 1)
                            act.activation(probsT[:, j, 0:S], sc[:, j, 0:S], ACT.Copy).then_inc(s["pt_a"], 1)
                    act.wait_ge(s["ot_ready"], b + 1)
                    for c in range(DC):
                        last = act.activation(onT[:, c, :], bank(c), ACT.Copy)
                    last.then_inc(s["onT_ready"], 1)

            @block.tensor
            def _(pe):
                ln.first_free(pe)
                pe.nop().then_inc(s["pj_ready"], 1)
                with pe.Fori(0, B) as b:
                    pe.wait_ge(s["am_ready"], b + 1)
                    for n, name in enumerate("qkvo"):
                        for c in range(DC):
                            last = pe.matmul(bank(n)[:, c * D:(c + 1) * D], am[:, n, c * P:(c + 1) * P],
                                             g["lora_b" + name][:, :], start=True, stop=True)
                    last.then_inc(s["fold_ready"], 1)
                    ln.turn(pe, g, [bank(4), bank(5)], b)
                    pe.wait_ge(ln.xnT_ready, b + 1)
                    pe.wait_ge(s["w_ready"], b + 1)
                    for i in range(TI):
                        for c in range(DC):
                            last = pe.matmul(bank(i // 2)[:, (i % 2) * D:(i % 2 + 1) * D],
                                             ln.xnT[:, c, i * P:(i + 1) * P], wvo[:, 0, c, :],
                                             start=(c == 0), stop=(c == DC - 1))
                    last.then_inc(s["v_ready"], 1)

                    def project(u, kind):
                        pe.wait_ge(s["staged"], u + 1)
                        pe.wait_ge(s["rope_in"], 2 * u + kind + 1)
                        for c in range(DC):
                            last = pe.matmul(pq[:, :], wst[:, c, kind, :], ln.xnT[:, c, :], start=(c == 0),
                                             stop=(c == DC - 1))
                        last.then_inc(s["pj_ready"], 1)

                    project(b * LORA_G, 0)
                    project(b * LORA_G, 1)

                    def pair(u, pr, last_group):
                        n = 2 * u + pr
                        pe.wait_ge(s["v_copied"], b + 1)
                        pe.wait_ge(s["rope_done"], 2 * u + 3)
                        for j in range(2):
                            rows = slice(32 * (2 * pr + j), 32 * (2 * pr + j) + 32)
                            for qi in CAUSAL_ORDER:
                                at = CAUSAL_COL[qi]
                                pe.matmul(sc[:, j, at:at + (qi + 1) * P], qkT[rows, 0, qi * P:(qi + 1) * P],
                                          qkT[rows, 1, 0:(qi + 1) * P], start=True, stop=False)
                                last = pe.matmul(sc[:, j, at + qi * P:at + (qi + 1) * P], ident_b[:, :], mask_b[:, :],
                                                 start=False, stop=True)
                                if qi != 2:
                                    last.then_inc(s["s_ready"], 1)
                        for j in range(2):
                            if pr == 1 and not last_group:
                                project(u + 1, j)
                            for qi in CAUSAL_ORDER:
                                if qi != 0:
                                    pe.wait_ge(s["e_ready"], 6 * n + 3 * j + CAUSAL_BANK[qi] + 1)
                                for kj in range(qi + 1):
                                    at = CAUSAL_COL[qi] + kj * P
                                    last = pe.transpose(sc[:, j, at:at + P], probs[:, j, at:at + P], ident[:, :])
                                if qi != 2:
                                    last.then_inc(s["t_ready"], 1)
                        pe.wait_ge(s["o_done"], n + 1)
                        for j in range(2):
                            pe.wait_ge(s["pt_a"], 2 * n + j + 1)
                            pe.wait_ge(s["pt_b"], 2 * n + j + 1)
                            head = values(u, 2 * pr + j)
                            for qi in range(TI):
                                for kj in range(qi + 1):
                                    at = CAUSAL_COL[qi] + kj * P
                                    last = pe.matmul(out2[:, j, qi, :], probsT[:, j, at:at + P],
                                                     v[:, kj, head], start=(kj == 0), stop=(kj == qi))
                        last.then_inc(s["o_ready"], 1)

                    with pe.Fori(0, LORA_G - 1) as gi:
                        def values(u, h):
                            return bass.ds((4 * gi + h) * LORA_HD, LORA_HD)

                        for pr in range(2):
                            pair(b * LORA_G + gi, pr, False)

                    def values(u, h):
                        return bass.ds((LORA_H - 4 + h) * LORA_HD, LORA_HD)

                    for pr in range(2):
                        pair(b * LORA_G + LORA_G - 1, pr, True)

                    pe.wait_ge(s["o_done"], b * PAIRS + PAIRS + 1)
                    for c in range(DC):
                        for i in range(TI):
                            last = pe.transpose(bank(c)[:, i * P:(i + 1) * P],
                                                on[:, i, 8 * c:8 * c + 8, :].rearrange("p h e -> p (h e)"), ident[:, :])
                    last.then_inc(s["ot_ready"], 1)
                    pe.wait_ge(s["onT_ready"], b + 1)
                    for i in range(TI):
                        for c in range(DC):
                            last = pe.matmul(bank(2 + i // 2)[:, (i % 2) * D:(i % 2 + 1) * D],
                                             onT[:, c, i * P:(i + 1) * P], wvo[:, 1, c, :],
                                             start=(c == 0), stop=(c == DC - 1))
                    last.then_inc(s["y_ready"], 1)
        k.clear_sems()


def rope_tables(length, dim, theta=10000.0):
    inv = (1.0 / theta ** (np.arange(0, dim, 2, dtype=np.float32) / np.float32(dim))).astype(np.float32)
    ang = np.arange(length, dtype=np.float32)[:, None] * inv
    return np.cos(ang).astype(np.float32), np.sin(ang).astype(np.float32)


def shape_constants():
    c = {}
    c["ident"] = np.eye(P, dtype=np.float32)
    causal = np.where(np.arange(P)[None, :] <= np.arange(P)[:, None], 0.0, NEG).astype(np.float32)
    c["mask"] = causal
    cos, sin = rope_tables(S, MLA_DR)
    q = np.arange(2)[:, None, None]
    e = np.arange(2)[None, :, None]
    r = np.arange(16)[None, None, :]
    freq = (16 * q + r + 0 * e).reshape(-1)
    sign = np.where(e + 0 * (q + r) == 0, -1.0, 1.0).reshape(-1).astype(np.float32)
    cn, sn = cos[:, freq], sin[:, freq] * sign
    t = np.stack([cn, sn], 1)
    c["ropeN"] = t.reshape(TI, P, 2, MLA_DR).transpose(1, 0, 2, 3)
    c["ropeT"] = np.concatenate([t, t], 2).transpose(2, 1, 0)
    hj, hk = np.arange(P) // 8, np.arange(P) // 8
    same = (hj[:, None] == hk[None, :])
    c["gla_sel"] = np.stack([same & (np.arange(P)[:, None] % 8 == j) for j in range(8)], 1).astype(np.float32)
    c["gla_hsum"] = (hk[:, None] == np.arange(GLA_H)[None, :]).astype(np.float32)
    cos, sin = rope_tables(S, LORA_HD)
    pad = np.zeros((S, 16), np.float32)
    t = np.stack([np.concatenate([cos, cos, pad], 1), np.concatenate([-sin, sin, pad], 1)], 1)
    c["lora_rope"] = np.tile(t, (1, 1, 4)).transpose(2, 1, 0)
    c["lora_row"] = (np.arange(LORA_ROWS)[:, None] // LORA_RANK).astype(np.float32)
    c["lora_batch"] = np.tile(np.arange(B, dtype=np.float32), (LORA_ROWS, 1))
    return {n: np.ascontiguousarray(a) for n, a in c.items()}


MLA_PE = np.array([2 * (16 * q + r) + e for q in range(2) for e in range(2) for r in range(16)])


def chunked(a):
    return a.reshape(-1, P, *a.shape[1:]).swapaxes(0, 1)


def lay_out(i):
    w = {}
    w["x"] = i["L0_attn_a_x"].reshape(NT, P, D).transpose(1, 0, 2)
    wq = i["L0_attn_a_wq"].reshape(D, MLA_H, MLA_DN + MLA_DR)
    w["mla_wqT"] = wq[:, :, :MLA_DN].transpose(2, 1, 0)
    pe = wq[:, :, MLA_DN:][:, :, MLA_PE].reshape(D, MLA_PAIRS, 2, MLA_DR)[:, :, ::-1]
    w["mla_wq_pe"] = chunked(pe.reshape(D, MLA_PAIRS, P))
    wkvb = i["L0_attn_a_wkv_b"].reshape(MLA_R, MLA_H, 2 * P)
    w["mla_wkT"] = wkvb[:, :, :P].transpose(2, 1, 0)
    w["mla_wvT"] = wkvb[:, :, P:].transpose(2, 1, 0)
    w["mla_wo"] = i["L0_attn_a_wo"].reshape(MLA_H, P, D).transpose(1, 0, 2)
    kva = i["L0_attn_a_wkv_a"]
    w["wkva"] = chunked(np.concatenate([kva[:, :MLA_R], kva[:, MLA_R:][:, MLA_PE]], 1))
    w["kvw"] = np.broadcast_to(i["L0_attn_a_kv_norm_w"], (P, MLA_R))
    w["ffn_w"] = chunked(i["L0_ffn_weight"])
    w["ffn_scale"] = np.broadcast_to(i["L0_ffn_scale"], (P, D))
    w["cos_g"] = chunked(i["L0_attn_b_g_norm"])
    w["cos_wq"] = chunked(i["L0_attn_b_Wq"])
    w["cos_wkv"] = chunked(i["L0_attn_b_Wkv"])
    w["cos_wout"] = chunked(i["L0_attn_b_Wout"])
    w["cos_gout"] = np.broadcast_to(i["L0_attn_b_g_out"], (P, D))
    for n, name in (("gla_wq", "Wq"), ("gla_wk", "Wk"), ("gla_wgk1", "Wgk1")):
        w[n] = chunked(i["L1_attn_a_" + name])
    wv = i["L1_attn_a_Wv"].reshape(D, GLA_H, 2, 8)
    w["gla_wv"] = chunked(wv.transpose(0, 2, 1, 3).reshape(D, D))
    w["gla_wg"] = chunked(i["L1_attn_a_Wg"].reshape(D, GLA_H, GLA_DV).swapaxes(1, 2).reshape(D, D))
    w["gla_wgk2"] = i["L1_attn_a_Wgk2"]
    w["gla_bgk2"] = i["L1_attn_a_bgk2"].reshape(P, 1)
    w["gla_normw"] = np.broadcast_to(i["L1_attn_a_norm_w"][:, None], (P, GLA_DV, GLA_H)).reshape(P, D)
    w["gla_wo"] = chunked(i["L1_attn_a_Wo"].reshape(GLA_H, GLA_DV, D).swapaxes(0, 1).reshape(D, D))
    def f(name):
        return i["L1_ffn_" + name]

    def slots(a):
        return np.broadcast_to(a, (B, *a.shape)).reshape(B * WS_S, -1)

    w["ws_start"] = slots(f("workspace"))
    w["ws_cw"] = chunked(f("compete_w").T)
    w["ws_cb"] = slots(f("compete_b")[:, None])
    w["ws_write"] = chunked(f("write_w").T)
    w["ws_write_b"] = f("write_b")[None]
    wq, wk, wv = f("in_proj_w")[:D], f("in_proj_w")[D:2 * D], f("in_proj_w")[2 * D:]
    w["ws_wq"], w["ws_wk"], w["ws_wv"] = chunked(wq), chunked(wk.T), chunked(wv.T)
    w["ws_in_b"] = chunked(f("in_proj_b"))
    w["ws_out"] = chunked(f("out_proj_w").T)
    w["ws_out_b"] = np.broadcast_to(f("out_proj_b"), (1, B, D))
    w["ws_pre"] = chunked(f("norm_pre_w"))
    w["ws_post"] = np.broadcast_to(f("norm_post_w"), (P, D))
    eo = (np.arange(LORA_H)[:, None, None] * LORA_HD + 2 * np.arange(8)[None, None, :]
          + np.arange(2)[None, :, None]).reshape(-1)
    for n in "qkvo":
        wt, bt = i["L1_attn_b_W" + n].T, i["L1_attn_b_B" + n].transpose(0, 2, 1).reshape(LORA_ROWS, D)
        if n in ("q", "k"):
            wt, bt = wt[:, eo], bt[:, eo]
        w["lora_w" + n], w["lora_b" + n] = chunked(wt), bt
        w["lora_a" + n] = i["L1_attn_b_A" + n].reshape(LORA_ROWS, D)
    w["lora_starts"] = np.broadcast_to(i["L1_attn_b_lora_start_indices"], (LORA_ROWS, LORA_N))
    w.update(shape_constants())
    return {n: np.ascontiguousarray(a) for n, a in w.items()}


def build(nc, w, out, stages=None):
    with ExitStack() as ctx:
        k = Kit(nc, ctx)
        g = {"x": k.sb("x", [P, NT, D]), "ident": k.sb("ident", [P, P]),
             "ident_b": k.sb("ident_b", [P, P], BF16), "mask_b": k.sb("mask_b", [P, P], BF16),
             "neg_half": k.sb("neg_half", [P, 64]), "pos_half": k.sb("pos_half", [P, 64]),
             "ws_eps": k.sb("ws_eps", [P, TI])}
        for n in ("x_loaded", "weights_loaded", "late_loaded", "consts_loaded"):
            g[n] = k.sem(n)
        def hold(names, loaded):
            for n in names:
                g[n] = k.sb(n, list(w[n].shape), w[n].dtype)
            return [(g[n][tuple(slice(None) for _ in w[n].shape)], w[n], loaded) for n in names]

        early = ["ffn_w", "ffn_scale", "cos_g", "cos_wq", "cos_wkv", "cos_wout", "cos_gout"]
        g["early_loads"] = hold(early, g["weights_loaded"])
        with ExitStack() as mla_ctx:
            m = Kit(nc, mla_ctx)
            g["wap"] = m.sb("wap", [P, DC, MLA_PAIRS, 2, P])
            g["wvo"] = m.sb("wvo", [P, MLA_PAIRS, D])
            g["wq_pe"] = m.sb("wq_pe", [P, DC, MLA_PAIRS, P])
            first = ["mask", "wkva", "kvw", "ropeT", "ropeN"]
            for n in first:
                g[n] = m.sb(n, list(w[n].shape))
            g["first_loads"] = [(g[n][tuple(slice(None) for _ in w[n].shape)], n) for n in ["ident"] + first]
            mla_fold_weights(nc, g, w)
            small_constants(nc, g)
            mla_attention(nc, g)
        late = ["gla_wq", "gla_wk", "gla_wgk1", "gla_wv", "gla_wg", "gla_wgk2", "gla_bgk2", "gla_normw", "gla_wo",
                "gla_sel", "gla_hsum", "ws_start", "ws_cw", "ws_cb", "ws_write", "ws_write_b", "ws_wq", "ws_wk",
                "ws_wv", "ws_in_b", "ws_out", "ws_out_b", "ws_pre", "ws_post",
                "lora_wq", "lora_wk", "lora_wv", "lora_wo", "lora_aq", "lora_ak", "lora_av", "lora_ao",
                "lora_bq", "lora_bk", "lora_bv", "lora_bo", "lora_starts", "lora_rope", "lora_row", "lora_batch"]
        wait_for_loads(nc, g["weights_loaded"], len(early))
        ternary_ffn(nc, g, "ffa", hold(late, g["late_loaded"]))
        cosine_attention(nc, g)
        ternary_ffn(nc, g, "ffb", [])
        wait_for_loads(nc, g["late_loaded"], len(late))
        gated_linear_attention(nc, g)
        workspace_ffn(nc, g, "wsa")
        lora_attention(nc, g)
        workspace_ffn(nc, g, "wsb")
        store_output(nc, g, out)


def wait_for_loads(nc, loaded, count):
    with nc.Block() as block:
        @block.sync
        def _(sp):
            sp.wait_ge(loaded, 16 * count)


def small_constants(nc, g):
    with nc.Block() as block:
        @block.vector
        def _(dve):
            dve.memset(g["neg_half"][:, :], -0.5)
            dve.memset(g["pos_half"][:, :], 0.5)
            dve.memset(g["ws_eps"][:, :], WS_EPS)
            dve.wait_ge(g["consts_loaded"], 16 * len(g["first_loads"]))
            dve.tensor_copy(g["ident_b"][:, :], g["ident"][:, :])
            dve.tensor_copy(g["mask_b"][:, :], g["mask"][:, :])


def store_output(nc, g, out):
    with ExitStack() as ctx:
        stored = Kit(nc, ctx).sem("stored")
        with nc.Block() as block:
            @block.sync
            def _(sp):
                sp.dma_start(out.rearrange("b (i p) d -> p (b i) d", p=P), g["x"][:, :, :]).then_inc(stored, 16)
                sp.wait_ge(stored, 16)


def kernel(**inputs):
    import concourse.bacc as bacc
    from concourse.bass_utils import run_bass_kernel_spmd

    nc = bacc.Bacc("TRN2", target_bir_lowering=False, num_devices=1)
    arrays = lay_out({n: np.asarray(a) for n, a in inputs.items()})
    w = {n: nc.dram_tensor("in_" + n, a.shape, mybir.dt.from_np(a.dtype), kind="ExternalInput").ap()
         for n, a in arrays.items()}
    out = nc.dram_tensor("out_0", (B, S, D), F32, kind="ExternalOutput").ap()
    build(nc, w, out)
    r = run_bass_kernel_spmd(nc, [{"in_" + n: a for n, a in arrays.items()}], core_ids=[0])
    return r.results[0]["out_0"]
```

```python
from contextlib import ExitStack

import numpy as np

import concourse.bass as bass
from concourse import mybir

F32 = mybir.dt.float32
BF16 = mybir.dt.bfloat16
ALU = mybir.AluOpType
ACT = mybir.ActivationFunctionType
AX = mybir.AxisListType

P = 128
B, S, D = 4, 512, 256
TI = S // P
NT = B * TI
DC = D // P
LN_EPS = 1e-5
NEG = -1e30

CAUSAL_ORDER = (3, 2, 0, 1)
CAUSAL_COL = {3: 0, 2: S, 0: S + 3 * P, 1: 2 * S}
CAUSAL_COLS = 2 * S + 2 * P
CAUSAL_BANK = {3: 0, 2: 1, 0: 1, 1: 2}


class Kit:

    def __init__(self, nc, ctx):
        self.nc, self.ctx = nc, ctx
        self.sems = []

    def sb(self, name, shape, dtype=F32):
        return self.ctx.enter_context(self.nc.sbuf_tensor(name, shape, dtype))

    def ps(self, name, shape, dtype=F32):
        return self.ctx.enter_context(self.nc.psum_tensor(name, shape, dtype))

    def sem(self, name):
        self.sems.append(self.ctx.enter_context(self.nc.semaphore(name)))
        return self.sems[-1]

    def clear_sems(self):
        with self.nc.Block() as block:
            @block.gpsimd
            def _(pool):
                for s in self.sems:
                    pool.sem_clear(s)


def layer_norm_stats(dve, stats, mv, var_eps, tiles, eps, var_ready):
    n = len(tiles)
    for i, x in enumerate(tiles):
        dve.bn_stats(stats[:, i, :], x)
    dve.drain()
    for i in range(n):
        dve.bn_aggr(mv[:, i, :], stats[:, i, :])
    dve.drain()
    dve.tensor_scalar(var_eps, mv[:, 0:n, 1], eps, None, ALU.add).then_inc(var_ready, 1)


MLA_H, MLA_DN, MLA_DR, MLA_R = 16, 128, 64, 64
MLA_SCALE = float((MLA_DN + MLA_DR) ** -0.5)
MLA_PAIRS = MLA_H // 2
MLA_EPS = 1e-6


def mla_fold_weights(nc, g, w):
    with ExitStack() as ctx:
        k = Kit(nc, ctx)
        wqT = k.sb("mla_wqT", [P, MLA_H, D])
        wkT = k.sb("mla_wkT", [P, MLA_H, MLA_R])
        wvT = k.sb("mla_wvT", [P, MLA_H, MLA_R])
        wo = k.sb("mla_wo", [P, MLA_H, D])
        fold = k.ps("mla_fold", [P, 8, 512])
        loaded = k.sem("mla_fold_loaded")
        loaded_v = k.sem("mla_fold_loaded_v")
        pe_loaded = k.sem("mla_fold_pe_loaded")
        q_folded = k.sem("mla_q_folded")
        v_folded = k.sem("mla_v_folded")
        wap, wvo = g["wap"], g["wvo"]

        with nc.Block() as block:
            @block.sync
            def _(sp):
                sp.dma_start(wqT[:, :, :], w["mla_wqT"]).then_inc(loaded, 16)
                sp.dma_start(g["x"][:, :, :], w["x"]).then_inc(g["x_loaded"], 16)
                sp.dma_start(wo[:, :, :], w["mla_wo"]).then_inc(loaded_v, 16)
                for dst, src, done in g["early_loads"]:
                    sp.dma_start(dst, src).then_inc(done, 16)

            @block.tensor
            def _(pe):
                pe.wait_ge(loaded, 32)
                for c in range(DC):
                    for h in range(MLA_H):
                        last = pe.matmul(fold[:, 2 * c + h // 8, (h % 8) * 64:(h % 8 + 1) * 64],
                                         wqT[:, h, c * P:(c + 1) * P], wkT[:, h, :], start=True, stop=True)
                        if h % 8 == 7:
                            last.then_inc(q_folded, 1)
                pe.wait_ge(loaded_v, 32)
                for h in range(MLA_H):
                    last = pe.matmul(fold[64 * (h % 2):64 * (h % 2) + 64, 4 + h // 4,
                                          (h // 2 % 2) * D:(h // 2 % 2 + 1) * D],
                                     wvT[:, h, :], wo[:, h, :], start=True, stop=True)
                    if h % 4 == 3:
                        last.then_inc(v_folded, 1)

            @block.vector
            def _(dve):
                dve.wait_ge(pe_loaded, 16)
                for c in range(DC):
                    dve.tensor_scalar(wap[:, c, :, 1, :], g["wq_pe"][:, c, :, :], MLA_SCALE, None, ALU.mult)
                for n in range(2 * DC):
                    dve.wait_ge(q_folded, n + 1)
                    dve.tensor_scalar(wap[:, n // 2, 4 * (n % 2):4 * (n % 2) + 4, 0, :],
                                      fold[:, n, :].rearrange("p (a b) -> p a b", a=4), MLA_SCALE, None, ALU.mult)

            @block.scalar
            def _(act):
                act.dma_start(wkT[:, :, :], w["mla_wkT"]).then_inc(loaded, 16)
                act.dma_start(g["wq_pe"][:, :, :, :], w["mla_wq_pe"]).then_inc(pe_loaded, 16)
                act.dma_start(wvT[:, :, :], w["mla_wvT"]).then_inc(loaded_v, 16)
                for dst, name in g["first_loads"]:
                    act.dma_start(dst, w[name]).then_inc(g["consts_loaded"], 16)
                for n in range(4):
                    act.wait_ge(v_folded, n + 1)
                    act.activation(wvo[:, 2 * n:2 * n + 2, :].rearrange("p a b -> p (a b)"), fold[:, 4 + n, :],
                                   ACT.Copy)
        k.clear_sems()


def mla_attention(nc, g):
    with ExitStack() as ctx:
        k = Kit(nc, ctx)
        x, wap, wvo, ident, ident_b, mask_b = (g[n] for n in ("x", "wap", "wvo", "ident", "ident_b", "mask_b"))
        wkva, kvw, ropeT, ropeN = (g[n] for n in ("wkva", "kvw", "ropeT", "ropeN"))
        stats = k.sb("stats", [P, TI, 6])
        mv = k.sb("mv", [P, TI, 2])
        ve = k.sb("ve", [P, 2, TI])
        rstd = k.sb("rstd", [P, 2, TI])
        xn = k.sb("xn", [P, TI, D])
        xnT = k.sb("xnT", [P, DC, S])
        kva = k.sb("kva", [P, TI, P])
        sq = k.sb("sq", [P, TI, MLA_R])
        ss = k.sb("ss", [P, TI])
        kr1 = k.sb("kr1", [P, TI, MLA_DR])
        kr2 = k.sb("kr2", [P, TI, MLA_DR])
        kc = k.sb("kc", [P, TI, 2, P])
        kT = k.sb("kT", [P, 2, S])
        wst = k.sb("wst", [P, DC, 2, P])
        qT = k.sb("qT", [P, 2, S])
        swp = k.sb("swp", [P, S])
        rot1 = k.sb("rot1", [P, S])
        rot2 = k.sb("rot2", [P, S])
        nmax = k.sb("nmax", [P, 2, TI])
        lsum = k.sb("lsum", [P, 2, TI])
        rl = k.sb("rl", [P, 2, TI])
        probs = k.sb("probs", [P, 2, CAUSAL_COLS])
        probsT = k.sb("probsT", [P, 2, CAUSAL_COLS])
        on = k.sb("on", [P, TI, MLA_PAIRS, 2, MLA_R])
        onT = k.sb("onT", [P, 2, MLA_PAIRS, P])
        sc = k.ps("sc", [P, 2, 3 * 512])
        po = k.ps("po", [P, 2, TI, MLA_R])
        pq = k.ps("pq", [P, 512])

        def bank(n):
            return sc[:, n // 3, (n % 3) * 512:(n % 3 + 1) * 512]

        names = ("var_ready", "rstd_ready", "xn_ready", "xt_ready", "xnT_ready", "kva_ready", "kvar_ready",
                 "krstd_ready", "kc_ready", "kt_ready", "kT_ready", "staged", "qb_ready", "rope_in", "rope_done",
                 "qa_ready", "qa_copied", "s_ready", "max_ready", "e_ready", "t_ready", "pt_a", "pt_b", "o_ready",
                 "o_done", "ot_ready", "onT_a", "onT_b", "y_ready", "x_done")
        s = {n: k.sem("mla_" + n) for n in names}

        with nc.Block() as block:
            @block.vector
            def _(dve):
                dve.nop().then_inc(s["x_done"], 1)
                dve.nop().then_inc(s["x_done"], 1)
                dve.nop().then_inc(s["o_done"], 1)
                dve.wait_ge(g["x_loaded"], 16)
                dve.wait_ge(g["consts_loaded"], 16 * len(g["first_loads"]))
                with dve.Fori(0, B) as b:
                    dve.wait_ge(s["xt_ready"], b + 1)
                    layer_norm_stats(dve, stats, mv, ve[:, 0, :], [x[:, b * TI + i, :] for i in range(TI)],
                                     LN_EPS, s["var_ready"])
                    dve.wait_ge(s["rstd_ready"], b + 1)
                    for i in range(TI):
                        last = dve.tensor_scalar(xn[:, i, :], x[:, b * TI + i, :], mv[:, i, 0:1], rstd[:, 0, i:i + 1],
                                                 ALU.subtract, ALU.mult)
                    last.then_inc(s["xn_ready"], 1)

                    def rope_queries(n):
                        dve.wait_ge(s["qb_ready"], n + 1)
                        dve.wait_ge(s["rope_done"], n + 1)
                        dve.tensor_tensor(rot1[:, :], pq[:, :], ropeT[:, 0, :], ALU.mult)
                        dve.stream_shuffle(swp[:, :], pq[:, :],
                                           [(r + 16) % 32 for r in range(32)]).then_inc(s["rope_in"], 1)

                    dve.wait_ge(s["kva_ready"], b + 1)
                    dve.tensor_copy(kva[:, :, :], bank(2).rearrange("p (i c) -> p i c", i=TI))
                    dve.drain()
                    kv, pe4 = kva[:, :, 0:MLA_R], kva[:, :, MLA_R:].rearrange("p i (q e r) -> p i q e r", q=2, e=2)
                    dve.tensor_tensor(sq[:, :, :], kv, kv, ALU.mult)
                    dve.tensor_tensor(kr1[:, :, :], kva[:, :, MLA_R:], ropeN[:, :, 0, :], ALU.mult)
                    for e in range(2):
                        for q in range(2):
                            lo = q * 32 + e * 16
                            dve.tensor_tensor(kr2[:, :, lo:lo + 16], pe4[:, :, q, 1 - e, :],
                                              ropeN[:, :, 1, lo:lo + 16], ALU.mult)
                    dve.drain()
                    dve.tensor_reduce(ss[:, :], sq[:, :, :], AX.X, ALU.add)
                    dve.tensor_tensor(kc[:, :, 0, MLA_R:], kr1[:, :, :], kr2[:, :, :], ALU.add)
                    dve.tensor_tensor(kc[:, :, 1, 0:MLA_R], kr1[:, :, :], kr2[:, :, :], ALU.add)
                    dve.drain()
                    dve.tensor_scalar(ve[:, 1, :], ss[:, :], 1.0 / MLA_R, MLA_EPS, ALU.mult,
                                      ALU.add).then_inc(s["kvar_ready"], 1)
                    dve.wait_ge(s["krstd_ready"], b + 1)
                    dve.tensor_tensor(sq[:, :, :], kv, rstd[:, 1, :].unsqueeze(2).to_broadcast([P, TI, MLA_R]),
                                      ALU.mult)
                    dve.drain()
                    kvw_b = kvw[:, :].unsqueeze(1).to_broadcast([P, TI, MLA_R])
                    dve.tensor_tensor(kc[:, :, 0, 0:MLA_R], sq[:, :, :], kvw_b, ALU.mult)
                    dve.tensor_tensor(kc[:, :, 1, MLA_R:], sq[:, :, :], kvw_b, ALU.mult).then_inc(s["kc_ready"], 1)
                    rope_queries(b * MLA_PAIRS)

                    def pair(p, last_pair):
                        n = b * MLA_PAIRS + p
                        for j in range(2):
                            for qi in CAUSAL_ORDER:
                                if qi != 0:
                                    dve.wait_ge(s["s_ready"], 6 * n + 3 * j + CAUSAL_BANK[qi] + 1)
                                at = CAUSAL_COL[qi]
                                red = dve.tensor_reduce(nmax[:, j, qi:qi + 1], sc[:, j, at:at + (qi + 1) * P],
                                                        AX.X, ALU.max, negate=True)
                                if qi != 2:
                                    red.then_inc(s["max_ready"], 1)
                        if not last_pair:
                            rope_queries(n + 1)
                        for j in range(2):
                            dve.wait_ge(s["t_ready"], 6 * n + 3 * j + 2)
                            dve.tensor_copy(probsT[:, j, S:2 * S], sc[:, j, S:2 * S])
                            dve.wait_ge(s["t_ready"], 6 * n + 3 * j + 3)
                            dve.tensor_copy(probsT[:, j, 2 * S:CAUSAL_COLS],
                                            sc[:, j, 2 * S:CAUSAL_COLS]).then_inc(s["pt_b"], 1)
                        dve.reciprocal(rl[:, :, :], lsum[:, :, :])
                        dve.drain()
                        dve.wait_ge(s["o_ready"], n + 1)
                        dve.tensor_tensor(on[:, :, p, :, :].rearrange("p q j r -> p j q r"), po[:, :, :, :],
                                          rl[:, :, :].unsqueeze(3).to_broadcast([P, 2, TI, MLA_R]),
                                          ALU.mult).then_inc(s["o_done"], 1)

                    with dve.Fori(0, MLA_PAIRS - 1) as p:
                        pair(p, False)
                    pair(MLA_PAIRS - 1, True)
                    for i in range(TI):
                        dve.wait_ge(s["ot_ready"], 2 * (b * TI + i) + 2)
                        dve.tensor_copy(onT[:, i % 2, 4:8, :].rearrange("p a t -> p (a t)"),
                                        bank(2 * (i % 2) + 1)).then_inc(s["onT_b"], 1)
                        if i:
                            dve.wait_ge(s["y_ready"], b * TI + i)
                            xi = x[:, b * TI + i - 1, :]
                            dve.tensor_tensor(xi, bank(4 + (i - 1) % 2)[:, 0:D], xi, ALU.add).then_inc(s["x_done"], 1)
                    dve.wait_ge(s["y_ready"], b * TI + TI)
                    xi = x[:, b * TI + TI - 1, :]
                    dve.tensor_tensor(xi, bank(4 + (TI - 1) % 2)[:, 0:D], xi, ALU.add).then_inc(s["x_done"], 1)

            @block.gpsimd
            def _(pool):
                pool.nop().then_inc(s["rope_done"], 1)
                with pool.Fori(0, B) as b:
                    def stage(p):
                        pool.tensor_copy(wst[:, :, :, :], wap[:, :, p, :, :]).then_inc(s["staged"], 1)

                    pool.wait_ge(s["qa_ready"], b * MLA_PAIRS + 1)
                    for which, (var, std) in enumerate((("var_ready", "rstd_ready"), ("kvar_ready", "krstd_ready"))):
                        pool.wait_ge(s[var], b + 1)
                        pool.tensor_tensor(rstd[:, which, :], ve[:, which, :], g["neg_half"][:, 0:TI],
                                           ALU.pow).then_inc(s[std], 1)
                        if which == 0:
                            stage(0)

                    def rope(n):
                        pool.wait_ge(s["rope_in"], n + 1)
                        pool.tensor_tensor(rot2[:, :], swp[:, :], ropeT[:, 1, :], ALU.mult)
                        pool.drain()
                        pool.tensor_tensor(qT[0:64, 1, :], rot1[0:64, :], rot2[0:64, :], ALU.add)
                        pool.drain()
                        pool.tensor_tensor(qT[64:P, 0, :], rot1[64:P, :], rot2[64:P, :],
                                           ALU.add).then_inc(s["rope_done"], 1)
                        pool.drain()

                    with pool.Fori(0, MLA_PAIRS - 1) as p:
                        rope(b * MLA_PAIRS + p)
                        pool.wait_ge(s["qa_ready"], b * MLA_PAIRS + p + 2)
                        stage(p + 1)
                    rope(b * MLA_PAIRS + MLA_PAIRS - 1)

            @block.scalar
            def _(act):
                act.nop().then_inc(s["qa_copied"], 1)
                with act.Fori(0, B) as b:
                    def copy_latent_queries(n):
                        act.wait_ge(s["qa_ready"], n + 2)
                        act.activation(qT[0:64, 0, :], pq[0:64, :], ACT.Copy)
                        act.activation(qT[64:P, 1, :], pq[64:P, :], ACT.Copy).then_inc(s["qa_copied"], 1)

                    act.wait_ge(s["xt_ready"], b + 2)
                    for c in range(DC):
                        last = act.activation(xnT[:, c, :], bank(c), ACT.Copy)
                    last.then_inc(s["xnT_ready"], 1)
                    copy_latent_queries(b * MLA_PAIRS)
                    act.wait_ge(s["kt_ready"], b + 1)
                    for v in range(2):
                        last = act.activation(kT[:, v, :], bank(v), ACT.Copy)
                    last.then_inc(s["kT_ready"], 1)

                    def pair(p, last_pair):
                        n = b * MLA_PAIRS + p
                        for j in range(2):
                            for qi in CAUSAL_ORDER:
                                if qi != 0:
                                    act.wait_ge(s["max_ready"], 6 * n + 3 * j + CAUSAL_BANK[qi] + 1)
                                at = CAUSAL_COL[qi]
                                ex = act.activation(probs[:, j, at:at + (qi + 1) * P], sc[:, j, at:at + (qi + 1) * P],
                                                    ACT.Exp, bias=nmax[:, j, qi:qi + 1],
                                                    accum_out=lsum[:, j, qi:qi + 1])
                                if qi != 2:
                                    ex.then_inc(s["e_ready"], 1)
                        for j in range(2):
                            act.wait_ge(s["t_ready"], 6 * n + 3 * j + 1)
                            act.activation(probsT[:, j, 0:S], sc[:, j, 0:S], ACT.Copy).then_inc(s["pt_a"], 1)
                            if j == 0 and not last_pair:
                                copy_latent_queries(n + 1)

                    with act.Fori(0, MLA_PAIRS - 1) as p:
                        pair(p, False)
                    pair(MLA_PAIRS - 1, True)
                    for i in range(TI):
                        act.wait_ge(s["ot_ready"], 2 * (b * TI + i) + 1)
                        act.activation(onT[:, i % 2, 0:4, :].rearrange("p a t -> p (a t)"), bank(2 * (i % 2)),
                                       ACT.Copy).then_inc(s["onT_a"], 1)

            @block.tensor
            def _(pe):
                pe.nop().then_inc(s["xt_ready"], 1)
                pe.nop().then_inc(s["qa_ready"], 1)
                with pe.Fori(0, B) as b:
                    pe.wait_ge(s["xn_ready"], b + 1)
                    for c in range(DC):
                        for i in range(TI):
                            last = pe.transpose(bank(c)[:, i * P:(i + 1) * P], xn[:, i, c * P:(c + 1) * P],
                                                ident[:, :])
                    last.then_inc(s["xt_ready"], 1)
                    pe.wait_ge(s["xnT_ready"], b + 1)
                    for i in range(TI):
                        for c in range(DC):
                            last = pe.matmul(bank(2)[:, i * P:(i + 1) * P], xnT[:, c, i * P:(i + 1) * P],
                                             wkva[:, c, :], start=(c == 0), stop=(c == DC - 1))
                    last.then_inc(s["kva_ready"], 1)

                    def project(n, kind):
                        if kind == 1:
                            pe.wait_ge(s["staged"], n + 1)
                            pe.wait_ge(s["qa_copied"], n + 1)
                        else:
                            pe.wait_ge(s["rope_in"], n + 1)
                        for c in range(DC):
                            last = pe.matmul(pq[:, :], wst[:, c, kind, :], xnT[:, c, :], start=(c == 0),
                                             stop=(c == DC - 1))
                        last.then_inc(s["qb_ready" if kind == 1 else "qa_ready"], 1)

                    project(b * MLA_PAIRS, 1)
                    pe.wait_ge(s["kc_ready"], b + 1)
                    for v in range(2):
                        for i in range(TI):
                            last = pe.transpose(bank(v)[:, i * P:(i + 1) * P], kc[:, i, v, :], ident[:, :])
                    last.then_inc(s["kt_ready"], 1)
                    project(b * MLA_PAIRS, 0)

                    def pair(p, last_pair):
                        n = b * MLA_PAIRS + p
                        pe.wait_ge(s["kT_ready"], b + 1)
                        pe.wait_ge(s["rope_done"], n + 2)
                        pe.wait_ge(s["qa_copied"], n + 2)
                        for j in range(2):
                            for qi in CAUSAL_ORDER:
                                at = CAUSAL_COL[qi]
                                pe.matmul(sc[:, j, at:at + (qi + 1) * P], qT[:, j, qi * P:(qi + 1) * P],
                                          kT[:, j, 0:(qi + 1) * P], start=True, stop=False)
                                last = pe.matmul(sc[:, j, at + qi * P:at + (qi + 1) * P], ident_b[:, :], mask_b[:, :],
                                                 start=False, stop=True)
                                if qi != 2:
                                    last.then_inc(s["s_ready"], 1)
                        for j in range(2):
                            if not last_pair:
                                project(n + 1, 1 - j)
                            for qi in CAUSAL_ORDER:
                                if qi != 0:
                                    pe.wait_ge(s["e_ready"], 6 * n + 3 * j + CAUSAL_BANK[qi] + 1)
                                for kj in range(qi + 1):
                                    at = CAUSAL_COL[qi] + kj * P
                                    last = pe.transpose(sc[:, j, at:at + P], probs[:, j, at:at + P], ident[:, :])
                                if qi != 2:
                                    last.then_inc(s["t_ready"], 1)
                        pe.wait_ge(s["o_done"], n + 1)
                        for j in range(2):
                            pe.wait_ge(s["pt_a"], 2 * n + j + 1)
                            pe.wait_ge(s["pt_b"], 2 * n + j + 1)
                            for qi in range(TI):
                                for kj in range(qi + 1):
                                    at = CAUSAL_COL[qi] + kj * P
                                    last = pe.matmul(po[:, j, qi, :], probsT[:, j, at:at + P], kc[:, kj, 0, 0:MLA_R],
                                                     start=(kj == 0), stop=(kj == qi))
                        last.then_inc(s["o_ready"], 1)

                    with pe.Fori(0, MLA_PAIRS - 1) as p:
                        pair(p, False)
                    pair(MLA_PAIRS - 1, True)

                    def turn(i):
                        for hp in range(MLA_PAIRS):
                            last = pe.transpose(bank(2 * (i % 2) + hp // 4)[:, (hp % 4) * P:(hp % 4 + 1) * P],
                                                on[:, i, hp, :, :].rearrange("p j r -> p (j r)"), ident[:, :])
                            if hp % 4 == 3:
                                last.then_inc(s["ot_ready"], 1)

                    pe.wait_ge(s["o_done"], b * MLA_PAIRS + MLA_PAIRS + 1)
                    turn(0)
                    for i in range(TI):
                        if i + 1 < TI:
                            turn(i + 1)
                        pe.wait_ge(s["onT_a"], b * TI + i + 1)
                        pe.wait_ge(s["onT_b"], b * TI + i + 1)
                        pe.wait_ge(s["x_done"], b * TI + i + 1)
                        for hp in range(MLA_PAIRS):
                            last = pe.matmul(bank(4 + i % 2)[:, 0:D], onT[:, i % 2, hp, :], wvo[:, hp, :],
                                             start=(hp == 0), stop=(hp == MLA_PAIRS - 1))
                        last.then_inc(s["y_ready"], 1)
        k.clear_sems()


class Normed:

    def __init__(self, k, tag):
        self.stats = k.sb(tag + "_stats", [P, TI, 6])
        self.mv = k.sb(tag + "_mv", [P, TI, 2])
        self.ve = k.sb(tag + "_ve", [P, TI])
        self.rstd = k.sb(tag + "_rstd", [P, TI])
        self.xn = k.sb(tag + "_xn", [P, TI, D])
        self.xnT = k.sb(tag + "_xnT", [P, DC, S])
        self.var_ready = k.sem(tag + "_var_ready")
        self.rstd_ready = k.sem(tag + "_rstd_ready")
        self.xn_ready = k.sem(tag + "_xn_ready")
        self.xt_ready = k.sem(tag + "_xt_ready")
        self.xnT_ready = k.sem(tag + "_xnT_ready")

    def scale_rows(self, dve, x, b):
        for i in range(TI):
            last = dve.tensor_scalar(self.xn[:, i, :], x[:, b * TI + i, :], self.mv[:, i, 0:1], self.rstd[:, i:i + 1],
                                     ALU.subtract, ALU.mult)
        return last

    def norm(self, dve, x, b):
        dve.wait_ge(self.xt_ready, b + 1)
        layer_norm_stats(dve, self.stats, self.mv, self.ve[:, :], [x[:, b * TI + i, :] for i in range(TI)],
                         LN_EPS, self.var_ready)
        dve.wait_ge(self.rstd_ready, b + 1)
        self.scale_rows(dve, x, b).then_inc(self.xn_ready, 1)

    def invert(self, pool, g, b):
        pool.wait_ge(self.var_ready, b + 1)
        pool.tensor_tensor(self.rstd[:, :], self.ve[:, :], g["neg_half"][:, 0:TI], ALU.pow).then_inc(self.rstd_ready, 1)

    def turn(self, pe, g, banks, b):
        pe.wait_ge(self.xn_ready, b + 1)
        for c in range(DC):
            for i in range(TI):
                last = pe.transpose(banks[c][:, i * P:(i + 1) * P], self.xn[:, i, c * P:(c + 1) * P], g["ident"][:, :])
        last.then_inc(self.xt_ready, 1)

    def first_free(self, pe):
        pe.nop().then_inc(self.xt_ready, 1)

    def copy(self, act, banks, b):
        act.wait_ge(self.xt_ready, b + 2)
        for c in range(DC):
            last = act.activation(self.xnT[:, c, :], banks[c], ACT.Copy)
        last.then_inc(self.xnT_ready, 1)


FFN_EPS = 1e-7


def ternary_ffn(nc, g, tag, loads):
    with ExitStack() as ctx:
        k = Kit(nc, ctx)
        x = g["x"]
        ln = Normed(k, tag)
        y = k.sb(tag + "_y", [P, NT, D])
        sq = k.sb(tag + "_sq", [P, TI, D])
        n2 = k.sb(tag + "_n2", [P, NT])
        norm = k.sb(tag + "_norm", [P, NT])
        t = k.sb(tag + "_t", [P, 8, NT])
        ps = k.ps(tag + "_ps", [P, 8, 512])
        y_ready = k.sem(tag + "_y_ready")
        y_scaled = k.sem(tag + "_y_scaled")
        norms_ready = k.sem(tag + "_norms_ready")
        root_ready = k.sem(tag + "_root_ready")
        clipped = k.sem(tag + "_clipped")
        tanh_ready = k.sem(tag + "_tanh_ready")
        banks = [ps[:, 0, :], ps[:, 1, :]]

        with nc.Block() as block:
            @block.sync
            def _(sp):
                for dst, src, done in loads:
                    sp.dma_start(dst, src).then_inc(done, 16)

            @block.vector
            def _(dve):
                dve.nop().then_inc(y_scaled, 1)
                with dve.Fori(0, B) as b:
                    ln.norm(dve, x, b)
                    dve.wait_ge(y_ready, b + 1)
                    for h in range(2):
                        dve.tensor_tensor(y[:, b * TI + 2 * h, :], ps[:, 2 + h, 0:D], g["ffn_scale"][:, :], ALU.mult)
                        last = dve.tensor_tensor(y[:, b * TI + 2 * h + 1, :], ps[:, 2 + h, D:2 * D],
                                                 g["ffn_scale"][:, :], ALU.mult)
                    last.then_inc(y_scaled, 1)
                    dve.drain()
                    for i in range(TI):
                        dve.tensor_tensor(sq[:, i, :], y[:, b * TI + i, :], y[:, b * TI + i, :], ALU.mult)
                    dve.drain()
                    for i in range(TI):
                        last = dve.tensor_reduce(n2[:, bass.ds(b * TI + i, 1)], sq[:, i, :], AX.X, ALU.add)
                    last.then_inc(norms_ready, 1)
                    dve.drain()
                dve.wait_ge(root_ready, 1)
                dve.tensor_scalar(t[:, 0, :], norm[:, :], FFN_EPS, None, ALU.max).then_inc(clipped, 1)
                dve.drain()
                dve.tensor_scalar(t[:, 2, :], t[:, 0, :], FFN_EPS, None, ALU.add)
                dve.drain()
                dve.reciprocal(t[:, 3, :], t[:, 2, :])
                dve.drain()
                dve.wait_ge(tanh_ready, 1)
                dve.tensor_tensor(t[:, 4, :], t[:, 1, :], t[:, 3, :], ALU.mult)
                dve.drain()
                dve.tensor_tensor(t[:, 5, :], norm[:, :], t[:, 4, :], ALU.mult)
                dve.drain()
                dve.tensor_scalar(t[:, 6, :], t[:, 5, :], FFN_EPS, None, ALU.max)
                dve.drain()
                dve.reciprocal(t[:, 7, :], t[:, 6, :])
                dve.drain()
                dve.tensor_scalar(t[:, 0, :], t[:, 7, :], 0.99, 1.0, ALU.mult, ALU.min)
                dve.drain()
                dve.tensor_tensor(t[:, 2, :], t[:, 0, :], t[:, 4, :], ALU.mult)
                dve.drain()
                with dve.Fori(0, NT) as i:
                    dve.scalar_tensor_tensor(x[:, i, :], y[:, i, :], t[:, 2, bass.ds(i, 1)], x[:, i, :],
                                             ALU.mult, ALU.add)

            @block.gpsimd
            def _(pool):
                with pool.Fori(0, B) as b:
                    ln.invert(pool, g, b)
                pool.wait_ge(norms_ready, B)
                pool.tensor_tensor(norm[:, :], n2[:, :], g["pos_half"][:, 0:NT], ALU.pow).then_inc(root_ready, 1)

            @block.scalar
            def _(act):
                with act.Fori(0, B) as b:
                    ln.copy(act, banks, b)
                act.wait_ge(clipped, 1)
                act.activation(t[:, 1, :], t[:, 0, :], ACT.Tanh).then_inc(tanh_ready, 1)

            @block.tensor
            def _(pe):
                ln.first_free(pe)
                with pe.Fori(0, B) as b:
                    ln.turn(pe, g, banks, b)
                    pe.wait_ge(ln.xnT_ready, b + 1)
                    pe.wait_ge(y_scaled, b + 1)
                    for i in range(TI):
                        for c in range(DC):
                            last = pe.matmul(ps[:, 2 + i // 2, (i % 2) * D:(i % 2 + 1) * D],
                                             ln.xnT[:, c, i * P:(i + 1) * P], g["ffn_w"][:, c, :],
                                             start=(c == 0), stop=(c == DC - 1))
                    last.then_inc(y_ready, 1)
        k.clear_sems()


COS_H, COS_D = 16, 128
COS_SCALE = 16.0


def cosine_attention(nc, g):
    with ExitStack() as ctx:
        k = Kit(nc, ctx)
        x, ident, wq, wkv, wout, gout = (g[n] for n in ("x", "ident", "cos_wq", "cos_wkv", "cos_wout", "cos_gout"))
        ln = Normed(k, "cos")
        var2 = k.sb("cos_var2", [P, 2, TI])
        rstd2 = k.sb("cos_rstd2", [P, TI])
        kk = k.sb("cos_kk", [P, TI, P])
        ksum = k.sb("cos_ksum", [P, 3, TI])
        kn = k.sb("cos_kn", [P, TI, P])
        kT = k.sb("cos_kT", [P, S])
        vx = k.sb("cos_vx", [P, TI, COS_D + 1])
        qsq = k.sb("cos_qsq", [P, 2, 4, P])
        qss = k.sb("cos_qss", [P, 2, 4])
        qse = k.sb("cos_qse", [P, 2, 4])
        qrs = k.sb("cos_qrs", [P, 2, 4])
        qn = k.sb("cos_qn", [P, 2, 4, P])
        qT = k.sb("cos_qT", [P, COS_H, S])
        probs = k.sb("cos_probs", [P, 2, TI, S])
        rl = k.sb("cos_rl", [P, 2, TI])
        on = qT[:, :, :].rearrange("p h (i c) -> p i h c", i=TI)
        onT = k.sb("cos_onT", [P, 2, COS_H, P])
        yn = k.sb("cos_yn", [P, TI, D])
        ps = k.ps("cos_ps", [P, 8, 512])
        po = ps[:, 4:8, 0:2 * (COS_D + 1)].rearrange("p (j a) (q c) -> p j a q c", j=2, c=COS_D + 1)
        names = ("scaled_w", "var2_ready", "rstd2_ready", "kv_ready", "k_var", "k_rstd", "kn_ready", "kt_ready",
                 "kT_ready", "q_ready", "q_sq", "q_var", "q_rstd", "qn_ready", "qt_ready", "qT_ready", "s_ready",
                 "e_ready", "o_ready", "o_done", "ot_ready", "onT_a", "onT_d", "y_ready", "y_var", "y_rstd",
                 "batch_done")
        s = {n: k.sem("cos_" + n) for n in names}
        banks = [ps[:, 0, :], ps[:, 1, :]]
        QU = COS_H // 4 * TI

        with nc.Block() as block:
            @block.vector
            def _(dve):
                for _ in range(2):
                    dve.nop().then_inc(s["o_done"], 1)
                    dve.nop().then_inc(s["qn_ready"], 1)
                for c in range(DC):
                    dve.tensor_scalar(wq[:, c, :], wq[:, c, :], g["cos_g"][:, c:c + 1], None, ALU.mult)
                    dve.tensor_scalar(wkv[:, c, :], wkv[:, c, :], g["cos_g"][:, c:c + 1], None, ALU.mult)
                dve.memset(vx[:, :, COS_D:], 1.0).then_inc(s["scaled_w"], 1)
                with dve.Fori(0, B) as b:
                    dve.wait_ge(ln.xt_ready, b + 1)
                    layer_norm_stats(dve, ln.stats, ln.mv, ln.ve[:, :], [x[:, b * TI + i, :] for i in range(TI)],
                                     LN_EPS, ln.var_ready)
                    dve.wait_ge(ln.rstd_ready, b + 1)
                    dve.tensor_tensor(var2[:, 0, :], ln.mv[:, :, 1], ln.rstd[:, :], ALU.mult)
                    dve.drain()
                    dve.tensor_tensor(var2[:, 0, :], var2[:, 0, :], ln.rstd[:, :], ALU.mult)
                    dve.drain()
                    dve.tensor_scalar(var2[:, 1, :], var2[:, 0, :], LN_EPS, None, ALU.add).then_inc(s["var2_ready"], 1)
                    dve.wait_ge(s["rstd2_ready"], b + 1)
                    dve.tensor_tensor(ln.rstd[:, :], rstd2[:, :], ln.rstd[:, :], ALU.mult)
                    dve.drain()
                    ln.scale_rows(dve, x, b).then_inc(ln.xn_ready, 1)
                    dve.wait_ge(s["kv_ready"], b + 1)
                    kv = ps[:, 2:4, :].rearrange("p a (i c) -> p a i c", i=2)
                    dve.tensor_copy(kk.rearrange("p (a i) c -> p a i c", a=2), kv[:, :, :, 0:P])
                    dve.tensor_copy(vx[:, :, 0:COS_D].rearrange("p (a i) c -> p a i c", a=2), kv[:, :, :, P:])
                    dve.drain()
                    dve.tensor_tensor(kn[:, :, :], kk[:, :, :], kk[:, :, :], ALU.mult)
                    dve.drain()
                    dve.tensor_reduce(ksum[:, 0, :], kn[:, :, :], AX.X, ALU.add)
                    dve.drain()
                    dve.tensor_scalar(ksum[:, 1, :], ksum[:, 0, :], 1e-12, None, ALU.add).then_inc(s["k_var"], 1)
                    dve.wait_ge(s["k_rstd"], b + 1)
                    for i in range(TI):
                        last = dve.tensor_scalar(kn[:, i, :], kk[:, i, :], ksum[:, 2, i:i + 1], COS_SCALE,
                                                 ALU.mult, ALU.mult)
                    last.then_inc(s["kn_ready"], 1)

                    with dve.Fori(0, COS_H // 4) as hq:
                        def sums(i):
                            u = b * QU + hq * TI + i
                            dve.wait_ge(s["q_sq"], u + 1)
                            dve.tensor_reduce(qss[:, i % 2, :], qsq[:, i % 2, :, :], AX.X, ALU.add)
                            dve.drain()
                            dve.tensor_scalar(qse[:, i % 2, :], qss[:, i % 2, :], 1e-12 / 256, None,
                                              ALU.add).then_inc(s["q_var"], 1)

                        def scale(i):
                            u = b * QU + hq * TI + i
                            dve.wait_ge(s["q_rstd"], u + 1)
                            dve.wait_ge(s["qt_ready"], u + 1)
                            dve.tensor_tensor(qn[:, i % 2, :, :],
                                              ps[:, i % 2, :].rearrange("p (h c) -> p h c", h=4),
                                              qrs[:, i % 2, :].unsqueeze(2).to_broadcast([P, 4, P]),
                                              ALU.mult).then_inc(s["qn_ready"], 1)

                        sums(0)
                        for i in range(TI):
                            if i + 1 < TI:
                                sums(i + 1)
                            scale(i)

                    with dve.Fori(0, COS_H // 2) as p:
                        for j in range(2):
                            h = b * COS_H + 2 * p + j
                            dve.wait_ge(s["o_ready"], h + 1)
                            dve.reciprocal(rl[:, j, :].rearrange("p (a q) -> p a q", a=2), po[:, j, :, :, COS_D])
                            dve.drain()
                            dve.tensor_tensor(on[:, :, 2 * p + j, :].rearrange("p (a q) c -> p a q c", a=2),
                                              po[:, j, :, :, 0:COS_D],
                                              rl[:, j, :].rearrange("p (a q) -> p a q", a=2).unsqueeze(3)
                                              .to_broadcast([P, 2, 2, COS_D]), ALU.mult).then_inc(s["o_done"], 1)
                    for i in range(TI):
                        for n in (1, 3):
                            dve.wait_ge(s["ot_ready"], 4 * (b * TI + i) + n + 1)
                            last = dve.tensor_copy(onT[:, i % 2, 4 * n:4 * n + 4, :].rearrange("p a t -> p (a t)"),
                                                   ps[:, n, :])
                        last.then_inc(s["onT_d"], 1)
                    dve.wait_ge(s["y_ready"], b + 1)
                    layer_norm_stats(dve, ln.stats, ln.mv, ln.ve[:, :], [ps[:, 4 + i, 0:D] for i in range(TI)],
                                     LN_EPS, s["y_var"])
                    dve.wait_ge(s["y_rstd"], b + 1)
                    for i in range(TI):
                        dve.tensor_scalar(yn[:, i, :], ps[:, 4 + i, 0:D], ln.mv[:, i, 0:1], ln.rstd[:, i:i + 1],
                                          ALU.subtract, ALU.mult)
                    dve.drain()
                    for i in range(TI):
                        dve.tensor_tensor(yn[:, i, :], yn[:, i, :], gout[:, :], ALU.mult)
                    dve.drain()
                    for i in range(TI):
                        xi = x[:, b * TI + i, :]
                        last = dve.tensor_tensor(xi, yn[:, i, :], xi, ALU.add)
                    last.then_inc(s["batch_done"], 1)

            @block.gpsimd
            def _(pool):
                nh = g["neg_half"]
                with pool.Fori(0, B) as b:
                    ln.invert(pool, g, b)
                    pool.wait_ge(s["var2_ready"], b + 1)
                    pool.tensor_tensor(rstd2[:, :], var2[:, 1, :], nh[:, 0:TI], ALU.pow).then_inc(s["rstd2_ready"], 1)
                    pool.wait_ge(s["k_var"], b + 1)
                    pool.tensor_tensor(ksum[:, 2, :], ksum[:, 1, :], nh[:, 0:TI], ALU.pow).then_inc(s["k_rstd"], 1)
                    with pool.Fori(0, COS_H // 4) as hq:
                        for i in range(TI):
                            pool.wait_ge(s["q_var"], b * QU + hq * TI + i + 1)
                            pool.tensor_tensor(qrs[:, i % 2, :], qse[:, i % 2, :], nh[:, 0:4],
                                               ALU.pow).then_inc(s["q_rstd"], 1)
                    pool.wait_ge(s["y_var"], b + 1)
                    pool.tensor_tensor(ln.rstd[:, :], ln.ve[:, :], nh[:, 0:TI], ALU.pow).then_inc(s["y_rstd"], 1)

            @block.scalar
            def _(act):
                for _ in range(TI):
                    act.nop().then_inc(s["e_ready"], 1)
                for _ in range(2):
                    act.nop().then_inc(s["qT_ready"], 1)
                with act.Fori(0, B) as b:
                    ln.copy(act, banks, b)
                    act.wait_ge(s["kt_ready"], b + 1)
                    act.activation(kT[:, :], ps[:, 4, :], ACT.Copy).then_inc(s["kT_ready"], 1)
                    with act.Fori(0, COS_H // 4) as hq:
                        def square(i):
                            u = b * QU + hq * TI + i
                            act.wait_ge(s["q_ready"], u + 1)
                            act.wait_ge(s["qn_ready"], u + 1)
                            act.activation(qsq[:, i % 2, :, :].rearrange("p h c -> p (h c)"), ps[:, i % 2, :],
                                           ACT.Square).then_inc(s["q_sq"], 1)

                        square(0)
                        for i in range(TI):
                            if i + 1 < TI:
                                square(i + 1)
                            act.wait_ge(s["qt_ready"], b * QU + hq * TI + i + 3)
                            act.activation(qT[:, bass.ts(hq, 4), i * P:(i + 1) * P],
                                           ps[:, 2 + i % 2, :].rearrange("p (h t) -> p h t", h=4),
                                           ACT.Copy).then_inc(s["qT_ready"], 1)
                    with act.Fori(0, COS_H // 2) as p:
                        for j in range(2):
                            for kj in range(TI):
                                act.wait_ge(s["s_ready"], TI * (b * COS_H + 2 * p + j) + kj + 1)
                                act.activation(probs[:, j, kj, :], ps[:, kj, :], ACT.Exp).then_inc(s["e_ready"], 1)
                    for i in range(TI):
                        for n in (0, 2):
                            act.wait_ge(s["ot_ready"], 4 * (b * TI + i) + n + 1)
                            last = act.activation(onT[:, i % 2, 4 * n:4 * n + 4, :].rearrange("p a t -> p (a t)"),
                                                  ps[:, n, :], ACT.Copy)
                        last.then_inc(s["onT_a"], 1)

            @block.tensor
            def _(pe):
                ln.first_free(pe)
                for _ in range(2):
                    pe.nop().then_inc(s["qt_ready"], 1)
                pe.wait_ge(s["scaled_w"], 1)
                with pe.Fori(0, B) as b:
                    ln.turn(pe, g, banks, b)
                    pe.wait_ge(ln.xnT_ready, b + 1)
                    for i in range(TI):
                        for c in range(DC):
                            last = pe.matmul(ps[:, 2 + i // 2, (i % 2) * D:(i % 2 + 1) * D],
                                             ln.xnT[:, c, i * P:(i + 1) * P], wkv[:, c, :],
                                             start=(c == 0), stop=(c == DC - 1))
                    last.then_inc(s["kv_ready"], 1)
                    pe.wait_ge(s["kn_ready"], b + 1)
                    for i in range(TI):
                        last = pe.transpose(ps[:, 4, i * P:(i + 1) * P], kn[:, i, :], ident[:, :])
                    last.then_inc(s["kt_ready"], 1)

                    with pe.Fori(0, COS_H // 4) as hq:
                        def project(i):
                            u = b * QU + hq * TI + i
                            pe.wait_ge(s["qn_ready"], u + 1)
                            for c in range(DC):
                                last = pe.matmul(ps[:, i % 2, :], ln.xnT[:, c, i * P:(i + 1) * P],
                                                 wq[:, c, bass.ts(hq, 512)], start=(c == 0), stop=(c == DC - 1))
                            last.then_inc(s["q_ready"], 1)

                        project(0)
                        for i in range(TI):
                            if i + 1 < TI:
                                project(i + 1)
                            u = b * QU + hq * TI + i
                            pe.wait_ge(s["qn_ready"], u + 3)
                            pe.wait_ge(s["qT_ready"], u + 1)
                            for h in range(4):
                                last = pe.transpose(ps[:, 2 + i % 2, h * P:(h + 1) * P], qn[:, i % 2, h, :],
                                                    ident[:, :])
                            last.then_inc(s["qt_ready"], 1)

                    with pe.Fori(0, COS_H // 2) as p:
                        pe.wait_ge(s["kT_ready"], b + 1)
                        pe.wait_ge(s["qT_ready"], b * QU + QU + 2)
                        for j in range(2):
                            h = b * COS_H + 2 * p + j
                            for kj in range(TI):
                                pe.wait_ge(s["e_ready"], TI * h + kj + 1)
                                pe.matmul(ps[:, kj, :], kT[:, kj * P:(kj + 1) * P], qT[:, 2 * p + j, :],
                                          start=True, stop=True).then_inc(s["s_ready"], 1)
                        for j in range(2):
                            h = b * COS_H + 2 * p + j
                            pe.wait_ge(s["e_ready"], TI * h + 2 * TI)
                            pe.wait_ge(s["o_done"], h + 1)
                            for qi in range(TI):
                                for kj in range(TI):
                                    last = pe.matmul(po[:, j, qi // 2, qi % 2, :],
                                                     probs[:, j, kj, qi * P:(qi + 1) * P], vx[:, kj, :],
                                                     start=(kj == 0), stop=(kj == TI - 1))
                            last.then_inc(s["o_ready"], 1)

                    def turn(i):
                        for h in range(COS_H):
                            last = pe.transpose(ps[:, h // 4, (h % 4) * P:(h % 4 + 1) * P], on[:, i, h, :],
                                                ident[:, :])
                            if h % 4 == 3:
                                last.then_inc(s["ot_ready"], 1)

                    pe.wait_ge(s["o_done"], b * COS_H + COS_H + 2)
                    turn(0)
                    for i in range(TI):
                        pe.wait_ge(s["onT_a"], b * TI + i + 1)
                        pe.wait_ge(s["onT_d"], b * TI + i + 1)
                        if i + 1 < TI:
                            turn(i + 1)
                        for h in range(COS_H):
                            last = pe.matmul(ps[:, 4 + i, 0:D], onT[:, i % 2, h, :], wout[:, h, :],
                                             start=(h == 0), stop=(h == COS_H - 1))
                    last.then_inc(s["y_ready"], 1)
        k.clear_sems()


GLA_H, GLA_DK, GLA_DV, GLA_LR = 16, 8, 16, 16
GLA_SCALE = float(GLA_DK ** -0.5)
GLA_EPS = 1e-5
GATE_NORMALIZER = 16.0
GLA_HALF = GLA_DV // 2


def gated_linear_attention(nc, g):
    with ExitStack() as ctx:
        k = Kit(nc, ctx)
        x = g["x"]
        ln = Normed(k, "gla")
        qT = k.sb("gla_qT", [P, B, S])
        kT = k.sb("gla_kT", [P, B, S])
        q_now = k.sb("gla_q_now", [P, S])
        vT = k.sb("gla_vT", [P, B, 2, S])
        z1 = k.sb("gla_z1", [GLA_LR, S])
        za = k.sb("gla_za", [P, S])
        z = k.sb("gla_z", [P, B, S])
        decay = k.sb("gla_decay", [P, B, S])
        gate = k.sb("gla_gate", [P, B, 2, S])
        ge = k.sb("gla_ge", [P, B, 2, S])
        room = [g["cos_wout"][:, 4 * n:4 * n + 4, :].rearrange("p h d -> p (h d)") for n in range(4)]
        kv = room[0].rearrange("p (n s) -> p n s", n=2)
        st = room[1].rearrange("p (n s) -> p n s", n=2)
        qs = k.sb("gla_qs", [P, 2, S])
        eps = k.sb("gla_eps", [P, 1])
        orstd = k.sb("gla_orstd", [P, S])
        o = room[2].rearrange("p (n s) -> p n s", n=2)
        osq = room[3].rearrange("p (n s) -> p n s", n=2)
        ogT = ln.xnT
        ps = k.ps("gla_ps", [P, 8, 512])
        names = ("q_ready", "k_ready", "v_ready", "z1_ready", "z1_copied", "z_ready", "g_ready", "g_read", "q_now_ready",
                 "kT_ready", "vT_ready", "za_ready", "ez_ready", "ln_ready", "lg_ready", "decay_ready", "ge_ready",
                 "sigmoid_ready", "vrep_ready", "kv_ready", "st_ready", "qs_ready", "qs_read",
                 "half_copied", "ms_ready", "orstd_ready", "ogT_ready", "y_ready")
        s = {n: k.sem("gla_" + n) for n in names}
        banks = [ps[:, 0, :], ps[:, 1, :]]
        gps = ps[:, 6:8, :]

        with nc.Block() as block:
            @block.vector
            def _(dve):
                dve.memset(eps[:, :], GLA_EPS)
                for _ in range(2):
                    dve.nop().then_inc(s["kv_ready"], 1)
                ln.norm(dve, x, 0)

                def gates(b, more):
                    dve.wait_ge(s["z_ready"], b + 1)
                    dve.tensor_scalar(z[:, bass.ds(b, 1), :].rearrange("p o s -> p (o s)"), ps[:, 5, :],
                                      g["gla_bgk2"][:, 0:1], None, ALU.add)
                    dve.drain()
                    zb = z[:, bass.ds(b, 1), :].rearrange("p o s -> p (o s)")
                    dve.scalar_tensor_tensor(za[:, :], zb, -1.0, zb, ALU.mult, ALU.min).then_inc(s["za_ready"], 1)
                    if more:
                        ln.norm(dve, x, b + 1)
                    dve.wait_ge(s["ge_ready"], b + 1)
                    for half in range(2):
                        last = dve.tensor_scalar(gate[:, bass.ds(b, 1), half, :], gps[:, half, :].unsqueeze(1),
                                                 g["gla_normw"][:, half:half + 1], None, ALU.mult)
                    last.then_inc(s["g_read"], 1)

                with dve.Fori(0, B - 1) as b:
                    gates(b, True)
                gates(B - 1, False)
                dve.wait_ge(s["ln_ready"], 1)
                dve.scalar_tensor_tensor(z[:, :, :], z[:, :, :], 0.0, decay[:, :, :], ALU.min,
                                         ALU.subtract).then_inc(s["lg_ready"], 1)

                def scan_half(b, half, between={}):
                    for j in range(GLA_HALF):
                        if j in between:
                            between[j](b - 1)
                        n = b * GLA_DV + half * GLA_HALF + j
                        if j == 0:
                            dve.wait_ge(s["decay_ready"], b + 1)
                        dve.wait_ge(s["vrep_ready"], n + 1)
                        dve.tensor_tensor(kv[:, j % 2, :], ps[:, j % 2, :],
                                          kT[:, bass.ds(b, 1), :].rearrange("p o s -> p (o s)"),
                                          ALU.mult).then_inc(s["kv_ready"], 1)
                        dve.drain()
                        dve.wait_ge(s["qs_ready"], n + 1)
                        dve.tensor_tensor_scan(st[:, j % 2, :],
                                               decay[:, bass.ds(b, 1), :].rearrange("p o s -> p (o s)"),
                                               kv[:, j % 2, :], 0.0, ALU.mult, ALU.add).then_inc(s["st_ready"], 1)

                def finish_gate(b):
                    dve.wait_ge(s["sigmoid_ready"], b + 1)
                    gb = gate[:, bass.ds(b, 1), :, :]
                    dve.tensor_tensor(gb, gb, ge[:, bass.ds(b, 1), :, :], ALU.mult)

                def gate_outputs(b):
                    dve.wait_ge(s["orstd_ready"], b + 1)
                    dve.tensor_tensor(o, o, orstd[:, :].unsqueeze(1).to_broadcast([P, 2, S]), ALU.mult)
                    dve.drain()
                    dve.tensor_tensor(ogT[:, :, :], o, gate[:, bass.ds(b, 1), :, :].rearrange("p o n s -> p (o n) s"),
                                      ALU.mult).then_inc(s["ogT_ready"], 1)

                def add_outputs(b):
                    dve.wait_ge(s["y_ready"], b + 1)
                    for i in range(TI):
                        xi = x[:, b * TI + i, :]
                        dve.tensor_tensor(xi, ps[:, 6 + i // 2, (i % 2) * D:(i % 2 + 1) * D], xi, ALU.add)

                scan_half(0, 0)
                with dve.Fori(0, B - 1) as b:
                    scan_half(b, 1)
                    scan_half(b + 1, 0, {2: finish_gate, 6: gate_outputs})
                    add_outputs(b)
                scan_half(B - 1, 1)
                finish_gate(B - 1)
                gate_outputs(B - 1)
                add_outputs(B - 1)

            @block.gpsimd
            def _(pool):
                for _ in range(2):
                    pool.nop().then_inc(s["qs_ready"], 1)
                with pool.Fori(0, B) as b:
                    ln.invert(pool, g, b)
                with pool.Fori(0, B) as b:
                    with pool.Fori(0, 2) as half:
                        for j in range(GLA_HALF):
                            if j == 0:
                                pool.wait_ge(s["q_now_ready"], b + 1)
                            n = b * GLA_DV + half * GLA_HALF + j
                            pool.wait_ge(s["qs_read"], n + 1)
                            pool.wait_ge(s["st_ready"], n + 1)
                            pool.tensor_tensor(qs[:, j % 2, :], st[:, j % 2, :],
                                               q_now[:, :], ALU.mult).then_inc(s["qs_ready"], 1)

            @block.scalar
            def _(act):
                act.nop().then_inc(s["half_copied"], 2)
                with act.Fori(0, B) as b:
                    ln.copy(act, banks, b)
                    act.wait_ge(s["z1_ready"], b + 1)
                    act.activation(z1[:, :], ps[0:GLA_LR, 4, :], ACT.Copy).then_inc(s["z1_copied"], 1)
                    act.wait_ge(s["q_ready"], b + 1)
                    act.activation(qT[:, bass.ds(b, 1), :], ps[:, 2, :].unsqueeze(1), ACT.Copy,
                                   scale=GLA_SCALE)
                    act.wait_ge(s["za_ready"], b + 1)
                    act.activation(decay[:, bass.ds(b, 1), :], za[:, :].unsqueeze(1), ACT.Exp).then_inc(s["ez_ready"], 1)
                    act.wait_ge(s["g_ready"], b + 1)
                    act.activation(ge[:, bass.ds(b, 1), :, :].rearrange("p o n s -> p (o n) s"), gps, ACT.Exp, scale=-1.0)\
                        .then_inc(s["ge_ready"], 1)
                    act.wait_ge(s["k_ready"], b + 1)
                    act.activation(kT[:, bass.ds(b, 1), :], ps[:, 0, :].unsqueeze(1), ACT.Copy)\
                        .then_inc(s["kT_ready"], 1)
                    act.wait_ge(s["v_ready"], b + 1)
                    act.activation(vT[:, bass.ds(b, 1), :, :].rearrange("p o c s -> p (o c) s"), ps[:, 3:5, :],
                                   ACT.Copy).then_inc(s["vT_ready"], 1)
                act.drain()
                act.activation(q_now[:, :], qT[:, 0, :], ACT.Copy).then_inc(s["q_now_ready"], 1)
                act.activation(decay[:, :, :], decay[:, :, :], ACT.Ln, bias=1.0).then_inc(s["ln_ready"], 1)
                act.activation(ge[:, :, :, :], ge[:, :, :, :], ACT.Ln, bias=1.0)
                act.drain()
                for b in range(B):
                    if b == 0:
                        act.wait_ge(s["lg_ready"], 1)
                    act.activation(decay[:, b, :], z[:, b, :], ACT.Exp,
                                   scale=1.0 / GATE_NORMALIZER).then_inc(s["decay_ready"], 1)
                for b in range(B):
                    act.activation(ge[:, b, :, :], ge[:, b, :, :], ACT.Exp, scale=-1.0).then_inc(s["sigmoid_ready"], 1)

                def collect(m, half):
                    act.wait_ge(s["qs_read"], GLA_HALF * m + GLA_HALF + 2)
                    act.activation(o[:, half, :], ps[:, 2 + half, :], ACT.Copy)
                    act.activation(osq[:, half, :], ps[:, 2 + half, :], ACT.Square).then_inc(s["half_copied"], 1)

                def invert(b):
                    act.wait_ge(s["ms_ready"], b + 1)
                    act.activation(orstd[:, :], ps[:, 4, :], ACT.Ln, bias=eps[:, 0:1], scale=1.0 / GLA_DV)
                    act.drain()
                    act.activation(orstd[:, :], orstd[:, :], ACT.Exp, scale=-0.5).then_inc(s["orstd_ready"], 1)

                collect(0, 0)
                with act.Fori(0, B - 1) as b:
                    act.wait_ge(s["qs_ready"], (b + 1) * GLA_DV + 2)
                    act.activation(q_now[:, :], qT[:, bass.ds(b + 1, 1), :].rearrange("p o s -> p (o s)"),
                                   ACT.Copy).then_inc(s["q_now_ready"], 1)
                    collect(2 * b + 1, 1)
                    invert(b)
                    collect(2 * b + 2, 0)
                collect(2 * B - 1, 1)
                invert(B - 1)

            @block.tensor
            def _(pe):
                ln.first_free(pe)
                for _ in range(2):
                    pe.nop().then_inc(s["qs_read"], 1)
                for n in ("kT_ready", "vT_ready", "g_read"):
                    pe.nop().then_inc(s[n], 1)
                with pe.Fori(0, B) as b:
                    def turned(bank, weights, rows, ready):
                        for c in range(DC):
                            last = pe.matmul(ps[0:rows, bank, :], weights[:, c, :], ln.xnT[:, c, :],
                                             start=(c == 0), stop=(c == DC - 1))
                        if ready:
                            last.then_inc(s[ready], 1)

                    pe.wait_ge(s["kT_ready"], b + 1)
                    ln.turn(pe, g, banks, b)
                    pe.wait_ge(s["vT_ready"], b + 1)
                    pe.wait_ge(ln.xnT_ready, b + 1)
                    turned(4, g["gla_wgk1"], GLA_LR, "z1_ready")
                    turned(2, g["gla_wq"], P, "q_ready")
                    pe.wait_ge(s["z1_copied"], b + 1)
                    pe.matmul(ps[:, 5, :], g["gla_wgk2"][:, :], z1[:, :], start=True,
                              stop=True).then_inc(s["z_ready"], 1)
                    pe.wait_ge(s["g_read"], b + 1)
                    turned(6, g["gla_wg"][:, :, 0:P], P, None)
                    turned(7, g["gla_wg"][:, :, P:D], P, "g_ready")
                    turned(0, g["gla_wk"], P, "k_ready")
                    turned(3, g["gla_wv"][:, :, 0:P], P, None)
                    turned(4, g["gla_wv"][:, :, P:D], P, "v_ready")

                def repeat(b, half, j):
                    pe.wait_ge(s["kv_ready"], b * GLA_DV + half * GLA_HALF + j + 1)
                    pe.matmul(ps[:, j % 2, :], g["gla_sel"][:, j, :], vT[:, bass.ds(b, 1), half, :].rearrange("p o s -> p (o s)"),
                              start=True, stop=True).then_inc(s["vrep_ready"], 1)

                def sums(b, half, j):
                    if j == 0:
                        pe.wait_ge(s["half_copied"], 2 * b + half + 1)
                    pe.wait_ge(s["qs_ready"], b * GLA_DV + half * GLA_HALF + j + 3)
                    at = (GLA_HALF - 1 - j) * GLA_H
                    pe.matmul(ps[:, 2 + half, :], g["gla_hsum"][:, at:at + P], qs[:, j % 2, :], start=(j == 0),
                              stop=(j == GLA_HALF - 1)).then_inc(s["qs_read"], 1)

                def scan_half(b, half, first=False, last=False, after=None):
                    for j in range(GLA_HALF):
                        if j + 1 < GLA_HALF:
                            repeat(b, half, j + 1)
                        elif half == 0:
                            repeat(b, 1, 0)
                        elif not last:
                            repeat(b + 1, 0, 0)
                        if j > 0:
                            sums(b, half, j - 1)
                        elif half == 1:
                            sums(b, 0, GLA_HALF - 1)
                        elif not first:
                            sums(b - 1, 1, GLA_HALF - 1)
                        if after and j == 4:
                            after()

                def mean_squares(b):
                    pe.wait_ge(s["half_copied"], 2 * b + 4)
                    for half in range(2):
                        last = pe.matmul(ps[:, 4, :], g["gla_same"][:, :], osq[:, half, :], start=(half == 0),
                                         stop=(half == 1))
                    last.then_inc(s["ms_ready"], 1)

                def project_outputs(b):
                    pe.wait_ge(s["ogT_ready"], b + 1)
                    for i in range(TI):
                        for c in range(DC):
                            last = pe.matmul(ps[:, 6 + i // 2, (i % 2) * D:(i % 2 + 1) * D],
                                             ogT[:, c, i * P:(i + 1) * P], g["gla_wo"][:, c, :],
                                             start=(c == 0), stop=(c == DC - 1))
                    last.then_inc(s["y_ready"], 1)

                for n in ("kT_ready", "vT_ready"):
                    pe.wait_ge(s[n], B + 1)
                repeat(0, 0, 0)
                scan_half(0, 0, first=True)
                with pe.Fori(0, B - 1) as b:
                    scan_half(b, 1)
                    scan_half(b + 1, 0, after=lambda: mean_squares(b))
                    project_outputs(b)
                scan_half(B - 1, 1, last=True)
                sums(B - 1, 1, GLA_HALF - 1)
                mean_squares(B - 1)
                project_outputs(B - 1)
        k.clear_sems()


WS_S, WS_K, WS_NB, WS_H = 16, 4, 2, 4
WS_HD = D // WS_H
WS_ROWS = B * WS_S
WS_EPS = 1e-6
SENTINEL = -3e38


def workspace_ffn(nc, g, tag):
    with ExitStack() as ctx:
        k = Kit(nc, ctx)
        x, ident = g["x"], g["ident"]

        def sb(name, shape):
            return k.sb(f"{tag}_{name}", shape)

        stats, mv = sb("stats", [P, TI, 6]), sb("mv", [P, TI, 2])
        ve, rstd = sb("ve", [P, TI]), sb("rstd", [P, TI])
        cw = sb("cw", [P, DC, WS_S])
        xf = sb("xf", [P, NT, D])
        xs = sb("xs", [P, TI, D])
        xsT = sb("xsT", [P, DC, S])
        xfT = sb("xfT", [P, DC, NT * P])
        junk = sb("junk", [P, D])
        msq, mse = sb("msq", [P, TI]), sb("mse", [P, TI])
        lg = sb("lg", [P, TI, WS_ROWS])
        lt = sb("lt", [WS_ROWS, S + 8])
        top, match = sb("top", [WS_ROWS, 8]), sb("match", [WS_ROWS, 8])
        ntop = sb("ntop", [WS_ROWS, 1])
        etop = sb("etop", [WS_ROWS, WS_K])
        zsum, rz = sb("zsum", [WS_ROWS, 1]), sb("rz", [WS_ROWS, 1])
        elt = sb("elt", [WS_ROWS, S])
        marked = sb("marked", [WS_ROWS, S + 8])
        chosen = sb("chosen", [WS_ROWS, S])
        selw = sb("selw", [WS_ROWS, S])
        selT = sb("selT", [P, TI, WS_ROWS])
        xselT = sb("xselT", [P, DC, WS_ROWS])
        ws = sb("ws", [WS_ROWS, D])
        wsum, wsq = sb("wsum", [WS_ROWS, D]), sb("wsq", [WS_ROWS, D])
        wss, wse, wsr = sb("wss", [WS_ROWS, 1]), sb("wse", [WS_ROWS, 1]), sb("wsr", [WS_ROWS, 1])
        wsT = sb("wsT", [P, DC, WS_ROWS])
        kbd = sb("kbd", [P, 2, B, 2, WS_S])
        vbd = sb("vbd", [P, 2, B, 2, WS_S])
        m = sb("m", [P, DC, 2, B, 2 * WS_S])
        cb = sb("cb", [1, 2, B, 2 * WS_S])
        nb_w = sb("nb", [65, B, D])
        ones = sb("ones", [1, P])
        amax, al = sb("amax", [P, TI * WS_H]), sb("al", [P, TI * WS_H])
        ar = sb("ar", [P, TI * WS_H])
        ash = sb("ash", [P, TI * WS_H, WS_S])
        att = sb("att", [P, TI, WS_H * WS_S])
        attT = sb("attT", [65, S])
        ps = k.ps(tag + "_ps", [P, 8, 512])
        names = ("setup", "bias_loaded", "var_ready", "rstd_ready", "xs_ready", "xt_ready", "xsT_ready", "xfT_ready",
                 "msq_ready", "r_ready", "lg_ready", "lg_done", "lt_ready", "ntop_ready", "exp_ready", "selw_ready",
                 "st_ready", "selT_ready", "xsel_ready", "xselT_ready", "written", "wss_ready", "wsr_ready",
                 "ws_ready", "wt_ready", "wsT_ready", "kv_ready", "bd_ready", "m_ready", "cb_ready", "nb_ready",
                 "fold_v", "fold_a", "xr_ready", "a_ready", "ash_ready", "ae_ready", "att_ready", "at_ready",
                 "attT_ready", "xb_ready", "xsum_ready", "m2_ready", "r2_ready")
        s = {n: k.sem(f"{tag}_{n}") for n in names}
        bias = g["ws_in_b"]

        with nc.Block() as block:
            @block.sync
            def _(sp):
                sp.dma_start(nb_w[64:65, :, :], g["ws_out_b"][:, :, :]).then_inc(s["bias_loaded"], 16)
                sp.dma_start(ws[:, :], g["ws_start"][:, :]).then_inc(s["bias_loaded"], 16)

            @block.vector
            def _(dve):
                dve.memset(kbd[:, :, :, :, :], 0.0)
                dve.memset(vbd[:, :, :, :, :], 0.0)
                dve.memset(ones[:, :], 1.0)
                dve.memset(attT[64:65, :], 1.0)
                dve.memset(lt[:, S:], SENTINEL)
                dve.memset(match[:, WS_K:], SENTINEL)
                for c in range(DC):
                    last = dve.tensor_scalar(cw[:, c, :], g["ws_cw"][:, c, :], g["ws_pre"][:, c:c + 1], None, ALU.mult)
                last.then_inc(s["setup"], 1)
                with dve.Fori(0, B) as b:
                    layer_norm_stats(dve, stats, mv, ve[:, :], [x[:, b * TI + i, :] for i in range(TI)], LN_EPS,
                                     s["var_ready"])
                    dve.wait_ge(s["rstd_ready"], b + 1)
                    for i in range(TI):
                        dve.tensor_scalar(xf[:, b * TI + i, :], x[:, b * TI + i, :], mv[:, i, 0:1], rstd[:, i:i + 1],
                                          ALU.subtract, ALU.mult)
                dve.nop().then_inc(s["xt_ready"], 1)
                dve.drain()
                with dve.Fori(0, WS_NB) as r:
                    with dve.Fori(0, B) as b:
                        n = r * B + b
                        dve.wait_ge(s["xt_ready"], n + 1)
                        dve.wait_ge(s["msq_ready"], n + 1)
                        dve.tensor_copy(xs[:, :, :], xf[:, bass.ts(b, TI), :]).then_inc(s["xs_ready"], 1)
                        dve.wait_ge(s["lg_ready"], n + 1)
                        dve.wait_ge(s["r_ready"], n + 1)
                        dve.tensor_tensor(lg[:, :, bass.ts(b, WS_S)],
                                          ps[:, 2, 0:TI * WS_S].rearrange("p (i s) -> p i s", i=TI),
                                          rstd[:, :].unsqueeze(2).to_broadcast([P, TI, WS_S]),
                                          ALU.mult).then_inc(s["lg_done"], 1)
                    dve.wait_ge(s["lt_ready"], r + 1)
                    dve.tensor_scalar(lt[:, 0:S], ps[0:WS_ROWS, 3, :], g["ws_cb"][:, 0:1], None, ALU.add)
                    dve.drain()
                    dve.max(top[:, :], lt[:, 0:S])
                    dve.drain()
                    dve.tensor_scalar(ntop[:, :], top[:, 0:1], -1.0, None, ALU.mult).then_inc(s["ntop_ready"], 1)
                    dve.tensor_copy(match[:, 0:WS_K], top[:, 0:WS_K])
                    dve.drain()
                    dve.match_replace(marked[:, :], match[:, :], lt[:, :], -SENTINEL)
                    dve.drain()
                    dve.tensor_tensor(chosen[:, :], marked[:, 0:S], lt[:, 0:S], ALU.not_equal)
                    dve.wait_ge(s["exp_ready"], r + 1)
                    dve.tensor_reduce(zsum[:, :], etop[:, :], AX.X, ALU.add)
                    dve.drain()
                    dve.reciprocal(rz[:, :], zsum[:, :])
                    dve.drain()
                    dve.scalar_tensor_tensor(selw[:, :], elt[:, :], rz[:, 0:1], chosen[:, :], ALU.mult,
                                             ALU.mult).then_inc(s["selw_ready"], 1)
                    dve.wait_ge(s["st_ready"], r + 1)
                    dve.tensor_copy(selT[:, :, :], ps[:, 4, 0:TI * WS_ROWS].rearrange("p (i s) -> p i s", i=TI))\
                       .then_inc(s["selT_ready"], 1)
                    dve.wait_ge(s["xsel_ready"], r + 1)
                    dve.tensor_copy(xselT[:, :, :], ps[:, 5, 0:DC * WS_ROWS].rearrange("p (c s) -> p c s", c=DC))\
                       .then_inc(s["xselT_ready"], 1)
                    dve.wait_ge(s["written"], r + 1)
                    dve.wait_ge(s["bias_loaded"], 32)
                    dve.tensor_tensor(wsum[:, :], ps[0:WS_ROWS, 6, 0:D], ws[:, :], ALU.add)
                    dve.drain()
                    dve.tensor_tensor(wsq[:, :], wsum[:, :], wsum[:, :], ALU.mult)
                    dve.drain()
                    dve.tensor_reduce(wss[:, :], wsq[:, :], AX.X, ALU.add)
                    dve.drain()
                    dve.tensor_scalar(wse[:, :], wss[:, :], 1.0 / D, WS_EPS, ALU.mult, ALU.add)\
                       .then_inc(s["wss_ready"], 1)
                    dve.wait_ge(s["wsr_ready"], r + 1)
                    dve.scalar_tensor_tensor(ws[:, :], wsum[:, :], wsr[:, 0:1], g["ws_post"][0:WS_ROWS, :],
                                             ALU.mult, ALU.mult).then_inc(s["ws_ready"], 1)
                    dve.wait_ge(s["wt_ready"], r + 1)
                    dve.tensor_copy(wsT[:, :, :], ps[:, 7, 0:DC * WS_ROWS].rearrange("p (c s) -> p c s", c=DC))\
                       .then_inc(s["wsT_ready"], 1)
                    dve.wait_ge(s["kv_ready"], r + 1)
                    for oc in range(2):
                        for hh in range(2):
                            rows = slice(64 * hh, 64 * hh + 64)
                            kv = ps[rows, 3, :].rearrange("p (v o b s) -> p v o b s", v=4, o=2, b=B)
                            dve.tensor_scalar(kbd[rows, oc, :, hh, :], kv[:, 0, oc], bias[rows, 2 + oc:3 + oc],
                                              float(WS_HD ** -0.5), ALU.add, ALU.mult)
                            last = dve.tensor_scalar(vbd[rows, oc, :, hh, :], kv[:, 1, oc], bias[rows, 4 + oc:5 + oc],
                                                     None, ALU.add)
                    last.then_inc(s["bd_ready"], 1)
                    dve.wait_ge(s["m_ready"], r + 1)
                    dve.tensor_copy(m[:, :, :, :, :].rearrange("p c o b s -> p (c o b s)"), ps[:, 4, :])
                    dve.wait_ge(s["cb_ready"], r + 1)
                    dve.tensor_copy(cb[:, :, :, :].rearrange("p o b s -> p (o b s)"), ps[0:1, 5, 0:2 * P])\
                       .then_inc(s["fold_v"], 1)
                    with dve.Fori(0, B) as b:
                        n = r * B + b
                        dve.wait_ge(s["a_ready"], n + 2)
                        sc = ps[:, 0, 0:TI * WS_H * WS_S].rearrange("p (a s) -> p a s", s=WS_S)
                        dve.tensor_reduce(amax[:, :], sc, AX.X, ALU.max)
                        dve.drain()
                        dve.tensor_tensor(ash[:, :, :], sc, amax[:, :].unsqueeze(2).to_broadcast(
                            [P, TI * WS_H, WS_S]), ALU.subtract).then_inc(s["ash_ready"], 1)
                        dve.wait_ge(s["ae_ready"], n + 1)
                        dve.tensor_reduce(al[:, :], ash[:, :, :], AX.X, ALU.add)
                        dve.drain()
                        dve.reciprocal(ar[:, :], al[:, :])
                        dve.drain()
                        dve.tensor_tensor(att[:, :, :].rearrange("p i (h s) -> p (i h) s", s=WS_S), ash[:, :, :],
                                          ar[:, :].unsqueeze(2).to_broadcast([P, TI * WS_H, WS_S]),
                                          ALU.mult).then_inc(s["att_ready"], 1)
                        dve.wait_ge(s["xb_ready"], n + 1)
                        for i in range(TI):
                            xi = xf[:, b * TI + i, :]
                            last = dve.tensor_tensor(xs[:, i, :], ps[:, 2 + i // 2, (i % 2) * D:(i % 2 + 1) * D],
                                                     xi, ALU.add)
                        last.then_inc(s["xsum_ready"], 1)
                        dve.wait_ge(s["r2_ready"], n + 1)
                        for i in range(TI):
                            dve.scalar_tensor_tensor(xf[:, b * TI + i, :], xs[:, i, :], rstd[:, i:i + 1],
                                                     g["ws_post"][:, :], ALU.mult, ALU.mult)
                        dve.drain()
                with dve.Fori(0, NT) as i:
                    dve.tensor_tensor(x[:, i, :], xf[:, i, :], x[:, i, :], ALU.add)

            @block.gpsimd
            def _(pool):
                nh = g["neg_half"]
                with pool.Fori(0, B) as b:
                    pool.wait_ge(s["var_ready"], b + 1)
                    pool.tensor_tensor(rstd[:, :], ve[:, :], nh[:, 0:TI], ALU.pow).then_inc(s["rstd_ready"], 1)
                pool.nop().then_inc(s["xfT_ready"], 1)

                def row_scales():
                    pool.tensor_tensor(mse[:, :], msq[:, :], g["ws_eps"][:, 0:TI], ALU.add)
                    pool.drain()
                    return pool.tensor_tensor(rstd[:, :], mse[:, :], nh[:, 0:TI], ALU.pow)

                with pool.Fori(0, WS_NB) as r:
                    with pool.Fori(0, B) as b:
                        n = r * B + b
                        pool.wait_ge(s["msq_ready"], n + 2)
                        row_scales().then_inc(s["r_ready"], 1)
                        pool.drain()
                        pool.wait_ge(s["xsT_ready"], n + 1)
                        pool.tensor_copy(xfT[:, :, bass.ts(b, S)], xsT[:, :, :]).then_inc(s["xfT_ready"], 1)
                        pool.drain()
                    pool.wait_ge(s["wss_ready"], r + 1)
                    pool.tensor_tensor(wsr[:, :], wse[:, :], nh[0:WS_ROWS, 0:1], ALU.pow).then_inc(s["wsr_ready"], 1)
                    with pool.Fori(0, B) as b:
                        n = r * B + b
                        pool.wait_ge(s["m2_ready"], n + 1)
                        row_scales().then_inc(s["r2_ready"], 1)
                        pool.drain()

            @block.scalar
            def _(act):
                act.nop().then_inc(s["msq_ready"], 1)

                def mean_squares():
                    for i in range(TI):
                        last = act.activation(junk[:, :], xs[:, i, :], ACT.Square, scale=float(D ** -0.5),
                                              accum_out=msq[:, i:i + 1])
                        if i + 1 < TI:
                            act.drain()
                    return last

                with act.Fori(0, WS_NB) as r:
                    with act.Fori(0, B) as b:
                        n = r * B + b
                        act.wait_ge(s["xs_ready"], n + 1)
                        mean_squares().then_inc(s["msq_ready"], 1)
                        act.wait_ge(s["xt_ready"], n + 2)
                        act.wait_ge(s["xfT_ready"], n + 1)
                        for c in range(DC):
                            last = act.activation(xsT[:, c, :], ps[:, c, :], ACT.Copy)
                        last.then_inc(s["xsT_ready"], 1)
                    act.wait_ge(s["ntop_ready"], r + 1)
                    act.activation(etop[:, :], top[:, 0:WS_K], ACT.Exp, bias=ntop[:, 0:1])
                    act.activation(elt[:, :], lt[:, 0:S], ACT.Exp, bias=ntop[:, 0:1]).then_inc(s["exp_ready"], 1)
                    act.wait_ge(s["nb_ready"], r + 1)
                    act.activation(nb_w[0:64, :, :].rearrange("p (a b) d -> p a (b d)", a=2), ps[0:64, 6:8, :],
                                   ACT.Copy).then_inc(s["fold_a"], 1)
                    with act.Fori(0, B) as b:
                        n = r * B + b
                        act.wait_ge(s["xfT_ready"], r * B + B + 1)
                        act.wait_ge(s["a_ready"], n + 1)
                        act.activation(xsT[:, :, :], xfT[:, :, bass.ts(b, S)], ACT.Copy).then_inc(s["xr_ready"], 1)
                        act.wait_ge(s["ash_ready"], n + 1)
                        act.activation(ash[:, :, :], ash[:, :, :], ACT.Exp).then_inc(s["ae_ready"], 1)
                        act.wait_ge(s["at_ready"], n + 1)
                        act.activation(attT[0:64, :], ps[0:64, 1, :], ACT.Copy).then_inc(s["attT_ready"], 1)
                        act.wait_ge(s["xsum_ready"], n + 1)
                        mean_squares().then_inc(s["m2_ready"], 1)

            @block.tensor
            def _(pe):
                def turn_small(out, tile, rows):
                    return pe.matmul(out, tile, ident[0:rows, 0:rows], start=True, stop=True)

                pe.nop().then_inc(s["a_ready"], 1)
                pe.wait_ge(s["setup"], 1)
                with pe.Fori(0, WS_NB) as r:
                    with pe.Fori(0, B) as b:
                        n = r * B + b
                        pe.wait_ge(s["xs_ready"], n + 1)
                        for c in range(DC):
                            for i in range(TI):
                                last = pe.transpose(ps[:, c, i * P:(i + 1) * P], xs[:, i, c * P:(c + 1) * P],
                                                    ident[:, :])
                        last.then_inc(s["xt_ready"], 1)
                        pe.wait_ge(s["xsT_ready"], n + 1)
                        for i in range(TI):
                            for c in range(DC):
                                last = pe.matmul(ps[:, 2, i * WS_S:(i + 1) * WS_S], xsT[:, c, i * P:(i + 1) * P],
                                                 cw[:, c, :], start=(c == 0), stop=(c == DC - 1))
                        last.then_inc(s["lg_ready"], 1)
                    pe.wait_ge(s["lg_done"], r * B + B)
                    for i in range(TI):
                        last = turn_small(ps[0:WS_ROWS, 3, i * P:(i + 1) * P], lg[:, i, :], P)
                    last.then_inc(s["lt_ready"], 1)
                    pe.wait_ge(s["selw_ready"], r + 1)
                    for i in range(TI):
                        last = turn_small(ps[:, 4, i * WS_ROWS:(i + 1) * WS_ROWS], selw[:, i * P:(i + 1) * P], WS_ROWS)
                    last.then_inc(s["st_ready"], 1)
                    pe.wait_ge(s["selT_ready"], r + 1)
                    for c in range(DC):
                        for b in range(B):
                            for i in range(TI):
                                at = c * WS_ROWS + b * WS_S
                                last = pe.matmul(ps[:, 5, at:at + WS_S], xf[:, b * TI + i, c * P:(c + 1) * P],
                                                 selT[:, i, b * WS_S:(b + 1) * WS_S],
                                                 start=(i == 0), stop=(i == TI - 1))
                    last.then_inc(s["xsel_ready"], 1)
                    pe.wait_ge(s["xselT_ready"], r + 1)
                    for c in range(DC):
                        pe.matmul(ps[0:WS_ROWS, 6, 0:D], xselT[:, c, :], g["ws_write"][:, c, :], start=(c == 0),
                                  stop=False)
                    pe.matmul(ps[0:WS_ROWS, 6, 0:D], ones[:, 0:WS_ROWS], g["ws_write_b"][:, :], start=False,
                              stop=True).then_inc(s["written"], 1)
                    pe.wait_ge(s["ws_ready"], r + 1)
                    for c in range(DC):
                        last = turn_small(ps[:, 7, c * WS_ROWS:(c + 1) * WS_ROWS], ws[:, c * P:(c + 1) * P], WS_ROWS)
                    last.then_inc(s["wt_ready"], 1)
                    pe.wait_ge(s["wsT_ready"], r + 1)
                    for v, name in enumerate(("ws_wk", "ws_wv")):
                        for oc in range(2):
                            at = v * 2 * WS_ROWS + oc * WS_ROWS
                            for c in range(DC):
                                last = pe.matmul(ps[:, 3, at:at + WS_ROWS], g[name][:, c, oc * P:(oc + 1) * P],
                                                 wsT[:, c, :], start=(c == 0), stop=(c == DC - 1))
                    last.then_inc(s["kv_ready"], 1)
                    pe.wait_ge(s["bd_ready"], r + 1)
                    for c in range(DC):
                        for oc in range(2):
                            at = (c * 2 + oc) * P
                            last = pe.matmul(ps[:, 4, at:at + P], g["ws_wq"][:, oc, c * P:(c + 1) * P],
                                             kbd[:, oc, :, :, :].rearrange("p b h s -> p (b h s)"),
                                             start=True, stop=True)
                    last.then_inc(s["m_ready"], 1)
                    for oc in range(2):
                        last = pe.matmul(ps[0:1, 5, oc * P:(oc + 1) * P], bias[:, oc:oc + 1],
                                         kbd[:, oc, :, :, :].rearrange("p b h s -> p (b h s)"),
                                         start=True, stop=True)
                    last.then_inc(s["cb_ready"], 1)
                    for b in range(B):
                        for oc in range(2):
                            last = pe.matmul(ps[32 * oc:32 * oc + 32, 6 + b // 2, (b % 2) * D:(b % 2 + 1) * D],
                                             vbd[:, oc, b, :, :].rearrange("p h s -> p (h s)"),
                                             g["ws_out"][:, oc, :], start=True, stop=True)
                    last.then_inc(s["nb_ready"], 1)
                    with pe.Fori(0, B) as b:
                        n = r * B + b
                        pe.wait_ge(s["fold_v"], r + 1)
                        pe.wait_ge(s["fold_a"], r + 1)
                        pe.wait_ge(s["xr_ready"], n + 1)
                        for i in range(TI):
                            out = ps[:, 0, i * 64:(i + 1) * 64].rearrange("p (o s) -> p o s", o=2)
                            for c in range(DC):
                                last = pe.matmul(out, xsT[:, c, i * P:(i + 1) * P], m[:, c, :, b, :],
                                                 start=(c == 0), stop=False)
                            last = pe.matmul(out, ones[:, :], cb[:, :, b, :], start=False, stop=True)
                        last.then_inc(s["a_ready"], 1)
                        pe.wait_ge(s["att_ready"], n + 1)
                        for i in range(TI):
                            last = turn_small(ps[0:64, 1, i * P:(i + 1) * P], att[:, i, :], P)
                        last.then_inc(s["at_ready"], 1)
                        pe.wait_ge(s["attT_ready"], n + 1)
                        for i in range(TI):
                            last = pe.matmul(ps[:, 2 + i // 2, (i % 2) * D:(i % 2 + 1) * D],
                                             attT[:, i * P:(i + 1) * P], nb_w[:, b, :], start=True, stop=True)
                        last.then_inc(s["xb_ready"], 1)
        k.clear_sems()


LORA_N, LORA_RANK = 4, 16
LORA_ROWS = LORA_N * LORA_RANK
LORA_H = 16
LORA_HD = D // LORA_H
LORA_SCALE = float(LORA_HD ** -0.5)
LORA_BLOCKS = P // LORA_HD
LORA_PART_1 = (slice(0, 3), slice(1, 6, 2))
LORA_PART_2 = (slice(3, 5), slice(2, 5, 2))
LORA_PART_3 = (5, 0)
LORA_BOTH_1, LORA_BOTH_2 = 1, 4


def lora_attention(nc, g):
    with ExitStack() as ctx:
        k = Kit(nc, ctx)
        x, ident, ident_b, mask_b, rope = (g[n] for n in ("x", "ident", "ident_b", "mask_b", "lora_rope"))
        ln = Normed(k, "lora")
        starts = k.sb("lora_startf", [LORA_ROWS, LORA_N])
        begun = k.sb("lora_begun", [LORA_ROWS, B, LORA_N])
        which = k.sb("lora_which", [LORA_ROWS, B])
        mine = k.sb("lora_mine", [LORA_ROWS, B])
        am = k.sb("lora_am", [LORA_ROWS, 4, D])
        w = k.sb("lora_w", [P, DC, 4, D])
        rot = k.sb("lora_rot", [P, 2, 2 * D])
        qk = k.sb("lora_qk", [P, TI, 2 * LORA_H, LORA_HD])
        rest = k.sb("lora_rest", [P, TI, 2 * LORA_H, LORA_HD])
        parts = k.sb("lora_parts", [P, TI, 2 * LORA_H, LORA_BLOCKS, LORA_HD], BF16)
        qkT = k.sb("lora_qkT", [P, 2, 2, S], BF16)
        v = k.sb("lora_v", [P, TI, D])
        nmax = k.sb("lora_nmax", [P, 2, TI])
        lsum = k.sb("lora_lsum", [P, LORA_H, TI])
        rl = k.sb("lora_rl", [P, 2, TI])
        probs = g["cos_wout"][:, :, :].rearrange("p h d -> p (h d)")[:, 0:2 * CAUSAL_COLS]\
            .rearrange("p (j c) -> p j c", j=2)
        probsT = k.sb("lora_probsT", [P, 2, CAUSAL_COLS])
        on = k.sb("lora_on", [P, TI, LORA_H, LORA_HD])
        onT = ln.xnT
        sc = k.ps("lora_sc", [P, 2, 3 * 512])
        po = k.ps("lora_po", [P, 512])
        tq = k.ps("lora_tq", [P, 2, S], BF16)
        out2 = po[:, 0:2 * TI * LORA_HD].rearrange("p (j q c) -> p j q c", j=2, q=TI)

        def bank(n):
            return sc[:, n // 3, (n % 3) * 512:(n % 3 + 1) * 512]

        names = ("am_ready", "fold_ready", "w_ready", "v_ready", "v_copied", "pj_ready", "pj_read", "part1_ready",
                 "rest_ready", "rest2_ready", "part2_ready", "part3_ready", "qk_rotated", "tq_ready", "tq_read",
                 "s_ready", "max_ready", "e_ready", "t_ready", "pt_a", "pt_b", "o_ready", "o_done", "ot_ready",
                 "onT_ready", "y_ready")
        s = {n: k.sem("lora_" + n) for n in names}
        PAIRS = LORA_H // 2

        with nc.Block() as block:
            @block.vector
            def _(dve):
                dve.nop().then_inc(s["o_done"], 1)
                dve.tensor_copy(starts[:, :], g["lora_starts"][:, :])
                dve.tensor_scalar(g["lora_wq"][:, :, :], g["lora_wq"][:, :, :], LORA_SCALE, None, ALU.mult)
                dve.memset(parts[:, :, :, 6:LORA_BLOCKS, :], 0.0)
                dve.drain()
                dve.tensor_tensor(begun[:, :, :], starts[:, :].unsqueeze(1).to_broadcast([LORA_ROWS, B, LORA_N]),
                                  g["lora_batch"][:, :].unsqueeze(2).to_broadcast([LORA_ROWS, B, LORA_N]), ALU.is_le)
                dve.drain()
                dve.tensor_reduce(which[:, :], begun[:, :, :], AX.X, ALU.add)
                dve.drain()
                dve.tensor_scalar(mine[:, :], which[:, :], -1.0, 0.0, ALU.add, ALU.max)
                dve.drain()
                dve.tensor_scalar(which[:, :], mine[:, :], float(LORA_N - 1), None, ALU.min)
                dve.drain()
                dve.tensor_scalar(mine[:, :], which[:, :], g["lora_row"][:, 0:1], None, ALU.is_equal)
                dve.drain()
                with dve.Fori(0, B) as b:
                    for n, name in enumerate("qkvo"):
                        last = dve.tensor_scalar(am[:, n, :], g["lora_a" + name][:, :], mine[:, bass.ds(b, 1)],
                                                 LORA_SCALE if name == "q" else 1.0, ALU.mult, ALU.mult)
                    last.then_inc(s["am_ready"], 1)
                    ln.norm(dve, x, b)
                    dve.wait_ge(s["fold_ready"], b + 1)
                    for n, name in enumerate("qkvo"):
                        last = dve.tensor_tensor(w[:, :, n, :], bank(n).rearrange("p (c d) -> p c d", c=DC),
                                                 g["lora_w" + name][:, :, :], ALU.add)
                    last.then_inc(s["w_ready"], 1)

                    for i in range(TI):
                        dve.wait_ge(s["pj_ready"], b * TI + i + 1)
                        values = bank(i).rearrange("p (n e f) -> p n e f", e=2, f=LORA_HD // 2)
                        cos = rope[:, i, 0, 0, :].unsqueeze(1).to_broadcast([P, 4 * LORA_H, LORA_HD // 2])
                        dve.tensor_tensor(rot[:, 0, :].rearrange("p (n f) -> p n f", f=LORA_HD // 2),
                                          bank(i).rearrange("p (n f) -> p n f", f=LORA_HD // 2), cos, ALU.mult)
                        for e in range(2):
                            sin = rope[:, i, 1, e, :].unsqueeze(1).to_broadcast([P, 2 * LORA_H, LORA_HD // 2])
                            last = dve.tensor_tensor(
                                rot[:, 1, :].rearrange("p (n e f) -> p n e f", e=2, f=LORA_HD // 2)[:, :, e, :],
                                values[:, :, 1 - e, :], sin, ALU.mult)
                        last.then_inc(s["pj_read"], 1)
                        dve.drain()
                        dve.tensor_tensor(qk[:, i, :, :].rearrange("p n c -> p (n c)"), rot[:, 0, :], rot[:, 1, :],
                                          ALU.add).then_inc(s["qk_rotated"], 1)
                        if i == 0:
                            dve.wait_ge(s["part1_ready"], b * TI + 1)
                            dve.tensor_tensor(rest[:, 0, :, :], qk[:, 0, :, :], parts[:, 0, :, LORA_BOTH_1, :],
                                              ALU.subtract).then_inc(s["rest_ready"], 1)
                        dve.drain()
                    for i in range(1, TI):
                        dve.wait_ge(s["part1_ready"], b * TI + i + 1)
                        dve.tensor_tensor(rest[:, i, :, :], qk[:, i, :, :], parts[:, i, :, LORA_BOTH_1, :],
                                          ALU.subtract).then_inc(s["rest_ready"], 1)
                    for i in range(TI):
                        dve.wait_ge(s["part2_ready"], b * TI + i + 1)
                        for n in range(2):
                            heads = slice(n * LORA_H, (n + 1) * LORA_H)
                            last = dve.tensor_tensor(parts[:, i, heads, LORA_PART_3[n], :], rest[:, i, heads, :],
                                                     parts[:, i, heads, LORA_BOTH_2, :], ALU.subtract)
                        last.then_inc(s["part3_ready"], 1)

                    def maxima(n, j):
                        for qi in CAUSAL_ORDER:
                            if qi != 0:
                                dve.wait_ge(s["s_ready"], 3 * n + CAUSAL_BANK[qi] + 1)
                            at = CAUSAL_COL[qi]
                            red = dve.tensor_reduce(nmax[:, j, qi:qi + 1], sc[:, j, at:at + (qi + 1) * P],
                                                    AX.X, ALU.max, negate=True)
                            if qi != 2:
                                red.then_inc(s["max_ready"], 1)

                    def head(p, j, normalise, more):
                        n = b * LORA_H + 2 * p + j
                        dve.wait_ge(s["t_ready"], 3 * n + 2)
                        dve.tensor_copy(probsT[:, j, S:2 * S], sc[:, j, S:2 * S])
                        dve.wait_ge(s["t_ready"], 3 * n + 3)
                        dve.tensor_copy(probsT[:, j, 2 * S:CAUSAL_COLS],
                                        sc[:, j, 2 * S:CAUSAL_COLS]).then_inc(s["pt_b"], 1)
                        if more:
                            maxima(n + 1, 1 - j)
                        if normalise:
                            weigh(p - 1)

                    def weigh(p):
                        dve.wait_ge(s["o_ready"], b * PAIRS + p + 1)
                        dve.reciprocal(rl[:, :, :], lsum[:, bass.ds(2 * p, 2), :])
                        dve.drain()
                        dve.tensor_tensor(on[:, :, bass.ds(2 * p, 2), :].rearrange("p q j r -> p j q r"),
                                          out2, rl[:, :, :].unsqueeze(3).to_broadcast([P, 2, TI, LORA_HD]),
                                          ALU.mult).then_inc(s["o_done"], 1)

                    maxima(b * LORA_H, 0)
                    head(0, 0, False, True)
                    head(0, 1, False, True)
                    with dve.Fori(1, PAIRS - 1) as p:
                        head(p, 0, True, True)
                        head(p, 1, False, True)
                    head(PAIRS - 1, 0, True, True)
                    head(PAIRS - 1, 1, False, False)
                    weigh(PAIRS - 1)
                    dve.wait_ge(s["y_ready"], b + 1)
                    for i in range(TI):
                        xi = x[:, b * TI + i, :]
                        dve.tensor_tensor(xi, bank(2 + i // 2)[:, (i % 2) * D:(i % 2 + 1) * D], xi, ALU.add)

            @block.gpsimd
            def _(pool):
                with pool.Fori(0, B) as b:
                    ln.invert(pool, g, b)

            @block.scalar
            def _(act):
                act.nop().then_inc(s["tq_read"], 1)
                with act.Fori(0, B) as b:
                    ln.copy(act, [bank(4), bank(5)], b)

                    def part_1(i):
                        act.wait_ge(s["qk_rotated"], b * TI + i + 1)
                        for n in range(2):
                            heads = slice(n * LORA_H, (n + 1) * LORA_H)
                            last = act.activation(parts[:, i, heads, LORA_PART_1[n], :],
                                                  qk[:, i, heads, :].unsqueeze(2)
                                                  .to_broadcast([P, LORA_H, 3, LORA_HD]), ACT.Copy)
                        last.then_inc(s["part1_ready"], 1)

                    def part_2(i):
                        act.wait_ge(s["rest_ready"], b * TI + i + 1)
                        for n in range(2):
                            heads = slice(n * LORA_H, (n + 1) * LORA_H)
                            last = act.activation(parts[:, i, heads, LORA_PART_2[n], :],
                                                  rest[:, i, heads, :].unsqueeze(2)
                                                  .to_broadcast([P, LORA_H, 2, LORA_HD]), ACT.Copy)
                        last.then_inc(s["part2_ready"], 1)

                    for i in range(TI):
                        part_1(i)
                        if i == 0:
                            act.wait_ge(s["v_ready"], b + 1)
                            for h in range(2):
                                last = act.activation(v[:, 2 * h:2 * h + 2, :].rearrange("p i d -> p (i d)"),
                                                      bank(4 + h), ACT.Copy)
                            last.then_inc(s["v_copied"], 1)
                    for i in range(TI):
                        part_2(i)

                    def turned(n, j):
                        act.wait_ge(s["tq_ready"], n + 1)
                        act.activation(qkT[:, j, :, :], tq[:, :, :], ACT.Copy).then_inc(s["tq_read"], 1)

                    def exponents(n, h, j):
                        for qi in CAUSAL_ORDER:
                            if qi != 0:
                                act.wait_ge(s["max_ready"], 3 * n + CAUSAL_BANK[qi] + 1)
                            at = CAUSAL_COL[qi]
                            ex = act.activation(probs[:, j, at:at + (qi + 1) * P], sc[:, j, at:at + (qi + 1) * P],
                                                ACT.Exp, bias=nmax[:, j, qi:qi + 1],
                                                accum_out=lsum[:, bass.ds(h, 1), qi])
                            if qi != 2:
                                ex.then_inc(s["e_ready"], 1)

                    def head(p, j, more, turns):
                        n = b * LORA_H + 2 * p + j
                        act.wait_ge(s["t_ready"], 3 * n + 1)
                        act.activation(probsT[:, j, 0:S], sc[:, j, 0:S], ACT.Copy).then_inc(s["pt_a"], 1)
                        if more:
                            exponents(n + 1, 2 * p + j + 1, 1 - j)
                        if turns:
                            turned(n + 2, j)

                    turned(b * LORA_H, 0)
                    turned(b * LORA_H + 1, 1)
                    exponents(b * LORA_H, 0, 0)
                    with act.Fori(0, PAIRS - 1) as p:
                        head(p, 0, True, True)
                        head(p, 1, True, True)
                    head(PAIRS - 1, 0, True, False)
                    head(PAIRS - 1, 1, False, False)
                    act.wait_ge(s["ot_ready"], b + 1)
                    for c in range(DC):
                        last = act.activation(onT[:, c, :], bank(c), ACT.Copy)
                    last.then_inc(s["onT_ready"], 1)

            @block.tensor
            def _(pe):
                ln.first_free(pe)
                with pe.Fori(0, B) as b:
                    pe.wait_ge(s["am_ready"], b + 1)
                    for n, name in enumerate("qkvo"):
                        for c in range(DC):
                            last = pe.matmul(bank(n)[:, c * D:(c + 1) * D], am[:, n, c * P:(c + 1) * P],
                                             g["lora_b" + name][:, :], start=True, stop=True)
                    last.then_inc(s["fold_ready"], 1)
                    ln.turn(pe, g, [bank(4), bank(5)], b)
                    pe.wait_ge(ln.xnT_ready, b + 1)
                    pe.wait_ge(s["w_ready"], b + 1)
                    for i in range(TI):
                        for c in range(DC):
                            last = pe.matmul(bank(i), ln.xnT[:, c, i * P:(i + 1) * P],
                                             w[:, c, 0:2, :].rearrange("p n d -> p (n d)"),
                                             start=(c == 0), stop=(c == DC - 1))
                        last.then_inc(s["pj_ready"], 1)
                    for i in range(TI):
                        for c in range(DC):
                            last = pe.matmul(bank(4 + i // 2)[:, (i % 2) * D:(i % 2 + 1) * D],
                                             ln.xnT[:, c, i * P:(i + 1) * P], w[:, c, 2, :],
                                             start=(c == 0), stop=(c == DC - 1))
                    last.then_inc(s["v_ready"], 1)

                    def turn(h):
                        n = b * LORA_H + h
                        pe.wait_ge(s["tq_read"], n + 1)
                        for kind in range(2):
                            for i in range(TI):
                                last = pe.transpose(tq[:, kind, i * P:(i + 1) * P],
                                                    parts[:, i, bass.ds(kind * LORA_H + h, 1), :, :]
                                                    .rearrange("p n u c -> p (n u c)"), ident_b[:, :])
                        last.then_inc(s["tq_ready"], 1)

                    def scores(n, j):
                        pe.wait_ge(s["tq_read"], n + 2)
                        for qi in CAUSAL_ORDER:
                            at = CAUSAL_COL[qi]
                            pe.matmul(sc[:, j, at:at + (qi + 1) * P], qkT[:, j, 0, qi * P:(qi + 1) * P],
                                      qkT[:, j, 1, 0:(qi + 1) * P], start=True, stop=False)
                            last = pe.matmul(sc[:, j, at + qi * P:at + (qi + 1) * P], ident_b[:, :], mask_b[:, :],
                                             start=False, stop=True)
                            if qi != 2:
                                last.then_inc(s["s_ready"], 1)

                    def turn_probs(n, j):
                        for qi in CAUSAL_ORDER:
                            if qi != 0:
                                pe.wait_ge(s["e_ready"], 3 * n + CAUSAL_BANK[qi] + 1)
                            for kj in range(qi + 1):
                                at = CAUSAL_COL[qi] + kj * P
                                last = pe.transpose(sc[:, j, at:at + P], probs[:, j, at:at + P], ident[:, :])
                            if qi != 2:
                                last.then_inc(s["t_ready"], 1)

                    def outputs(n, h, j, pairs_done):
                        for qi in range(TI):
                            for kj in range(qi + 1):
                                at = CAUSAL_COL[qi] + kj * P
                                last = pe.matmul(out2[:, j, qi, :], probsT[:, j, at:at + P],
                                                 v[:, kj, bass.ds(h * LORA_HD, LORA_HD)],
                                                 start=(kj == 0), stop=(kj == qi))
                        if j == 1:
                            last.then_inc(s["o_ready"], 1)

                    def head(p, j, before, after, turns):
                        h = 2 * p + j
                        n = b * LORA_H + h
                        turn_probs(n, j)
                        if before:
                            pe.wait_ge(s["pt_a"], n)
                            pe.wait_ge(s["pt_b"], n)
                        if after:
                            scores(n + 1, 1 - j)
                        if before:
                            if j == 1:
                                pe.wait_ge(s["o_done"], b * PAIRS + p + 1)
                            outputs(n - 1, h - 1, 1 - j, p)
                        if turns:
                            turn(h + 2)

                    pe.wait_ge(s["part3_ready"], b * TI + TI)
                    turn(0)
                    turn(1)
                    pe.wait_ge(s["v_copied"], b + 1)
                    scores(b * LORA_H, 0)
                    head(0, 0, False, True, True)
                    head(0, 1, True, True, True)
                    with pe.Fori(1, PAIRS - 1) as p:
                        head(p, 0, True, True, True)
                        head(p, 1, True, True, True)
                    head(PAIRS - 1, 0, True, True, False)
                    head(PAIRS - 1, 1, True, False, False)
                    pe.wait_ge(s["pt_a"], (b + 1) * LORA_H)
                    pe.wait_ge(s["pt_b"], (b + 1) * LORA_H)
                    outputs(b * LORA_H + LORA_H - 1, LORA_H - 1, 1, PAIRS)

                    pe.wait_ge(s["o_done"], b * PAIRS + PAIRS + 1)
                    for c in range(DC):
                        for i in range(TI):
                            last = pe.transpose(bank(c)[:, i * P:(i + 1) * P],
                                                on[:, i, 8 * c:8 * c + 8, :].rearrange("p h e -> p (h e)"), ident[:, :])
                    last.then_inc(s["ot_ready"], 1)
                    pe.wait_ge(s["onT_ready"], b + 1)
                    for i in range(TI):
                        for c in range(DC):
                            last = pe.matmul(bank(2 + i // 2)[:, (i % 2) * D:(i % 2 + 1) * D],
                                             onT[:, c, i * P:(i + 1) * P], w[:, c, 3, :],
                                             start=(c == 0), stop=(c == DC - 1))
                    last.then_inc(s["y_ready"], 1)
        k.clear_sems()


def rope_tables(length, dim, theta=10000.0):
    inv = (1.0 / theta ** (np.arange(0, dim, 2, dtype=np.float32) / np.float32(dim))).astype(np.float32)
    ang = np.arange(length, dtype=np.float32)[:, None] * inv
    return np.cos(ang).astype(np.float32), np.sin(ang).astype(np.float32)


def shape_constants():
    c = {}
    c["ident"] = np.eye(P, dtype=np.float32)
    causal = np.where(np.arange(P)[None, :] <= np.arange(P)[:, None], 0.0, NEG).astype(np.float32)
    c["mask"] = causal
    cos, sin = rope_tables(S, MLA_DR)
    q = np.arange(2)[:, None, None]
    e = np.arange(2)[None, :, None]
    r = np.arange(16)[None, None, :]
    freq = (16 * q + r + 0 * e).reshape(-1)
    sign = np.where(e + 0 * (q + r) == 0, -1.0, 1.0).reshape(-1).astype(np.float32)
    cn, sn = cos[:, freq], sin[:, freq] * sign
    t = np.stack([cn, sn], 1)
    c["ropeN"] = t.reshape(TI, P, 2, MLA_DR).transpose(1, 0, 2, 3)
    c["ropeT"] = np.concatenate([t, t], 2).transpose(2, 1, 0)
    hj, hk = np.arange(P) // 8, np.arange(P) // 8
    same = (hj[:, None] == hk[None, :])
    c["gla_sel"] = np.stack([same & (np.arange(P)[:, None] % 8 == j) for j in range(8)], 1).astype(np.float32)
    edge = np.zeros((P, P - GLA_H), bool)
    c["gla_hsum"] = np.concatenate([edge, hk[:, None] == np.arange(GLA_H)[None, :], edge], 1).astype(np.float32)
    c["gla_same"] = (np.arange(P)[:, None] % GLA_H == np.arange(P)[None, :] % GLA_H).astype(np.float32)
    cos, sin = rope_tables(S, LORA_HD)
    t = np.stack([np.stack([cos, cos], 1), np.stack([-sin, sin], 1)], 1)
    c["lora_rope"] = t.reshape(TI, P, 2, 2, LORA_HD // 2).transpose(1, 0, 2, 3, 4)
    c["lora_row"] = (np.arange(LORA_ROWS)[:, None] // LORA_RANK).astype(np.float32)
    c["lora_batch"] = np.tile(np.arange(B, dtype=np.float32), (LORA_ROWS, 1))
    return {n: np.ascontiguousarray(a) for n, a in c.items()}


MLA_PE = np.array([2 * (16 * q + r) + e for q in range(2) for e in range(2) for r in range(16)])


def chunked(a):
    return a.reshape(-1, P, *a.shape[1:]).swapaxes(0, 1)


def lay_out(i):
    w = {}
    w["x"] = i["L0_attn_a_x"].reshape(NT, P, D).transpose(1, 0, 2)
    wq = i["L0_attn_a_wq"].reshape(D, MLA_H, MLA_DN + MLA_DR)
    w["mla_wqT"] = wq[:, :, :MLA_DN].transpose(2, 1, 0)
    pe = wq[:, :, MLA_DN:][:, :, MLA_PE].reshape(D, MLA_PAIRS, 2, MLA_DR)[:, :, ::-1]
    w["mla_wq_pe"] = chunked(pe.reshape(D, MLA_PAIRS, P))
    wkvb = i["L0_attn_a_wkv_b"].reshape(MLA_R, MLA_H, 2 * P)
    w["mla_wkT"] = wkvb[:, :, :P].transpose(2, 1, 0)
    w["mla_wvT"] = wkvb[:, :, P:].transpose(2, 1, 0)
    w["mla_wo"] = i["L0_attn_a_wo"].reshape(MLA_H, P, D).transpose(1, 0, 2)
    kva = i["L0_attn_a_wkv_a"]
    w["wkva"] = chunked(np.concatenate([kva[:, :MLA_R], kva[:, MLA_R:][:, MLA_PE]], 1))
    w["kvw"] = np.broadcast_to(i["L0_attn_a_kv_norm_w"], (P, MLA_R))
    w["ffn_w"] = chunked(i["L0_ffn_weight"])
    w["ffn_scale"] = np.broadcast_to(i["L0_ffn_scale"], (P, D))
    w["cos_g"] = chunked(i["L0_attn_b_g_norm"])
    w["cos_wq"] = chunked(i["L0_attn_b_Wq"])
    w["cos_wkv"] = chunked(i["L0_attn_b_Wkv"])
    w["cos_wout"] = chunked(i["L0_attn_b_Wout"])
    w["cos_gout"] = np.broadcast_to(i["L0_attn_b_g_out"], (P, D))
    for n, name in (("gla_wq", "Wq"), ("gla_wk", "Wk"), ("gla_wgk1", "Wgk1")):
        w[n] = chunked(i["L1_attn_a_" + name])
    wv = i["L1_attn_a_Wv"].reshape(D, GLA_H, 2, 8)
    w["gla_wv"] = chunked(wv.transpose(0, 2, 1, 3).reshape(D, D))
    w["gla_wg"] = chunked(i["L1_attn_a_Wg"].reshape(D, GLA_H, GLA_DV).swapaxes(1, 2).reshape(D, D))
    w["gla_wgk2"] = i["L1_attn_a_Wgk2"]
    w["gla_bgk2"] = i["L1_attn_a_bgk2"].reshape(P, 1)
    w["gla_normw"] = np.repeat(i["L1_attn_a_norm_w"].reshape(2, GLA_HALF), GLA_H, axis=1).T
    w["gla_wo"] = chunked(i["L1_attn_a_Wo"].reshape(GLA_H, GLA_DV, D).swapaxes(0, 1).reshape(D, D))
    def f(name):
        return i["L1_ffn_" + name]

    def slots(a):
        return np.broadcast_to(a, (B, *a.shape)).reshape(B * WS_S, -1)

    w["ws_start"] = slots(f("workspace"))
    w["ws_cw"] = chunked(f("compete_w").T)
    w["ws_cb"] = slots(f("compete_b")[:, None])
    w["ws_write"] = chunked(f("write_w").T)
    w["ws_write_b"] = f("write_b")[None]
    wq, wk, wv = f("in_proj_w")[:D], f("in_proj_w")[D:2 * D], f("in_proj_w")[2 * D:]
    w["ws_wq"], w["ws_wk"], w["ws_wv"] = chunked(wq), chunked(wk.T), chunked(wv.T)
    w["ws_in_b"] = chunked(f("in_proj_b"))
    w["ws_out"] = chunked(f("out_proj_w").T)
    w["ws_out_b"] = np.broadcast_to(f("out_proj_b"), (1, B, D))
    w["ws_pre"] = chunked(f("norm_pre_w"))
    w["ws_post"] = np.broadcast_to(f("norm_post_w"), (P, D))
    eo = (np.arange(LORA_H)[:, None, None] * LORA_HD + 2 * np.arange(8)[None, None, :]
          + np.arange(2)[None, :, None]).reshape(-1)
    for n in "qkvo":
        wt, bt = i["L1_attn_b_W" + n].T, i["L1_attn_b_B" + n].transpose(0, 2, 1).reshape(LORA_ROWS, D)
        if n in ("q", "k"):
            wt, bt = wt[:, eo], bt[:, eo]
        w["lora_w" + n], w["lora_b" + n] = chunked(wt), bt
        w["lora_a" + n] = i["L1_attn_b_A" + n].reshape(LORA_ROWS, D)
    w["lora_starts"] = np.broadcast_to(i["L1_attn_b_lora_start_indices"], (LORA_ROWS, LORA_N))
    w.update(shape_constants())
    return {n: np.ascontiguousarray(a) for n, a in w.items()}


def build(nc, w, out, stages=None):
    with ExitStack() as ctx:
        k = Kit(nc, ctx)
        g = {"x": k.sb("x", [P, NT, D]), "ident": k.sb("ident", [P, P]),
             "ident_b": k.sb("ident_b", [P, P], BF16), "mask_b": k.sb("mask_b", [P, P], BF16),
             "neg_half": k.sb("neg_half", [P, 64]), "pos_half": k.sb("pos_half", [P, 64]),
             "ws_eps": k.sb("ws_eps", [P, TI])}
        for n in ("x_loaded", "weights_loaded", "late_loaded", "consts_loaded"):
            g[n] = k.sem(n)
        def hold(names, loaded):
            for n in names:
                g[n] = k.sb(n, list(w[n].shape), w[n].dtype)
            return [(g[n][tuple(slice(None) for _ in w[n].shape)], w[n], loaded) for n in names]

        early = ["ffn_w", "ffn_scale", "cos_g", "cos_wq", "cos_wkv", "cos_wout", "cos_gout"]
        g["early_loads"] = hold(early, g["weights_loaded"])
        with ExitStack() as mla_ctx:
            m = Kit(nc, mla_ctx)
            g["wap"] = m.sb("wap", [P, DC, MLA_PAIRS, 2, P])
            g["wvo"] = m.sb("wvo", [P, MLA_PAIRS, D])
            g["wq_pe"] = m.sb("wq_pe", [P, DC, MLA_PAIRS, P])
            first = ["mask", "wkva", "kvw", "ropeT", "ropeN"]
            for n in first:
                g[n] = m.sb(n, list(w[n].shape))
            g["first_loads"] = [(g[n][tuple(slice(None) for _ in w[n].shape)], n) for n in ["ident"] + first]
            mla_fold_weights(nc, g, w)
            small_constants(nc, g)
            mla_attention(nc, g)
        late = ["gla_wq", "gla_wk", "gla_wgk1", "gla_wv", "gla_wg", "gla_wgk2", "gla_bgk2", "gla_normw", "gla_wo",
                "gla_sel", "gla_hsum", "gla_same", "ws_start", "ws_cw", "ws_cb", "ws_write", "ws_write_b", "ws_wq", "ws_wk",
                "ws_wv", "ws_in_b", "ws_out", "ws_out_b", "ws_pre", "ws_post",
                "lora_wq", "lora_wk", "lora_wv", "lora_wo", "lora_aq", "lora_ak", "lora_av", "lora_ao",
                "lora_bq", "lora_bk", "lora_bv", "lora_bo", "lora_starts", "lora_rope", "lora_row", "lora_batch"]
        wait_for_loads(nc, g["weights_loaded"], len(early))
        ternary_ffn(nc, g, "ffa", hold(late, g["late_loaded"]))
        cosine_attention(nc, g)
        ternary_ffn(nc, g, "ffb", [])
        wait_for_loads(nc, g["late_loaded"], len(late))
        gated_linear_attention(nc, g)
        workspace_ffn(nc, g, "wsa")
        lora_attention(nc, g)
        workspace_ffn(nc, g, "wsb")
        store_output(nc, g, out)


def wait_for_loads(nc, loaded, count):
    with nc.Block() as block:
        @block.sync
        def _(sp):
            sp.wait_ge(loaded, 16 * count)


def small_constants(nc, g):
    with nc.Block() as block:
        @block.vector
        def _(dve):
            dve.memset(g["neg_half"][:, :], -0.5)
            dve.memset(g["pos_half"][:, :], 0.5)
            dve.memset(g["ws_eps"][:, :], WS_EPS)
            dve.wait_ge(g["consts_loaded"], 16 * len(g["first_loads"]))
            dve.tensor_copy(g["ident_b"][:, :], g["ident"][:, :])
            dve.tensor_copy(g["mask_b"][:, :], g["mask"][:, :])


def store_output(nc, g, out):
    with ExitStack() as ctx:
        stored = Kit(nc, ctx).sem("stored")
        with nc.Block() as block:
            @block.sync
            def _(sp):
                sp.dma_start(out.rearrange("b (i p) d -> p (b i) d", p=P), g["x"][:, :, :]).then_inc(stored, 16)
                sp.wait_ge(stored, 16)


def kernel(**inputs):
    import concourse.bacc as bacc
    from concourse.bass_utils import run_bass_kernel_spmd

    nc = bacc.Bacc("TRN2", target_bir_lowering=False, num_devices=1)
    arrays = lay_out({n: np.asarray(a) for n, a in inputs.items()})
    w = {n: nc.dram_tensor("in_" + n, a.shape, mybir.dt.from_np(a.dtype), kind="ExternalInput").ap()
         for n, a in arrays.items()}
    out = nc.dram_tensor("out_0", (B, S, D), F32, kind="ExternalOutput").ap()
    build(nc, w, out)
    r = run_bass_kernel_spmd(nc, [{"in_" + n: a for n, a in arrays.items()}], core_ids=[0])
    return r.results[0]["out_0"]
```

```python
from contextlib import ExitStack

import numpy as np

import concourse.bass as bass
from concourse import mybir

F32 = mybir.dt.float32
BF16 = mybir.dt.bfloat16
ALU = mybir.AluOpType
ACT = mybir.ActivationFunctionType
AX = mybir.AxisListType

P = 128
B, S, D = 4, 512, 256
TI = S // P
NT = B * TI
DC = D // P
LN_EPS = 1e-5
NEG = -1e30

CAUSAL_ORDER = (3, 2, 0, 1)
CAUSAL_COL = {3: 0, 2: S, 0: S + 3 * P, 1: 2 * S}
CAUSAL_COLS = 2 * S + 2 * P
CAUSAL_BANK = {3: 0, 2: 1, 0: 1, 1: 2}


class Kit:

    def __init__(self, nc, ctx):
        self.nc, self.ctx = nc, ctx
        self.sems = []

    def sb(self, name, shape, dtype=F32):
        return self.ctx.enter_context(self.nc.sbuf_tensor(name, shape, dtype))

    def ps(self, name, shape, dtype=F32):
        return self.ctx.enter_context(self.nc.psum_tensor(name, shape, dtype))

    def sem(self, name):
        self.sems.append(self.ctx.enter_context(self.nc.semaphore(name)))
        return self.sems[-1]

    def clear_sems(self):
        with self.nc.Block() as block:
            @block.gpsimd
            def _(pool):
                for s in self.sems:
                    pool.sem_clear(s)


def layer_norm_stats(dve, stats, mv, var_eps, tiles, eps, var_ready):
    n = len(tiles)
    for i, x in enumerate(tiles):
        dve.bn_stats(stats[:, i, :], x)
    dve.drain()
    for i in range(n):
        dve.bn_aggr(mv[:, i, :], stats[:, i, :])
    dve.drain()
    dve.tensor_scalar(var_eps, mv[:, 0:n, 1], eps, None, ALU.add).then_inc(var_ready, 1)


MLA_H, MLA_DN, MLA_DR, MLA_R = 16, 128, 64, 64
MLA_SCALE = float((MLA_DN + MLA_DR) ** -0.5)
MLA_PAIRS = MLA_H // 2
MLA_EPS = 1e-6


def mla_fold_weights(nc, g, w):
    with ExitStack() as ctx:
        k = Kit(nc, ctx)
        wqT = k.sb("mla_wqT", [P, MLA_H, D])
        wkT = k.sb("mla_wkT", [P, MLA_H, MLA_R])
        wvT = k.sb("mla_wvT", [P, MLA_H, MLA_R])
        wo = k.sb("mla_wo", [P, MLA_H, D])
        fold = k.ps("mla_fold", [P, 8, 512])
        loaded = k.sem("mla_fold_loaded")
        loaded_v = k.sem("mla_fold_loaded_v")
        pe_loaded = k.sem("mla_fold_pe_loaded")
        q_folded = k.sem("mla_q_folded")
        v_folded = k.sem("mla_v_folded")
        wap, wvo = g["wap"], g["wvo"]

        with nc.Block() as block:
            @block.sync
            def _(sp):
                sp.dma_start(wqT[:, :, :], w["mla_wqT"]).then_inc(loaded, 16)
                sp.dma_start(g["x"][:, :, :], w["x"]).then_inc(g["x_loaded"], 16)
                sp.dma_start(wo[:, :, :], w["mla_wo"]).then_inc(loaded_v, 16)
                for dst, src, done in g["early_loads"]:
                    sp.dma_start(dst, src).then_inc(done, 16)

            @block.tensor
            def _(pe):
                pe.wait_ge(loaded, 32)
                for c in range(DC):
                    for h in range(MLA_H):
                        last = pe.matmul(fold[:, 2 * c + h // 8, (h % 8) * 64:(h % 8 + 1) * 64],
                                         wqT[:, h, c * P:(c + 1) * P], wkT[:, h, :], start=True, stop=True)
                        if h % 8 == 7:
                            last.then_inc(q_folded, 1)
                pe.wait_ge(loaded_v, 32)
                for h in range(MLA_H):
                    last = pe.matmul(fold[64 * (h % 2):64 * (h % 2) + 64, 4 + h // 4,
                                          (h // 2 % 2) * D:(h // 2 % 2 + 1) * D],
                                     wvT[:, h, :], wo[:, h, :], start=True, stop=True)
                    if h % 4 == 3:
                        last.then_inc(v_folded, 1)

            @block.vector
            def _(dve):
                dve.wait_ge(pe_loaded, 16)
                for c in range(DC):
                    dve.tensor_scalar(wap[:, c, :, 1, :], g["wq_pe"][:, c, :, :], MLA_SCALE, None, ALU.mult)
                for n in range(2 * DC):
                    dve.wait_ge(q_folded, n + 1)
                    dve.tensor_scalar(wap[:, n // 2, 4 * (n % 2):4 * (n % 2) + 4, 0, :],
                                      fold[:, n, :].rearrange("p (a b) -> p a b", a=4), MLA_SCALE, None, ALU.mult)

            @block.scalar
            def _(act):
                act.dma_start(wkT[:, :, :], w["mla_wkT"]).then_inc(loaded, 16)
                act.dma_start(g["wq_pe"][:, :, :, :], w["mla_wq_pe"]).then_inc(pe_loaded, 16)
                act.dma_start(wvT[:, :, :], w["mla_wvT"]).then_inc(loaded_v, 16)
                for dst, name in g["first_loads"]:
                    act.dma_start(dst, w[name]).then_inc(g["consts_loaded"], 16)
                for n in range(4):
                    act.wait_ge(v_folded, n + 1)
                    act.activation(wvo[:, 2 * n:2 * n + 2, :].rearrange("p a b -> p (a b)"), fold[:, 4 + n, :],
                                   ACT.Copy)
        k.clear_sems()


def mla_attention(nc, g):
    with ExitStack() as ctx:
        k = Kit(nc, ctx)
        x, wap, wvo, ident, ident_b, mask_b = (g[n] for n in ("x", "wap", "wvo", "ident", "ident_b", "mask_b"))
        wkva, kvw, ropeT, ropeN = (g[n] for n in ("wkva", "kvw", "ropeT", "ropeN"))
        stats = k.sb("stats", [P, TI, 6])
        mv = k.sb("mv", [P, TI, 2])
        ve = k.sb("ve", [P, 2, TI])
        rstd = k.sb("rstd", [P, 2, TI])
        xn = k.sb("xn", [P, TI, D])
        xnT = k.sb("xnT", [P, DC, S])
        kva = k.sb("kva", [P, TI, P])
        sq = k.sb("sq", [P, TI, MLA_R])
        ss = k.sb("ss", [P, TI])
        kr1 = k.sb("kr1", [P, TI, MLA_DR])
        kr2 = k.sb("kr2", [P, TI, MLA_DR])
        kc = k.sb("kc", [P, TI, 2, P])
        kT = k.sb("kT", [P, 2, S])
        wst = k.sb("wst", [P, DC, 2, P])
        qT = k.sb("qT", [P, 2, S])
        swp = k.sb("swp", [P, S])
        rot1 = k.sb("rot1", [P, S])
        rot2 = k.sb("rot2", [P, S])
        nmax = k.sb("nmax", [P, 2, TI])
        lsum = k.sb("lsum", [P, 2, TI])
        rl = k.sb("rl", [P, 2, TI])
        probs = k.sb("probs", [P, 2, CAUSAL_COLS])
        probsT = k.sb("probsT", [P, 2, CAUSAL_COLS])
        on = k.sb("on", [P, TI, MLA_PAIRS, 2, MLA_R])
        onT = k.sb("onT", [P, 2, MLA_PAIRS, P])
        sc = k.ps("sc", [P, 2, 3 * 512])
        po = k.ps("po", [P, 2, TI, MLA_R])
        pq = k.ps("pq", [P, 512])
        row_banks = [po[:, :, :, :].rearrange("p j q r -> p (j q r)"), pq[:, :]]
        latent = row_banks[0].rearrange("p (i c) -> p i c", i=TI)

        def bank(n):
            return sc[:, n // 3, (n % 3) * 512:(n % 3 + 1) * 512]

        names = ("var_ready", "rstd_ready", "xn_ready", "xt_ready", "xnT_ready", "kva_ready", "kvar_ready",
                 "krstd_ready", "kc_ready", "kt_ready", "kT_ready", "staged", "qb_ready", "rope_in", "rope_done",
                 "qa_ready", "qa_copied", "s_ready", "max_ready", "e_ready", "t_ready", "pt_a", "pt_b", "o_ready",
                 "o_done", "ot_ready", "onT_a", "onT_b", "y_ready", "x_done")
        s = {n: k.sem("mla_" + n) for n in names}

        with nc.Block() as block:
            @block.vector
            def _(dve):
                dve.nop().then_inc(s["x_done"], 1)
                dve.nop().then_inc(s["x_done"], 1)
                dve.nop().then_inc(s["o_done"], 1)
                dve.wait_ge(g["x_loaded"], 16)
                dve.wait_ge(g["consts_loaded"], 16 * len(g["first_loads"]))
                def norm_rows(b):
                    dve.wait_ge(s["xt_ready"], b + 1)
                    layer_norm_stats(dve, stats, mv, ve[:, 0, :], [x[:, b * TI + i, :] for i in range(TI)],
                                     LN_EPS, s["var_ready"])
                    dve.wait_ge(s["rstd_ready"], b + 1)
                    for i in range(TI):
                        last = dve.tensor_scalar(xn[:, i, :], x[:, b * TI + i, :], mv[:, i, 0:1], rstd[:, 0, i:i + 1],
                                                 ALU.subtract, ALU.mult)
                    last.then_inc(s["xn_ready"], 1)

                def rope_queries(n):
                    dve.wait_ge(s["qb_ready"], n + 1)
                    dve.wait_ge(s["rope_done"], n + 1)
                    dve.tensor_tensor(rot1[:, :], pq[:, :], ropeT[:, 0, :], ALU.mult)
                    dve.stream_shuffle(swp[:, :], pq[:, :],
                                       [(r + 16) % 32 for r in range(32)]).then_inc(s["rope_in"], 1)

                def keys_values(b):
                    dve.wait_ge(s["kva_ready"], b + 1)
                    dve.tensor_copy(kva[:, :, :], latent[:, :, :])
                    dve.drain()
                    kv, pe4 = kva[:, :, 0:MLA_R], kva[:, :, MLA_R:].rearrange("p i (q e r) -> p i q e r", q=2, e=2)
                    dve.tensor_tensor(sq[:, :, :], kv, kv, ALU.mult)
                    dve.tensor_tensor(kr1[:, :, :], kva[:, :, MLA_R:], ropeN[:, :, 0, :], ALU.mult)
                    for e in range(2):
                        for q in range(2):
                            lo = q * 32 + e * 16
                            dve.tensor_tensor(kr2[:, :, lo:lo + 16], pe4[:, :, q, 1 - e, :],
                                              ropeN[:, :, 1, lo:lo + 16], ALU.mult)
                    dve.drain()
                    dve.tensor_reduce(ss[:, :], sq[:, :, :], AX.X, ALU.add)
                    dve.tensor_tensor(kc[:, :, 0, MLA_R:], kr1[:, :, :], kr2[:, :, :], ALU.add)
                    dve.tensor_tensor(kc[:, :, 1, 0:MLA_R], kr1[:, :, :], kr2[:, :, :], ALU.add)
                    dve.drain()
                    dve.tensor_scalar(ve[:, 1, :], ss[:, :], 1.0 / MLA_R, MLA_EPS, ALU.mult,
                                      ALU.add).then_inc(s["kvar_ready"], 1)
                    dve.wait_ge(s["krstd_ready"], b + 1)
                    dve.tensor_tensor(sq[:, :, :], kv, rstd[:, 1, :].unsqueeze(2).to_broadcast([P, TI, MLA_R]),
                                      ALU.mult)
                    dve.drain()
                    kvw_b = kvw[:, :].unsqueeze(1).to_broadcast([P, TI, MLA_R])
                    dve.tensor_tensor(kc[:, :, 0, 0:MLA_R], sq[:, :, :], kvw_b, ALU.mult)
                    dve.tensor_tensor(kc[:, :, 1, MLA_R:], sq[:, :, :], kvw_b, ALU.mult).then_inc(s["kc_ready"], 1)
                def batch(b, more):
                    def pair(p, last_pair):
                        n = b * MLA_PAIRS + p
                        for j in range(2):
                            for qi in CAUSAL_ORDER:
                                if qi != 0:
                                    dve.wait_ge(s["s_ready"], 6 * n + 3 * j + CAUSAL_BANK[qi] + 1)
                                at = CAUSAL_COL[qi]
                                red = dve.tensor_reduce(nmax[:, j, qi:qi + 1], sc[:, j, at:at + (qi + 1) * P],
                                                        AX.X, ALU.max, negate=True)
                                if qi != 2:
                                    red.then_inc(s["max_ready"], 1)
                        if not last_pair:
                            rope_queries(n + 1)
                        for j in range(2):
                            dve.wait_ge(s["t_ready"], 6 * n + 3 * j + 2)
                            dve.tensor_copy(probsT[:, j, S:2 * S], sc[:, j, S:2 * S])
                            dve.wait_ge(s["t_ready"], 6 * n + 3 * j + 3)
                            dve.tensor_copy(probsT[:, j, 2 * S:CAUSAL_COLS],
                                            sc[:, j, 2 * S:CAUSAL_COLS]).then_inc(s["pt_b"], 1)
                        dve.reciprocal(rl[:, :, :], lsum[:, :, :])
                        dve.drain()
                        dve.wait_ge(s["o_ready"], n + 1)
                        dve.tensor_tensor(on[:, :, p, :, :].rearrange("p q j r -> p j q r"), po[:, :, :, :],
                                          rl[:, :, :].unsqueeze(3).to_broadcast([P, 2, TI, MLA_R]),
                                          ALU.mult).then_inc(s["o_done"], 1)

                    with dve.Fori(0, MLA_PAIRS - 1) as p:
                        pair(p, False)
                    pair(MLA_PAIRS - 1, True)
                    def copy_turned(i):
                        dve.wait_ge(s["ot_ready"], 2 * (b * TI + i) + 2)
                        dve.tensor_copy(onT[:, i % 2, 4:8, :].rearrange("p a t -> p (a t)"),
                                        bank(2 * (i % 2) + 1)).then_inc(s["onT_b"], 1)

                    def add_output(i):
                        dve.wait_ge(s["y_ready"], b * TI + i + 1)
                        xi = x[:, b * TI + i, :]
                        dve.tensor_tensor(xi, bank(4 + i % 2)[:, 0:D], xi, ALU.add).then_inc(s["x_done"], 1)

                    copy_turned(0)
                    if more:
                        norm_rows(b + 1)
                    copy_turned(1)
                    add_output(0)
                    copy_turned(2)
                    add_output(1)
                    if more:
                        keys_values(b + 1)
                    copy_turned(3)
                    add_output(2)
                    add_output(3)
                    if more:
                        rope_queries((b + 1) * MLA_PAIRS)

                norm_rows(0)
                keys_values(0)
                rope_queries(0)
                with dve.Fori(0, B - 1) as b:
                    batch(b, True)
                batch(B - 1, False)

            @block.gpsimd
            def _(pool):
                pool.nop().then_inc(s["rope_done"], 1)

                def stage(p):
                    pool.tensor_copy(wst[:, :, :, :], wap[:, :, p, :, :]).then_inc(s["staged"], 1)

                def norms(b):
                    pool.wait_ge(s["qa_ready"], b * MLA_PAIRS + 1)
                    for which, (var, std) in enumerate((("var_ready", "rstd_ready"), ("kvar_ready", "krstd_ready"))):
                        pool.wait_ge(s[var], b + 1)
                        pool.tensor_tensor(rstd[:, which, :], ve[:, which, :], g["neg_half"][:, 0:TI],
                                           ALU.pow).then_inc(s[std], 1)
                        if which == 0:
                            stage(0)

                def batch(b, more):
                    def rope(n):
                        pool.wait_ge(s["rope_in"], n + 1)
                        pool.tensor_tensor(rot2[:, :], swp[:, :], ropeT[:, 1, :], ALU.mult)
                        pool.drain()
                        pool.tensor_tensor(qT[0:64, 1, :], rot1[0:64, :], rot2[0:64, :], ALU.add)
                        pool.drain()
                        pool.tensor_tensor(qT[64:P, 0, :], rot1[64:P, :], rot2[64:P, :],
                                           ALU.add).then_inc(s["rope_done"], 1)
                        pool.drain()

                    with pool.Fori(0, MLA_PAIRS - 1) as p:
                        rope(b * MLA_PAIRS + p)
                        pool.wait_ge(s["qa_ready"], b * MLA_PAIRS + p + 2)
                        stage(p + 1)
                    rope(b * MLA_PAIRS + MLA_PAIRS - 1)
                    if more:
                        norms(b + 1)

                norms(0)
                with pool.Fori(0, B - 1) as b:
                    batch(b, True)
                batch(B - 1, False)

            @block.scalar
            def _(act):
                act.nop().then_inc(s["qa_copied"], 1)

                def copy_latent_queries(n):
                    act.wait_ge(s["qa_ready"], n + 2)
                    act.activation(qT[0:64, 0, :], pq[0:64, :], ACT.Copy)
                    act.activation(qT[64:P, 1, :], pq[64:P, :], ACT.Copy).then_inc(s["qa_copied"], 1)

                def copy_rows(b):
                    act.wait_ge(s["xt_ready"], b + 2)
                    for c in range(DC):
                        last = act.activation(xnT[:, c, :], row_banks[c], ACT.Copy)
                    last.then_inc(s["xnT_ready"], 1)

                def copy_keys(b):
                    act.wait_ge(s["kt_ready"], b + 1)
                    for v in range(2):
                        last = act.activation(kT[:, v, :], bank(v), ACT.Copy)
                    last.then_inc(s["kT_ready"], 1)
                    copy_latent_queries(b * MLA_PAIRS)

                def batch(b, more):
                    def pair(p, last_pair):
                        n = b * MLA_PAIRS + p
                        for j in range(2):
                            for qi in CAUSAL_ORDER:
                                if qi != 0:
                                    act.wait_ge(s["max_ready"], 6 * n + 3 * j + CAUSAL_BANK[qi] + 1)
                                at = CAUSAL_COL[qi]
                                ex = act.activation(probs[:, j, at:at + (qi + 1) * P], sc[:, j, at:at + (qi + 1) * P],
                                                    ACT.Exp, bias=nmax[:, j, qi:qi + 1],
                                                    accum_out=lsum[:, j, qi:qi + 1])
                                if qi != 2:
                                    ex.then_inc(s["e_ready"], 1)
                        for j in range(2):
                            act.wait_ge(s["t_ready"], 6 * n + 3 * j + 1)
                            act.activation(probsT[:, j, 0:S], sc[:, j, 0:S], ACT.Copy).then_inc(s["pt_a"], 1)
                            if j == 0 and not last_pair:
                                copy_latent_queries(n + 1)

                    with act.Fori(0, MLA_PAIRS - 1) as p:
                        pair(p, False)
                    pair(MLA_PAIRS - 1, True)
                    for i in range(TI):
                        act.wait_ge(s["ot_ready"], 2 * (b * TI + i) + 1)
                        act.activation(onT[:, i % 2, 0:4, :].rearrange("p a t -> p (a t)"), bank(2 * (i % 2)),
                                       ACT.Copy).then_inc(s["onT_a"], 1)
                        if more and i == 1:
                            copy_rows(b + 1)
                    if more:
                        copy_keys(b + 1)

                copy_rows(0)
                copy_keys(0)
                with act.Fori(0, B - 1) as b:
                    batch(b, True)
                batch(B - 1, False)

            @block.tensor
            def _(pe):
                pe.nop().then_inc(s["xt_ready"], 1)
                pe.nop().then_inc(s["qa_ready"], 1)

                def turn_rows(b):
                    pe.wait_ge(s["xn_ready"], b + 1)
                    for c in range(DC):
                        for i in range(TI):
                            last = pe.transpose(row_banks[c][:, i * P:(i + 1) * P], xn[:, i, c * P:(c + 1) * P],
                                                ident[:, :])
                    last.then_inc(s["xt_ready"], 1)

                def latents(b):
                    pe.wait_ge(s["xnT_ready"], b + 1)
                    for i in range(TI):
                        for c in range(DC):
                            last = pe.matmul(latent[:, i, :], xnT[:, c, i * P:(i + 1) * P],
                                             wkva[:, c, :], start=(c == 0), stop=(c == DC - 1))
                    last.then_inc(s["kva_ready"], 1)
                    project(b * MLA_PAIRS, 1)

                def project(n, kind):
                    if kind == 1:
                        pe.wait_ge(s["staged"], n + 1)
                        pe.wait_ge(s["qa_copied"], n + 1)
                    else:
                        pe.wait_ge(s["rope_in"], n + 1)
                    for c in range(DC):
                        last = pe.matmul(pq[:, :], wst[:, c, kind, :], xnT[:, c, :], start=(c == 0),
                                         stop=(c == DC - 1))
                    last.then_inc(s["qb_ready" if kind == 1 else "qa_ready"], 1)

                def turn_keys(b):
                    pe.wait_ge(s["kc_ready"], b + 1)
                    for v in range(2):
                        for i in range(TI):
                            last = pe.transpose(bank(v)[:, i * P:(i + 1) * P], kc[:, i, v, :], ident[:, :])
                    last.then_inc(s["kt_ready"], 1)
                    project(b * MLA_PAIRS, 0)

                def batch(b, more):
                    def pair(p, last_pair):
                        n = b * MLA_PAIRS + p
                        pe.wait_ge(s["kT_ready"], b + 1)
                        pe.wait_ge(s["rope_done"], n + 2)
                        pe.wait_ge(s["qa_copied"], n + 2)
                        for j in range(2):
                            for qi in CAUSAL_ORDER:
                                at = CAUSAL_COL[qi]
                                pe.matmul(sc[:, j, at:at + (qi + 1) * P], qT[:, j, qi * P:(qi + 1) * P],
                                          kT[:, j, 0:(qi + 1) * P], start=True, stop=False)
                                last = pe.matmul(sc[:, j, at + qi * P:at + (qi + 1) * P], ident_b[:, :], mask_b[:, :],
                                                 start=False, stop=True)
                                if qi != 2:
                                    last.then_inc(s["s_ready"], 1)
                        for j in range(2):
                            if not last_pair:
                                project(n + 1, 1 - j)
                            for qi in CAUSAL_ORDER:
                                if qi != 0:
                                    pe.wait_ge(s["e_ready"], 6 * n + 3 * j + CAUSAL_BANK[qi] + 1)
                                for kj in range(qi + 1):
                                    at = CAUSAL_COL[qi] + kj * P
                                    last = pe.transpose(sc[:, j, at:at + P], probs[:, j, at:at + P], ident[:, :])
                                if qi != 2:
                                    last.then_inc(s["t_ready"], 1)
                        pe.wait_ge(s["o_done"], n + 1)
                        for j in range(2):
                            pe.wait_ge(s["pt_a"], 2 * n + j + 1)
                            pe.wait_ge(s["pt_b"], 2 * n + j + 1)
                            for qi in range(TI):
                                for kj in range(qi + 1):
                                    at = CAUSAL_COL[qi] + kj * P
                                    last = pe.matmul(po[:, j, qi, :], probsT[:, j, at:at + P], kc[:, kj, 0, 0:MLA_R],
                                                     start=(kj == 0), stop=(kj == qi))
                        last.then_inc(s["o_ready"], 1)

                    with pe.Fori(0, MLA_PAIRS - 1) as p:
                        pair(p, False)
                    pair(MLA_PAIRS - 1, True)

                    def turn(i):
                        for hp in range(MLA_PAIRS):
                            last = pe.transpose(bank(2 * (i % 2) + hp // 4)[:, (hp % 4) * P:(hp % 4 + 1) * P],
                                                on[:, i, hp, :, :].rearrange("p j r -> p (j r)"), ident[:, :])
                            if hp % 4 == 3:
                                last.then_inc(s["ot_ready"], 1)

                    def project_outputs(i):
                        pe.wait_ge(s["onT_a"], b * TI + i + 1)
                        pe.wait_ge(s["onT_b"], b * TI + i + 1)
                        pe.wait_ge(s["x_done"], b * TI + i + 1)
                        for hp in range(MLA_PAIRS):
                            last = pe.matmul(bank(4 + i % 2)[:, 0:D], onT[:, i % 2, hp, :], wvo[:, hp, :],
                                             start=(hp == 0), stop=(hp == MLA_PAIRS - 1))
                        last.then_inc(s["y_ready"], 1)

                    pe.wait_ge(s["o_done"], b * MLA_PAIRS + MLA_PAIRS + 1)
                    turn(0)
                    turn(1)
                    project_outputs(0)
                    if more:
                        turn_rows(b + 1)
                    turn(2)
                    project_outputs(1)
                    if more:
                        latents(b + 1)
                    turn(3)
                    project_outputs(2)
                    project_outputs(3)
                    if more:
                        turn_keys(b + 1)

                turn_rows(0)
                latents(0)
                turn_keys(0)
                with pe.Fori(0, B - 1) as b:
                    batch(b, True)
                batch(B - 1, False)
        k.clear_sems()


class Normed:

    def __init__(self, k, tag):
        self.stats = k.sb(tag + "_stats", [P, TI, 6])
        self.mv = k.sb(tag + "_mv", [P, TI, 2])
        self.ve = k.sb(tag + "_ve", [P, TI])
        self.rstd = k.sb(tag + "_rstd", [P, TI])
        self.xn = k.sb(tag + "_xn", [P, TI, D])
        self.xnT = k.sb(tag + "_xnT", [P, DC, S])
        self.var_ready = k.sem(tag + "_var_ready")
        self.rstd_ready = k.sem(tag + "_rstd_ready")
        self.xn_ready = k.sem(tag + "_xn_ready")
        self.xt_ready = k.sem(tag + "_xt_ready")
        self.xnT_ready = k.sem(tag + "_xnT_ready")

    def scale_rows(self, dve, x, b):
        for i in range(TI):
            last = dve.tensor_scalar(self.xn[:, i, :], x[:, b * TI + i, :], self.mv[:, i, 0:1], self.rstd[:, i:i + 1],
                                     ALU.subtract, ALU.mult)
        return last

    def norm(self, dve, x, b):
        dve.wait_ge(self.xt_ready, b + 1)
        layer_norm_stats(dve, self.stats, self.mv, self.ve[:, :], [x[:, b * TI + i, :] for i in range(TI)],
                         LN_EPS, self.var_ready)
        dve.wait_ge(self.rstd_ready, b + 1)
        self.scale_rows(dve, x, b).then_inc(self.xn_ready, 1)

    def invert(self, pool, g, b):
        pool.wait_ge(self.var_ready, b + 1)
        pool.tensor_tensor(self.rstd[:, :], self.ve[:, :], g["neg_half"][:, 0:TI], ALU.pow).then_inc(self.rstd_ready, 1)

    def turn(self, pe, g, banks, b):
        pe.wait_ge(self.xn_ready, b + 1)
        for c in range(DC):
            for i in range(TI):
                last = pe.transpose(banks[c][:, i * P:(i + 1) * P], self.xn[:, i, c * P:(c + 1) * P], g["ident"][:, :])
        last.then_inc(self.xt_ready, 1)

    def first_free(self, pe):
        pe.nop().then_inc(self.xt_ready, 1)

    def copy(self, act, banks, b):
        act.wait_ge(self.xt_ready, b + 2)
        for c in range(DC):
            last = act.activation(self.xnT[:, c, :], banks[c], ACT.Copy)
        last.then_inc(self.xnT_ready, 1)


FFN_EPS = 1e-7


def ternary_ffn(nc, g, tag, loads):
    with ExitStack() as ctx:
        k = Kit(nc, ctx)
        x = g["x"]
        ln = Normed(k, tag)
        y = k.sb(tag + "_y", [P, NT, D])
        sq = k.sb(tag + "_sq", [P, TI, D])
        n2 = k.sb(tag + "_n2", [P, NT])
        norm = k.sb(tag + "_norm", [P, NT])
        t = k.sb(tag + "_t", [P, 8, NT])
        ps = k.ps(tag + "_ps", [P, 8, 512])
        y_ready = k.sem(tag + "_y_ready")
        y_scaled = k.sem(tag + "_y_scaled")
        norms_ready = k.sem(tag + "_norms_ready")
        root_ready = k.sem(tag + "_root_ready")
        clipped = k.sem(tag + "_clipped")
        tanh_ready = k.sem(tag + "_tanh_ready")
        banks = [ps[:, 0, :], ps[:, 1, :]]

        with nc.Block() as block:
            @block.sync
            def _(sp):
                for dst, src, done in loads:
                    sp.dma_start(dst, src).then_inc(done, 16)

            @block.vector
            def _(dve):
                dve.nop().then_inc(y_scaled, 1)

                def scale_products(b):
                    dve.wait_ge(y_ready, b + 1)
                    dve.tensor_tensor(y[:, bass.ds(b * TI, TI), :].rearrange("p (h i) d -> p h i d", i=2),
                                      ps[:, 2:4, :].rearrange("p h (i d) -> p h i d", i=2),
                                      g["ffn_scale"][:, :].unsqueeze(1).unsqueeze(1).to_broadcast([P, 2, 2, D]),
                                      ALU.mult).then_inc(y_scaled, 1)

                ln.norm(dve, x, 0)
                with dve.Fori(0, B - 1) as b:
                    ln.norm(dve, x, b + 1)
                    scale_products(b)
                scale_products(B - 1)
                dve.wait_ge(root_ready, 1)
                dve.tensor_scalar(t[:, 0, :], norm[:, :], FFN_EPS, None, ALU.max).then_inc(clipped, 1)
                dve.drain()
                dve.tensor_scalar(t[:, 2, :], t[:, 0, :], FFN_EPS, None, ALU.add)
                dve.drain()
                dve.reciprocal(t[:, 3, :], t[:, 2, :])
                dve.drain()
                dve.wait_ge(tanh_ready, 1)
                dve.tensor_tensor(t[:, 4, :], t[:, 1, :], t[:, 3, :], ALU.mult)
                dve.drain()
                dve.tensor_tensor(t[:, 5, :], norm[:, :], t[:, 4, :], ALU.mult)
                dve.drain()
                dve.tensor_scalar(t[:, 6, :], t[:, 5, :], FFN_EPS, None, ALU.max)
                dve.drain()
                dve.reciprocal(t[:, 7, :], t[:, 6, :])
                dve.drain()
                dve.tensor_scalar(t[:, 0, :], t[:, 7, :], 0.99, 1.0, ALU.mult, ALU.min)
                dve.drain()
                dve.tensor_tensor(t[:, 2, :], t[:, 0, :], t[:, 4, :], ALU.mult)
                dve.drain()
                for i in range(NT):
                    dve.scalar_tensor_tensor(x[:, i, :], y[:, i, :], t[:, 2, i:i + 1], x[:, i, :],
                                             ALU.mult, ALU.add)

            @block.gpsimd
            def _(pool):
                with pool.Fori(0, B) as b:
                    ln.invert(pool, g, b)
                pool.wait_ge(norms_ready, B)
                pool.tensor_tensor(norm[:, :], n2[:, :], g["pos_half"][:, 0:NT], ALU.pow).then_inc(root_ready, 1)

            @block.scalar
            def _(act):
                def squares(b):
                    act.wait_ge(y_scaled, b + 2)
                    for i in range(TI):
                        last = act.activation(sq[:, i:i + 1, :], y[:, bass.ds(b * TI + i, 1), :], ACT.Square,
                                              accum_out=n2[:, bass.ds(b * TI + i, 1)])
                    last.then_inc(norms_ready, 1)
                    act.drain()

                ln.copy(act, banks, 0)
                with act.Fori(0, B - 1) as b:
                    ln.copy(act, banks, b + 1)
                    squares(b)
                squares(B - 1)
                act.wait_ge(clipped, 1)
                act.activation(t[:, 1, :], t[:, 0, :], ACT.Tanh).then_inc(tanh_ready, 1)

            @block.tensor
            def _(pe):
                ln.first_free(pe)

                def product(b):
                    pe.wait_ge(ln.xnT_ready, b + 1)
                    pe.wait_ge(y_scaled, b + 1)
                    for i in range(TI):
                        for c in range(DC):
                            last = pe.matmul(ps[:, 2 + i // 2, (i % 2) * D:(i % 2 + 1) * D],
                                             ln.xnT[:, c, i * P:(i + 1) * P], g["ffn_w"][:, c, :],
                                             start=(c == 0), stop=(c == DC - 1))
                    last.then_inc(y_ready, 1)

                ln.turn(pe, g, banks, 0)
                with pe.Fori(0, B - 1) as b:
                    product(b)
                    ln.turn(pe, g, banks, b + 1)
                product(B - 1)
        k.clear_sems()


COS_H, COS_D = 16, 128
COS_SCALE = 16.0


def cosine_attention(nc, g):
    with ExitStack() as ctx:
        k = Kit(nc, ctx)
        x, ident, wq, wkv, wout, gout = (g[n] for n in ("x", "ident", "cos_wq", "cos_wkv", "cos_wout", "cos_gout"))
        ln = Normed(k, "cos")
        var2 = k.sb("cos_var2", [P, 2, TI])
        rstd2 = k.sb("cos_rstd2", [P, TI])
        kk = k.sb("cos_kk", [P, TI, P])
        ksum = k.sb("cos_ksum", [P, 3, TI])
        kn = k.sb("cos_kn", [P, TI, P])
        kT = k.sb("cos_kT", [P, S])
        vx = k.sb("cos_vx", [P, TI, COS_D + 1])
        qsq = k.sb("cos_qsq", [P, 2, 4, P])
        qss = k.sb("cos_qss", [P, 2, 4])
        qse = k.sb("cos_qse", [P, 2, 4])
        qrs = k.sb("cos_qrs", [P, 2, 4])
        qn = k.sb("cos_qn", [P, 2, 4, P])
        qT = k.sb("cos_qT", [P, COS_H, S])
        probs = k.sb("cos_probs", [P, 2, TI, S])
        rl = k.sb("cos_rl", [P, 2, TI])
        on = qT[:, :, :].rearrange("p h (i c) -> p i h c", i=TI)
        onT = k.sb("cos_onT", [P, 2, COS_H, P])
        yn = k.sb("cos_yn", [P, TI, D])
        ps = k.ps("cos_ps", [P, 8, 512])
        po = ps[:, 4:8, 0:2 * (COS_D + 1)].rearrange("p (j a) (q c) -> p j a q c", j=2, c=COS_D + 1)
        names = ("scaled_w", "var2_ready", "rstd2_ready", "kv_ready", "k_var", "k_rstd", "kn_ready", "kt_ready",
                 "kT_ready", "q_ready", "q_sq", "q_var", "q_rstd", "qn_ready", "qt_ready", "qT_ready", "s_ready",
                 "e_ready", "o_ready", "o_done", "ot_ready", "onT_a", "onT_d", "y_ready", "y_var", "y_rstd")
        s = {n: k.sem("cos_" + n) for n in names}
        banks = [ps[:, 6, :], ps[:, 7, :]]
        q_bank = (0, 1, 6, 7)
        y = [ps[:, 4 + i // 2, (i % 2) * D:(i % 2 + 1) * D] for i in range(TI)]
        LAST = COS_H // 4 - 1
        QU = COS_H // 4 * TI

        with nc.Block() as block:
            @block.vector
            def _(dve):
                dve.nop().then_inc(s["o_done"], 2)
                dve.nop().then_inc(s["qn_ready"], TI)
                dve.nop().then_inc(s["q_var"], 2)
                for c in range(DC):
                    dve.tensor_scalar(wq[:, c, :], wq[:, c, :], g["cos_g"][:, c:c + 1], None, ALU.mult)
                    dve.tensor_scalar(wkv[:, c, :], wkv[:, c, :], g["cos_g"][:, c:c + 1], None, ALU.mult)
                dve.memset(vx[:, :, COS_D:], 1.0).then_inc(s["scaled_w"], 1)

                def norm_rows(b):
                    dve.wait_ge(ln.xt_ready, b + 1)
                    layer_norm_stats(dve, ln.stats, ln.mv, ln.ve[:, :], [x[:, b * TI + i, :] for i in range(TI)],
                                     LN_EPS, ln.var_ready)
                    dve.wait_ge(ln.rstd_ready, b + 1)
                    dve.tensor_tensor(var2[:, 0, :], ln.mv[:, :, 1], ln.rstd[:, :], ALU.mult)
                    dve.drain()
                    dve.tensor_tensor(var2[:, 0, :], var2[:, 0, :], ln.rstd[:, :], ALU.mult)
                    dve.drain()
                    dve.tensor_scalar(var2[:, 1, :], var2[:, 0, :], LN_EPS, None, ALU.add).then_inc(s["var2_ready"], 1)
                    dve.wait_ge(s["rstd2_ready"], b + 1)
                    dve.tensor_tensor(ln.rstd[:, :], rstd2[:, :], ln.rstd[:, :], ALU.mult)
                    dve.drain()
                    ln.scale_rows(dve, x, b).then_inc(ln.xn_ready, 1)

                def keys_values(b):
                    dve.wait_ge(s["kv_ready"], b + 1)
                    kv = ps[:, 6:8, :].rearrange("p a (i c) -> p a i c", i=2)
                    dve.tensor_copy(kk.rearrange("p (a i) c -> p a i c", a=2), kv[:, :, :, 0:P])
                    dve.tensor_copy(vx[:, :, 0:COS_D].rearrange("p (a i) c -> p a i c", a=2), kv[:, :, :, P:])
                    dve.drain()
                    dve.tensor_tensor(kn[:, :, :], kk[:, :, :], kk[:, :, :], ALU.mult)
                    dve.drain()
                    dve.tensor_reduce(ksum[:, 0, :], kn[:, :, :], AX.X, ALU.add)
                    dve.drain()
                    dve.tensor_scalar(ksum[:, 1, :], ksum[:, 0, :], 1e-12, None, ALU.add).then_inc(s["k_var"], 1)
                    dve.wait_ge(s["k_rstd"], b + 1)
                    for i in range(TI):
                        last = dve.tensor_scalar(kn[:, i, :], kk[:, i, :], ksum[:, 2, i:i + 1], COS_SCALE,
                                                 ALU.mult, ALU.mult)
                    last.then_inc(s["kn_ready"], 1)

                def batch(b, more):
                    def sums(u, i):
                        dve.wait_ge(s["q_sq"], u + 1)
                        dve.tensor_reduce(qss[:, i % 2, :], qsq[:, i % 2, :, :], AX.X, ALU.add)
                        dve.drain()
                        dve.tensor_scalar(qse[:, i % 2, :], qss[:, i % 2, :], 1e-12 / 256, None,
                                          ALU.add).then_inc(s["q_var"], 1)

                    def scale(u, i):
                        dve.wait_ge(s["q_rstd"], u + 1)
                        dve.wait_ge(s["qt_ready"], u + 1)
                        dve.tensor_tensor(qn[:, i % 2, :, :],
                                          ps[:, q_bank[i], :].rearrange("p (h c) -> p h c", h=4),
                                          qrs[:, i % 2, :].unsqueeze(2).to_broadcast([P, 4, P]),
                                          ALU.mult).then_inc(s["qn_ready"], 1)

                    def four_heads(hq, last_four):
                        for i in range(TI):
                            u = b * QU + hq * TI + i
                            if not (last_four and i + 1 == TI):
                                sums(u + 1, (i + 1) % TI)
                            scale(u, i)

                    sums(b * QU, 0)
                    with dve.Fori(0, LAST) as hq:
                        four_heads(hq, False)
                    four_heads(LAST, True)
                    if more:
                        norm_rows(b + 1)

                    with dve.Fori(0, COS_H // 2) as p:
                        for j in range(2):
                            h = b * COS_H + 2 * p + j
                            dve.wait_ge(s["o_ready"], h + 1)
                            dve.reciprocal(rl[:, j, :].rearrange("p (a q) -> p a q", a=2), po[:, j, :, :, COS_D])
                            dve.drain()
                            dve.tensor_tensor(on[:, :, 2 * p + j, :].rearrange("p (a q) c -> p a q c", a=2),
                                              po[:, j, :, :, 0:COS_D],
                                              rl[:, j, :].rearrange("p (a q) -> p a q", a=2).unsqueeze(3)
                                              .to_broadcast([P, 2, 2, COS_D]), ALU.mult).then_inc(s["o_done"], 1)
                    for i in range(TI):
                        for n in (1, 3):
                            dve.wait_ge(s["ot_ready"], 4 * (b * TI + i) + n + 1)
                            last = dve.tensor_copy(onT[:, i % 2, 4 * n:4 * n + 4, :].rearrange("p a t -> p (a t)"),
                                                   ps[:, n, :])
                        last.then_inc(s["onT_d"], 1)
                        if i == 0 and more:
                            keys_values(b + 1)
                    dve.wait_ge(s["y_ready"], b + 1)
                    layer_norm_stats(dve, ln.stats, ln.mv, ln.ve[:, :], y, LN_EPS, s["y_var"])
                    dve.wait_ge(s["y_rstd"], b + 1)
                    for i in range(TI):
                        dve.tensor_scalar(yn[:, i, :], y[i], ln.mv[:, i, 0:1], ln.rstd[:, i:i + 1],
                                          ALU.subtract, ALU.mult)
                    dve.drain()
                    dve.tensor_tensor(yn[:, :, :], yn[:, :, :], gout[:, :].unsqueeze(1).to_broadcast([P, TI, D]),
                                      ALU.mult)
                    dve.drain()
                    for i in range(TI):
                        xi = x[:, b * TI + i, :]
                        dve.tensor_tensor(xi, yn[:, i, :], xi, ALU.add)

                norm_rows(0)
                keys_values(0)
                with dve.Fori(0, B - 1) as b:
                    batch(b, True)
                batch(B - 1, False)

            @block.gpsimd
            def _(pool):
                nh = g["neg_half"]

                def norms(b):
                    ln.invert(pool, g, b)
                    pool.wait_ge(s["var2_ready"], b + 1)
                    pool.tensor_tensor(rstd2[:, :], var2[:, 1, :], nh[:, 0:TI], ALU.pow).then_inc(s["rstd2_ready"], 1)
                    pool.wait_ge(s["k_var"], b + 1)
                    pool.tensor_tensor(ksum[:, 2, :], ksum[:, 1, :], nh[:, 0:TI], ALU.pow).then_inc(s["k_rstd"], 1)

                def batch(b, more):
                    with pool.Fori(0, COS_H // 4) as hq:
                        for i in range(TI):
                            pool.wait_ge(s["q_var"], b * QU + hq * TI + i + 3)
                            pool.tensor_tensor(qrs[:, i % 2, :], qse[:, i % 2, :], nh[:, 0:4],
                                               ALU.pow).then_inc(s["q_rstd"], 1)
                    if more:
                        norms(b + 1)
                    pool.wait_ge(s["y_var"], b + 1)
                    pool.tensor_tensor(ln.rstd[:, :], ln.ve[:, :], nh[:, 0:TI], ALU.pow).then_inc(s["y_rstd"], 1)

                norms(0)
                with pool.Fori(0, B - 1) as b:
                    batch(b, True)
                batch(B - 1, False)

            @block.scalar
            def _(act):
                for _ in range(TI):
                    act.nop().then_inc(s["e_ready"], 1)
                for _ in range(2):
                    act.nop().then_inc(s["qT_ready"], 1)

                def copy_keys(b):
                    act.wait_ge(s["kt_ready"], b + 1)
                    act.activation(kT[:, :], ps[:, 6, :], ACT.Copy).then_inc(s["kT_ready"], 1)

                def batch(b, more):
                    def square(u, i):
                        act.wait_ge(s["q_ready"], u + 1)
                        act.wait_ge(s["q_var"], u + 1)
                        act.activation(qsq[:, i % 2, :, :].rearrange("p h c -> p (h c)"), ps[:, q_bank[i], :],
                                       ACT.Square).then_inc(s["q_sq"], 1)

                    def four_heads(hq, last_four):
                        for i in range(TI):
                            u = b * QU + hq * TI + i
                            if not (last_four and i + 2 >= TI):
                                square(u + 2, (i + 2) % TI)
                            act.wait_ge(s["qt_ready"], u + 3)
                            act.activation(qT[:, bass.ts(hq, 4), i * P:(i + 1) * P],
                                           ps[:, 2 + i % 2, :].rearrange("p (h t) -> p h t", h=4),
                                           ACT.Copy).then_inc(s["qT_ready"], 1)

                    square(b * QU, 0)
                    square(b * QU + 1, 1)
                    with act.Fori(0, LAST) as hq:
                        four_heads(hq, False)
                    four_heads(LAST, True)
                    with act.Fori(0, COS_H // 2) as p:
                        for j in range(2):
                            for kj in range(TI):
                                act.wait_ge(s["s_ready"], TI * (b * COS_H + 2 * p + j) + kj + 1)
                                act.activation(probs[:, j, kj, :], ps[:, kj, :], ACT.Exp).then_inc(s["e_ready"], 1)
                    if more:
                        ln.copy(act, banks, b + 1)
                    for i in range(TI):
                        for n in (0, 2):
                            act.wait_ge(s["ot_ready"], 4 * (b * TI + i) + n + 1)
                            last = act.activation(onT[:, i % 2, 4 * n:4 * n + 4, :].rearrange("p a t -> p (a t)"),
                                                  ps[:, n, :], ACT.Copy)
                        last.then_inc(s["onT_a"], 1)
                    if more:
                        copy_keys(b + 1)

                ln.copy(act, banks, 0)
                copy_keys(0)
                with act.Fori(0, B - 1) as b:
                    batch(b, True)
                batch(B - 1, False)

            @block.tensor
            def _(pe):
                ln.first_free(pe)
                for _ in range(2):
                    pe.nop().then_inc(s["qt_ready"], 1)
                pe.wait_ge(s["scaled_w"], 1)

                def keys_values(b):
                    pe.wait_ge(ln.xnT_ready, b + 1)
                    for i in range(TI):
                        for c in range(DC):
                            last = pe.matmul(ps[:, 6 + i // 2, (i % 2) * D:(i % 2 + 1) * D],
                                             ln.xnT[:, c, i * P:(i + 1) * P], wkv[:, c, :],
                                             start=(c == 0), stop=(c == DC - 1))
                    last.then_inc(s["kv_ready"], 1)

                def turn_keys(b):
                    pe.wait_ge(s["kn_ready"], b + 1)
                    for i in range(TI):
                        last = pe.transpose(ps[:, 6, i * P:(i + 1) * P], kn[:, i, :], ident[:, :])
                    last.then_inc(s["kt_ready"], 1)

                def batch(b, more):
                    def project(u, hq, i):
                        pe.wait_ge(s["qn_ready"], u + 1)
                        for c in range(DC):
                            last = pe.matmul(ps[:, q_bank[i], :], ln.xnT[:, c, i * P:(i + 1) * P],
                                             wq[:, c, bass.ts(hq, 512)], start=(c == 0), stop=(c == DC - 1))
                        last.then_inc(s["q_ready"], 1)

                    def four_heads(hq, last_four):
                        for i in range(TI):
                            u = b * QU + hq * TI + i
                            if i == 0:
                                project(u + 3, hq, 3)
                            elif not last_four:
                                project(u + 3, hq + 1, i - 1)
                            pe.wait_ge(s["qn_ready"], u + TI + 1)
                            pe.wait_ge(s["qT_ready"], u + 1)
                            for h in range(4):
                                last = pe.transpose(ps[:, 2 + i % 2, h * P:(h + 1) * P], qn[:, i % 2, h, :],
                                                    ident[:, :])
                            last.then_inc(s["qt_ready"], 1)

                    project(b * QU, 0, 0)
                    project(b * QU + 1, 0, 1)
                    pe.wait_ge(s["kT_ready"], b + 1)
                    project(b * QU + 2, 0, 2)
                    with pe.Fori(0, LAST) as hq:
                        four_heads(hq, False)
                    four_heads(LAST, True)

                    with pe.Fori(0, COS_H // 2) as p:
                        pe.wait_ge(s["qT_ready"], b * QU + QU + 2)
                        for j in range(2):
                            h = b * COS_H + 2 * p + j
                            for kj in range(TI):
                                pe.wait_ge(s["e_ready"], TI * h + kj + 1)
                                pe.matmul(ps[:, kj, :], kT[:, kj * P:(kj + 1) * P], qT[:, 2 * p + j, :],
                                          start=True, stop=True).then_inc(s["s_ready"], 1)
                        for j in range(2):
                            h = b * COS_H + 2 * p + j
                            pe.wait_ge(s["e_ready"], TI * h + 2 * TI)
                            pe.wait_ge(s["o_done"], h + 1)
                            for qi in range(TI):
                                for kj in range(TI):
                                    last = pe.matmul(po[:, j, qi // 2, qi % 2, :],
                                                     probs[:, j, kj, qi * P:(qi + 1) * P], vx[:, kj, :],
                                                     start=(kj == 0), stop=(kj == TI - 1))
                            last.then_inc(s["o_ready"], 1)

                    def turn(i):
                        for h in range(COS_H):
                            last = pe.transpose(ps[:, h // 4, (h % 4) * P:(h % 4 + 1) * P], on[:, i, h, :],
                                                ident[:, :])
                            if h % 4 == 3:
                                last.then_inc(s["ot_ready"], 1)

                    pe.wait_ge(s["o_done"], b * COS_H + COS_H + 2)
                    if more:
                        ln.turn(pe, g, banks, b + 1)
                    turn(0)
                    if more:
                        keys_values(b + 1)
                    for i in range(TI):
                        pe.wait_ge(s["onT_a"], b * TI + i + 1)
                        pe.wait_ge(s["onT_d"], b * TI + i + 1)
                        if i + 1 < TI:
                            turn(i + 1)
                        for h in range(COS_H):
                            last = pe.matmul(y[i], onT[:, i % 2, h, :], wout[:, h, :],
                                             start=(h == 0), stop=(h == COS_H - 1))
                    last.then_inc(s["y_ready"], 1)
                    if more:
                        turn_keys(b + 1)

                ln.turn(pe, g, banks, 0)
                keys_values(0)
                turn_keys(0)
                with pe.Fori(0, B - 1) as b:
                    batch(b, True)
                batch(B - 1, False)
        k.clear_sems()


GLA_H, GLA_DK, GLA_DV, GLA_LR = 16, 8, 16, 16
GLA_SCALE = float(GLA_DK ** -0.5)
GLA_EPS = 1e-5
GATE_NORMALIZER = 16.0
GLA_HALF = GLA_DV // 2


def gated_linear_attention(nc, g):
    with ExitStack() as ctx:
        k = Kit(nc, ctx)
        x = g["x"]
        ln = Normed(k, "gla")
        qT = k.sb("gla_qT", [P, B, S])
        kT = k.sb("gla_kT", [P, B, S])
        q_now = k.sb("gla_q_now", [P, S])
        vT = k.sb("gla_vT", [P, B, 2, S])
        z1 = k.sb("gla_z1", [GLA_LR, S])
        za = k.sb("gla_za", [P, S])
        z = k.sb("gla_z", [P, B, S])
        decay = k.sb("gla_decay", [P, B, S])
        gate = k.sb("gla_gate", [P, B, 2, S])
        ge = k.sb("gla_ge", [P, B, 2, S])
        room = [g["cos_wout"][:, 4 * n:4 * n + 4, :].rearrange("p h d -> p (h d)") for n in range(4)]
        kv = room[0].rearrange("p (n s) -> p n s", n=2)
        st = room[1].rearrange("p (n s) -> p n s", n=2)
        qs = k.sb("gla_qs", [P, 2, S])
        eps = k.sb("gla_eps", [P, 1])
        orstd = k.sb("gla_orstd", [P, S])
        o = room[2].rearrange("p (n s) -> p n s", n=2)
        osq = room[3].rearrange("p (n s) -> p n s", n=2)
        ogT = ln.xnT
        ps = k.ps("gla_ps", [P, 8, 512])
        names = ("q_ready", "k_ready", "v_ready", "z1_ready", "z1_copied", "z_ready", "g_ready", "g_read", "q_now_ready",
                 "kT_ready", "vT_ready", "za_ready", "ez_ready", "ln_ready", "lg_ready", "decay_ready", "ge_ready",
                 "sigmoid_ready", "vrep_ready", "kv_ready", "st_ready", "qs_ready", "qs_read",
                 "half_copied", "ms_ready", "orstd_ready", "ogT_ready", "y_ready")
        s = {n: k.sem("gla_" + n) for n in names}
        banks = [ps[:, 0, :], ps[:, 1, :]]
        gps = ps[:, 6:8, :]

        with nc.Block() as block:
            @block.vector
            def _(dve):
                dve.memset(eps[:, :], GLA_EPS)
                for _ in range(2):
                    dve.nop().then_inc(s["kv_ready"], 1)
                ln.norm(dve, x, 0)

                def gates(b, more):
                    dve.wait_ge(s["z_ready"], b + 1)
                    dve.tensor_scalar(z[:, bass.ds(b, 1), :].rearrange("p o s -> p (o s)"), ps[:, 5, :],
                                      g["gla_bgk2"][:, 0:1], None, ALU.add)
                    dve.drain()
                    zb = z[:, bass.ds(b, 1), :].rearrange("p o s -> p (o s)")
                    dve.scalar_tensor_tensor(za[:, :], zb, -1.0, zb, ALU.mult, ALU.min).then_inc(s["za_ready"], 1)
                    if more:
                        ln.norm(dve, x, b + 1)
                    dve.wait_ge(s["ge_ready"], b + 1)
                    for half in range(2):
                        last = dve.tensor_scalar(gate[:, bass.ds(b, 1), half, :], gps[:, half, :].unsqueeze(1),
                                                 g["gla_normw"][:, half:half + 1], None, ALU.mult)
                    last.then_inc(s["g_read"], 1)

                with dve.Fori(0, B - 1) as b:
                    gates(b, True)
                gates(B - 1, False)
                dve.wait_ge(s["ln_ready"], 1)
                dve.scalar_tensor_tensor(z[:, :, :], z[:, :, :], 0.0, decay[:, :, :], ALU.min,
                                         ALU.subtract).then_inc(s["lg_ready"], 1)

                def scan_half(b, half, between={}):
                    for j in range(GLA_HALF):
                        if j in between:
                            between[j](b - 1)
                        n = b * GLA_DV + half * GLA_HALF + j
                        if j == 0:
                            dve.wait_ge(s["decay_ready"], b + 1)
                        dve.wait_ge(s["vrep_ready"], n + 1)
                        dve.tensor_tensor(kv[:, j % 2, :], ps[:, j % 2, :],
                                          kT[:, bass.ds(b, 1), :].rearrange("p o s -> p (o s)"),
                                          ALU.mult).then_inc(s["kv_ready"], 1)
                        dve.drain()
                        dve.wait_ge(s["qs_ready"], n + 1)
                        dve.tensor_tensor_scan(st[:, j % 2, :],
                                               decay[:, bass.ds(b, 1), :].rearrange("p o s -> p (o s)"),
                                               kv[:, j % 2, :], 0.0, ALU.mult, ALU.add).then_inc(s["st_ready"], 1)

                def finish_gate(b):
                    dve.wait_ge(s["sigmoid_ready"], b + 1)
                    gb = gate[:, bass.ds(b, 1), :, :]
                    dve.tensor_tensor(gb, gb, ge[:, bass.ds(b, 1), :, :], ALU.mult)

                def gate_outputs(b):
                    dve.wait_ge(s["orstd_ready"], b + 1)
                    dve.tensor_tensor(o, o, orstd[:, :].unsqueeze(1).to_broadcast([P, 2, S]), ALU.mult)
                    dve.drain()
                    dve.tensor_tensor(ogT[:, :, :], o, gate[:, bass.ds(b, 1), :, :].rearrange("p o n s -> p (o n) s"),
                                      ALU.mult).then_inc(s["ogT_ready"], 1)

                def add_outputs(b):
                    dve.wait_ge(s["y_ready"], b + 1)
                    for i in range(TI):
                        xi = x[:, b * TI + i, :]
                        dve.tensor_tensor(xi, ps[:, 6 + i // 2, (i % 2) * D:(i % 2 + 1) * D], xi, ALU.add)

                scan_half(0, 0)
                with dve.Fori(0, B - 1) as b:
                    scan_half(b, 1)
                    scan_half(b + 1, 0, {2: finish_gate, 6: gate_outputs})
                    add_outputs(b)
                scan_half(B - 1, 1)
                finish_gate(B - 1)
                gate_outputs(B - 1)
                add_outputs(B - 1)

            @block.gpsimd
            def _(pool):
                for _ in range(2):
                    pool.nop().then_inc(s["qs_ready"], 1)
                with pool.Fori(0, B) as b:
                    ln.invert(pool, g, b)
                with pool.Fori(0, B) as b:
                    with pool.Fori(0, 2) as half:
                        for j in range(GLA_HALF):
                            if j == 0:
                                pool.wait_ge(s["q_now_ready"], b + 1)
                            n = b * GLA_DV + half * GLA_HALF + j
                            pool.wait_ge(s["qs_read"], n + 1)
                            pool.wait_ge(s["st_ready"], n + 1)
                            pool.tensor_tensor(qs[:, j % 2, :], st[:, j % 2, :],
                                               q_now[:, :], ALU.mult).then_inc(s["qs_ready"], 1)

            @block.scalar
            def _(act):
                act.nop().then_inc(s["half_copied"], 2)
                with act.Fori(0, B) as b:
                    ln.copy(act, banks, b)
                    act.wait_ge(s["z1_ready"], b + 1)
                    act.activation(z1[:, :], ps[0:GLA_LR, 4, :], ACT.Copy).then_inc(s["z1_copied"], 1)
                    act.wait_ge(s["q_ready"], b + 1)
                    act.activation(qT[:, bass.ds(b, 1), :], ps[:, 2, :].unsqueeze(1), ACT.Copy,
                                   scale=GLA_SCALE)
                    act.wait_ge(s["za_ready"], b + 1)
                    act.activation(decay[:, bass.ds(b, 1), :], za[:, :].unsqueeze(1), ACT.Exp).then_inc(s["ez_ready"], 1)
                    act.wait_ge(s["g_ready"], b + 1)
                    act.activation(ge[:, bass.ds(b, 1), :, :].rearrange("p o n s -> p (o n) s"), gps, ACT.Exp, scale=-1.0)\
                        .then_inc(s["ge_ready"], 1)
                    act.wait_ge(s["k_ready"], b + 1)
                    act.activation(kT[:, bass.ds(b, 1), :], ps[:, 0, :].unsqueeze(1), ACT.Copy)\
                        .then_inc(s["kT_ready"], 1)
                    act.wait_ge(s["v_ready"], b + 1)
                    act.activation(vT[:, bass.ds(b, 1), :, :].rearrange("p o c s -> p (o c) s"), ps[:, 3:5, :],
                                   ACT.Copy).then_inc(s["vT_ready"], 1)
                act.drain()
                act.activation(q_now[:, :], qT[:, 0, :], ACT.Copy).then_inc(s["q_now_ready"], 1)
                act.activation(decay[:, :, :], decay[:, :, :], ACT.Ln, bias=1.0).then_inc(s["ln_ready"], 1)
                act.activation(ge[:, :, :, :], ge[:, :, :, :], ACT.Ln, bias=1.0)
                act.drain()
                for b in range(B):
                    if b == 0:
                        act.wait_ge(s["lg_ready"], 1)
                    act.activation(decay[:, b, :], z[:, b, :], ACT.Exp,
                                   scale=1.0 / GATE_NORMALIZER).then_inc(s["decay_ready"], 1)
                for b in range(B):
                    act.activation(ge[:, b, :, :], ge[:, b, :, :], ACT.Exp, scale=-1.0).then_inc(s["sigmoid_ready"], 1)

                def collect(m, half):
                    act.wait_ge(s["qs_read"], GLA_HALF * m + GLA_HALF + 2)
                    act.activation(o[:, half, :], ps[:, 2 + half, :], ACT.Copy)
                    act.activation(osq[:, half, :], ps[:, 2 + half, :], ACT.Square).then_inc(s["half_copied"], 1)

                def invert(b):
                    act.wait_ge(s["ms_ready"], b + 1)
                    act.activation(orstd[:, :], ps[:, 4, :], ACT.Ln, bias=eps[:, 0:1], scale=1.0 / GLA_DV)
                    act.drain()
                    act.activation(orstd[:, :], orstd[:, :], ACT.Exp, scale=-0.5).then_inc(s["orstd_ready"], 1)

                collect(0, 0)
                with act.Fori(0, B - 1) as b:
                    act.wait_ge(s["qs_ready"], (b + 1) * GLA_DV + 2)
                    act.activation(q_now[:, :], qT[:, bass.ds(b + 1, 1), :].rearrange("p o s -> p (o s)"),
                                   ACT.Copy).then_inc(s["q_now_ready"], 1)
                    collect(2 * b + 1, 1)
                    invert(b)
                    collect(2 * b + 2, 0)
                collect(2 * B - 1, 1)
                invert(B - 1)

            @block.tensor
            def _(pe):
                ln.first_free(pe)
                for _ in range(2):
                    pe.nop().then_inc(s["qs_read"], 1)
                for n in ("kT_ready", "vT_ready", "g_read"):
                    pe.nop().then_inc(s[n], 1)
                with pe.Fori(0, B) as b:
                    def turned(bank, weights, rows, ready):
                        for c in range(DC):
                            last = pe.matmul(ps[0:rows, bank, :], weights[:, c, :], ln.xnT[:, c, :],
                                             start=(c == 0), stop=(c == DC - 1))
                        if ready:
                            last.then_inc(s[ready], 1)

                    pe.wait_ge(s["kT_ready"], b + 1)
                    ln.turn(pe, g, banks, b)
                    pe.wait_ge(s["vT_ready"], b + 1)
                    pe.wait_ge(ln.xnT_ready, b + 1)
                    turned(4, g["gla_wgk1"], GLA_LR, "z1_ready")
                    turned(2, g["gla_wq"], P, "q_ready")
                    pe.wait_ge(s["z1_copied"], b + 1)
                    pe.matmul(ps[:, 5, :], g["gla_wgk2"][:, :], z1[:, :], start=True,
                              stop=True).then_inc(s["z_ready"], 1)
                    pe.wait_ge(s["g_read"], b + 1)
                    turned(6, g["gla_wg"][:, :, 0:P], P, None)
                    turned(7, g["gla_wg"][:, :, P:D], P, "g_ready")
                    turned(0, g["gla_wk"], P, "k_ready")
                    turned(3, g["gla_wv"][:, :, 0:P], P, None)
                    turned(4, g["gla_wv"][:, :, P:D], P, "v_ready")

                def repeat(b, half, j):
                    pe.wait_ge(s["kv_ready"], b * GLA_DV + half * GLA_HALF + j + 1)
                    pe.matmul(ps[:, j % 2, :], g["gla_sel"][:, j, :], vT[:, bass.ds(b, 1), half, :].rearrange("p o s -> p (o s)"),
                              start=True, stop=True).then_inc(s["vrep_ready"], 1)

                def sums(b, half, j):
                    if j == 0:
                        pe.wait_ge(s["half_copied"], 2 * b + half + 1)
                    pe.wait_ge(s["qs_ready"], b * GLA_DV + half * GLA_HALF + j + 3)
                    at = (GLA_HALF - 1 - j) * GLA_H
                    pe.matmul(ps[:, 2 + half, :], g["gla_hsum"][:, at:at + P], qs[:, j % 2, :], start=(j == 0),
                              stop=(j == GLA_HALF - 1)).then_inc(s["qs_read"], 1)

                def scan_half(b, half, first=False, last=False, after=None):
                    for j in range(GLA_HALF):
                        if j + 1 < GLA_HALF:
                            repeat(b, half, j + 1)
                        elif half == 0:
                            repeat(b, 1, 0)
                        elif not last:
                            repeat(b + 1, 0, 0)
                        if j > 0:
                            sums(b, half, j - 1)
                        elif half == 1:
                            sums(b, 0, GLA_HALF - 1)
                        elif not first:
                            sums(b - 1, 1, GLA_HALF - 1)
                        if after and j == 4:
                            after()

                def mean_squares(b):
                    pe.wait_ge(s["half_copied"], 2 * b + 4)
                    for half in range(2):
                        last = pe.matmul(ps[:, 4, :], g["gla_same"][:, :], osq[:, half, :], start=(half == 0),
                                         stop=(half == 1))
                    last.then_inc(s["ms_ready"], 1)

                def project_outputs(b):
                    pe.wait_ge(s["ogT_ready"], b + 1)
                    for i in range(TI):
                        for c in range(DC):
                            last = pe.matmul(ps[:, 6 + i // 2, (i % 2) * D:(i % 2 + 1) * D],
                                             ogT[:, c, i * P:(i + 1) * P], g["gla_wo"][:, c, :],
                                             start=(c == 0), stop=(c == DC - 1))
                    last.then_inc(s["y_ready"], 1)

                for n in ("kT_ready", "vT_ready"):
                    pe.wait_ge(s[n], B + 1)
                repeat(0, 0, 0)
                scan_half(0, 0, first=True)
                with pe.Fori(0, B - 1) as b:
                    scan_half(b, 1)
                    scan_half(b + 1, 0, after=lambda: mean_squares(b))
                    project_outputs(b)
                scan_half(B - 1, 1, last=True)
                sums(B - 1, 1, GLA_HALF - 1)
                mean_squares(B - 1)
                project_outputs(B - 1)
        k.clear_sems()


WS_S, WS_K, WS_NB, WS_H = 16, 4, 2, 4
WS_HD = D // WS_H
WS_ROWS = B * WS_S
WS_EPS = 1e-6
SENTINEL = -3e38


def workspace_ffn(nc, g, tag):
    with ExitStack() as ctx:
        k = Kit(nc, ctx)
        x, ident = g["x"], g["ident"]

        def sb(name, shape):
            return k.sb(f"{tag}_{name}", shape)

        stats, mv = sb("stats", [P, NT, 6]), sb("mv", [P, NT, 2])
        ve, rstd = sb("ve", [P, NT]), sb("rstd", [P, NT])
        cw = sb("cw", [P, DC, WS_S])
        xf = sb("xf", [P, NT, D])
        xsum = sb("xsum", [P, 2, TI, D])
        xfT = sb("xfT", [P, DC, NT * P])
        junk = sb("junk", [P, 2, D])
        msq, mse, inv = sb("msq", [P, 2, NT]), sb("mse", [P, 2, NT]), sb("inv", [P, 2, NT])
        lg = sb("lg", [P, TI, WS_ROWS])
        lt = sb("lt", [WS_ROWS, S + 8])
        top, match = sb("top", [WS_ROWS, 8]), sb("match", [WS_ROWS, 8])
        ntop = sb("ntop", [WS_ROWS, 1])
        etop = sb("etop", [WS_ROWS, WS_K])
        zsum, rz = sb("zsum", [WS_ROWS, 1]), sb("rz", [WS_ROWS, 1])
        elt = sb("elt", [WS_ROWS, S])
        marked = sb("marked", [WS_ROWS, S + 8])
        chosen = sb("chosen", [WS_ROWS, S])
        selw = sb("selw", [WS_ROWS, S])
        selT = sb("selT", [P, TI, WS_ROWS])
        xselT = sb("xselT", [P, DC, WS_ROWS])
        ws = sb("ws", [WS_ROWS, D])
        wsum, wsq = sb("wsum", [WS_ROWS, D]), sb("wsq", [WS_ROWS, D])
        wss, wse, wsr = sb("wss", [WS_ROWS, 1]), sb("wse", [WS_ROWS, 1]), sb("wsr", [WS_ROWS, 1])
        wsT = sb("wsT", [P, DC, WS_ROWS])
        kbd = sb("kbd", [P, 2, B, 2, WS_S])
        vbd = sb("vbd", [P, 2, B, 2, WS_S])
        m = sb("m", [P, DC, 2, B, 2 * WS_S])
        cb = sb("cb", [1, 2, B, 2 * WS_S])
        nb_w = sb("nb", [65, B, D])
        ones = sb("ones", [1, P])
        amax, al = sb("amax", [P, B, TI * WS_H]), sb("al", [P, B, TI * WS_H])
        ar = sb("ar", [P, B, TI * WS_H])
        ash = sb("ash", [P, B, TI * WS_H, WS_S])
        att = sb("att", [P, B, TI, WS_H * WS_S])
        attT = sb("attT", [65, B, S])
        ps = k.ps(tag + "_ps", [P, 8, 512])
        names = ("setup", "bias_loaded", "var_ready", "rstd_ready", "xf_ready", "xt_ready", "xfT_ready",
                 "msq_ready", "r_ready", "lg_ready", "lg_done", "lt_ready", "ntop_ready", "exp_ready", "selw_ready",
                 "st_ready", "selT_ready", "xsel_ready", "xselT_ready", "written", "wss_ready", "wsr_ready",
                 "ws_ready", "wt_ready", "wsT_ready", "kv_ready", "bd_ready", "m_ready", "cb_ready", "nb_ready",
                 "fold_v", "fold_a", "a_ready", "ash_ready", "ae_ready", "att_ready", "at_ready",
                 "attT_ready", "xb_ready", "xsum_ready", "m2_ready", "r2_ready")
        s = {n: k.sem(f"{tag}_{n}") for n in names}
        bias = g["ws_in_b"]

        def tiles(b):
            return slice(b * TI, (b + 1) * TI)

        def staggered(*steps):
            for t in range(B + len(steps) - 1):
                for n, step in enumerate(steps):
                    if 0 <= t - n < B:
                        step(t - n)

        with nc.Block() as block:
            @block.sync
            def _(sp):
                sp.dma_start(nb_w[64:65, :, :], g["ws_out_b"][:, :, :]).then_inc(s["bias_loaded"], 16)
                sp.dma_start(ws[:, :], g["ws_start"][:, :]).then_inc(s["bias_loaded"], 16)

            @block.vector
            def _(dve):
                dve.memset(kbd[:, :, :, :, :], 0.0)
                dve.memset(vbd[:, :, :, :, :], 0.0)
                dve.memset(ones[:, :], 1.0)
                dve.memset(attT[64:65, :, :], 1.0)
                dve.memset(lt[:, S:], SENTINEL)
                dve.memset(match[:, WS_K:], SENTINEL)
                for c in range(DC):
                    last = dve.tensor_scalar(cw[:, c, :], g["ws_cw"][:, c, :], g["ws_pre"][:, c:c + 1], None, ALU.mult)
                last.then_inc(s["setup"], 1)

                def statistics(b):
                    layer_norm_stats(dve, stats[:, tiles(b), :], mv[:, tiles(b), :], ve[:, tiles(b)],
                                     [x[:, b * TI + i, :] for i in range(TI)], LN_EPS, s["var_ready"])

                def scale_rows(b):
                    dve.wait_ge(s["rstd_ready"], b + 1)
                    for i in range(b * TI, (b + 1) * TI):
                        last = dve.tensor_scalar(xf[:, i, :], x[:, i, :], mv[:, i, 0:1], rstd[:, i:i + 1],
                                                 ALU.subtract, ALU.mult)
                    last.then_inc(s["xf_ready"], 1)

                staggered(statistics, scale_rows)
                dve.drain()
                with dve.Fori(0, WS_NB) as r:
                    for b in range(B):
                        dve.wait_ge(s["lg_ready"], r * B + b + 1)
                        dve.wait_ge(s["r_ready"], r * B + b + 1)
                        dve.tensor_tensor(lg[:, :, b * WS_S:(b + 1) * WS_S],
                                          ps[:, 4 + b % 2, 0:TI * WS_S].rearrange("p (i s) -> p i s", i=TI),
                                          inv[:, 0, tiles(b)].unsqueeze(2).to_broadcast([P, TI, WS_S]),
                                          ALU.mult).then_inc(s["lg_done"], 1)
                    dve.wait_ge(s["lt_ready"], r + 1)
                    dve.tensor_scalar(lt[:, 0:S], ps[0:WS_ROWS, 6, :], g["ws_cb"][:, 0:1], None, ALU.add)
                    dve.drain()
                    dve.max(top[:, :], lt[:, 0:S])
                    dve.drain()
                    dve.tensor_scalar(ntop[:, :], top[:, 0:1], -1.0, None, ALU.mult).then_inc(s["ntop_ready"], 1)
                    dve.tensor_copy(match[:, 0:WS_K], top[:, 0:WS_K])
                    dve.drain()
                    dve.match_replace(marked[:, :], match[:, :], lt[:, :], -SENTINEL)
                    dve.drain()
                    dve.tensor_tensor(chosen[:, :], marked[:, 0:S], lt[:, 0:S], ALU.not_equal)
                    dve.wait_ge(s["exp_ready"], r + 1)
                    dve.tensor_reduce(zsum[:, :], etop[:, :], AX.X, ALU.add)
                    dve.drain()
                    dve.reciprocal(rz[:, :], zsum[:, :])
                    dve.drain()
                    dve.scalar_tensor_tensor(selw[:, :], elt[:, :], rz[:, 0:1], chosen[:, :], ALU.mult,
                                             ALU.mult).then_inc(s["selw_ready"], 1)
                    dve.wait_ge(s["st_ready"], r + 1)
                    dve.tensor_copy(selT[:, :, :], ps[:, 4, 0:TI * WS_ROWS].rearrange("p (i s) -> p i s", i=TI))\
                       .then_inc(s["selT_ready"], 1)
                    dve.wait_ge(s["xsel_ready"], r + 1)
                    dve.tensor_copy(xselT[:, :, :], ps[:, 5, 0:DC * WS_ROWS].rearrange("p (c s) -> p c s", c=DC))\
                       .then_inc(s["xselT_ready"], 1)
                    dve.wait_ge(s["written"], r + 1)
                    dve.wait_ge(s["bias_loaded"], 32)
                    dve.tensor_tensor(wsum[:, :], ps[0:WS_ROWS, 2, 0:D], ws[:, :], ALU.add)
                    dve.drain()
                    dve.tensor_tensor(wsq[:, :], wsum[:, :], wsum[:, :], ALU.mult)
                    dve.drain()
                    dve.tensor_reduce(wss[:, :], wsq[:, :], AX.X, ALU.add)
                    dve.drain()
                    dve.tensor_scalar(wse[:, :], wss[:, :], 1.0 / D, WS_EPS, ALU.mult, ALU.add)\
                       .then_inc(s["wss_ready"], 1)
                    dve.wait_ge(s["wsr_ready"], r + 1)
                    dve.scalar_tensor_tensor(ws[:, :], wsum[:, :], wsr[:, 0:1], g["ws_post"][0:WS_ROWS, :],
                                             ALU.mult, ALU.mult).then_inc(s["ws_ready"], 1)
                    dve.wait_ge(s["wt_ready"], r + 1)
                    dve.tensor_copy(wsT[:, :, :], ps[:, 7, 0:DC * WS_ROWS].rearrange("p (c s) -> p c s", c=DC))\
                       .then_inc(s["wsT_ready"], 1)
                    dve.wait_ge(s["kv_ready"], r + 1)
                    for oc in range(2):
                        for hh in range(2):
                            rows = slice(64 * hh, 64 * hh + 64)
                            kv = ps[rows, 3, :].rearrange("p (v o b s) -> p v o b s", v=4, o=2, b=B)
                            dve.tensor_scalar(kbd[rows, oc, :, hh, :], kv[:, 0, oc], bias[rows, 2 + oc:3 + oc],
                                              float(WS_HD ** -0.5), ALU.add, ALU.mult)
                            last = dve.tensor_scalar(vbd[rows, oc, :, hh, :], kv[:, 1, oc], bias[rows, 4 + oc:5 + oc],
                                                     None, ALU.add)
                    last.then_inc(s["bd_ready"], 1)
                    dve.wait_ge(s["m_ready"], r + 1)
                    dve.tensor_copy(m[:, :, :, :, :].rearrange("p c o b s -> p (c o b s)"), ps[:, 4, :])
                    dve.wait_ge(s["cb_ready"], r + 1)
                    dve.tensor_copy(cb[:, :, :, :].rearrange("p o b s -> p (o b s)"), ps[0:1, 5, 0:2 * P])\
                       .then_inc(s["fold_v"], 1)
                    def shift(b):
                        dve.wait_ge(s["a_ready"], r * B + b + 1)
                        sc = ps[:, b % 2, 0:TI * WS_H * WS_S].rearrange("p (a s) -> p a s", s=WS_S)
                        dve.tensor_reduce(amax[:, b, :], sc, AX.X, ALU.max)
                        dve.drain()
                        dve.tensor_tensor(ash[:, b, :, :], sc, amax[:, b, :].unsqueeze(2).to_broadcast(
                            [P, TI * WS_H, WS_S]), ALU.subtract).then_inc(s["ash_ready"], 1)

                    def divide(b):
                        dve.wait_ge(s["ae_ready"], r * B + b + 1)
                        dve.tensor_reduce(al[:, b, :], ash[:, b, :, :], AX.X, ALU.add)
                        dve.drain()
                        dve.reciprocal(ar[:, b, :], al[:, b, :])
                        dve.drain()
                        dve.tensor_tensor(att[:, b, :, :].rearrange("p i (h s) -> p (i h) s", s=WS_S),
                                          ash[:, b, :, :],
                                          ar[:, b, :].unsqueeze(2).to_broadcast([P, TI * WS_H, WS_S]),
                                          ALU.mult).then_inc(s["att_ready"], 1)

                    def add_read(b):
                        dve.wait_ge(s["xb_ready"], r * B + b + 1)
                        for h in range(2):
                            at = b * TI + 2 * h
                            last = dve.tensor_tensor(
                                xsum[:, b % 2, 2 * h:2 * h + 2, :],
                                ps[:, 4 + 2 * (b % 2) + h, :].rearrange("p (i d) -> p i d", i=2),
                                xf[:, at:at + 2, :], ALU.add)
                        last.then_inc(s["xsum_ready"], 1)

                    def norm_sum(b):
                        dve.wait_ge(s["r2_ready"], r * B + b + 1)
                        for i in range(TI):
                            n = b * TI + i
                            last = dve.scalar_tensor_tensor(xf[:, n, :], xsum[:, b % 2, i, :], inv[:, 1, n:n + 1],
                                                            g["ws_post"][:, :], ALU.mult, ALU.mult)
                        last.then_inc(s["xf_ready"], 1)

                    shift(0)
                    shift(1)
                    divide(0)
                    shift(2)
                    divide(1)
                    add_read(0)
                    shift(3)
                    divide(2)
                    add_read(1)
                    norm_sum(0)
                    divide(3)
                    dve.drain()
                    add_read(2)
                    norm_sum(1)
                    dve.drain()
                    add_read(3)
                    norm_sum(2)
                    norm_sum(3)
                    dve.drain()
                dve.tensor_tensor(x[:, :, :], xf[:, :, :], x[:, :, :], ALU.add)

            @block.gpsimd
            def _(pool):
                nh = g["neg_half"]
                for b in range(B):
                    pool.wait_ge(s["var_ready"], b + 1)
                    pool.tensor_tensor(rstd[:, tiles(b)], ve[:, tiles(b)], nh[:, 0:TI], ALU.pow)\
                        .then_inc(s["rstd_ready"], 1)

                def row_scales(kind, b):
                    pool.tensor_tensor(mse[:, kind, tiles(b)], msq[:, kind, tiles(b)], g["ws_eps"][:, 0:TI], ALU.add)
                    pool.drain()
                    return pool.tensor_tensor(inv[:, kind, tiles(b)], mse[:, kind, tiles(b)], nh[:, 0:TI], ALU.pow)

                with pool.Fori(0, WS_NB) as r:
                    for b in range(B):
                        pool.wait_ge(s["msq_ready"], r * B + b + 1)
                        row_scales(0, b).then_inc(s["r_ready"], 1)
                    pool.wait_ge(s["wss_ready"], r + 1)
                    pool.tensor_tensor(wsr[:, :], wse[:, :], nh[0:WS_ROWS, 0:1], ALU.pow).then_inc(s["wsr_ready"], 1)
                    for b in range(B):
                        pool.wait_ge(s["m2_ready"], r * B + b + 1)
                        row_scales(1, b).then_inc(s["r2_ready"], 1)
                    pool.drain()

            @block.scalar
            def _(act):
                def mean_squares(kind, b, rows):
                    for i in range(TI):
                        last = act.activation(junk[:, i % 2, :], rows[i], ACT.Square, scale=float(D ** -0.5),
                                              accum_out=msq[:, kind, b * TI + i:b * TI + i + 1])
                        if i % 2 == 1:
                            act.drain()
                    return last

                with act.Fori(0, WS_NB) as r:
                    def copy_turned(b):
                        act.wait_ge(s["xt_ready"], r * B + b + 1)
                        for c in range(DC):
                            last = act.activation(xfT[:, c, b * S:(b + 1) * S], ps[:, 2 * (b % 2) + c, :], ACT.Copy)
                        last.then_inc(s["xfT_ready"], 1)

                    def squares(b):
                        mean_squares(0, b, [xf[:, b * TI + i, :] for i in range(TI)]).then_inc(s["msq_ready"], 1)

                    staggered(copy_turned, squares)
                    act.wait_ge(s["ntop_ready"], r + 1)
                    act.activation(etop[:, :], top[:, 0:WS_K], ACT.Exp, bias=ntop[:, 0:1])
                    act.activation(elt[:, :], lt[:, 0:S], ACT.Exp, bias=ntop[:, 0:1]).then_inc(s["exp_ready"], 1)
                    act.wait_ge(s["nb_ready"], r + 1)
                    act.activation(nb_w[0:64, :, :].rearrange("p (a b) d -> p a (b d)", a=2), ps[0:64, 6:8, :],
                                   ACT.Copy).then_inc(s["fold_a"], 1)

                    def exponents(b):
                        act.wait_ge(s["ash_ready"], r * B + b + 1)
                        act.activation(ash[:, b, :, :], ash[:, b, :, :], ACT.Exp).then_inc(s["ae_ready"], 1)

                    def copy_probs(b):
                        act.wait_ge(s["at_ready"], r * B + b + 1)
                        act.activation(attT[0:64, b, :], ps[0:64, 2 + b % 2, :], ACT.Copy)\
                           .then_inc(s["attT_ready"], 1)

                    def sum_squares(b):
                        act.wait_ge(s["xsum_ready"], r * B + b + 1)
                        mean_squares(1, b, [xsum[:, b % 2, i, :] for i in range(TI)]).then_inc(s["m2_ready"], 1)

                    staggered(exponents, copy_probs, sum_squares)

            @block.tensor
            def _(pe):
                def turn_small(out, tile, rows):
                    return pe.matmul(out, tile, ident[0:rows, 0:rows], start=True, stop=True)

                pe.wait_ge(s["setup"], 1)
                with pe.Fori(0, WS_NB) as r:
                    def turn(b):
                        pe.wait_ge(s["xf_ready"], r * B + b + 1)
                        for c in range(DC):
                            for i in range(TI):
                                last = pe.transpose(ps[:, 2 * (b % 2) + c, i * P:(i + 1) * P],
                                                    xf[:, b * TI + i, c * P:(c + 1) * P], ident[:, :])
                        last.then_inc(s["xt_ready"], 1)

                    def bid(b):
                        pe.wait_ge(s["xfT_ready"], r * B + b + 1)
                        if b >= 2:
                            pe.wait_ge(s["lg_done"], r * B + b - 1)
                        for i in range(TI):
                            for c in range(DC):
                                at = b * S + i * P
                                last = pe.matmul(ps[:, 4 + b % 2, i * WS_S:(i + 1) * WS_S], xfT[:, c, at:at + P],
                                                 cw[:, c, :], start=(c == 0), stop=(c == DC - 1))
                        last.then_inc(s["lg_ready"], 1)

                    staggered(turn, bid)
                    pe.wait_ge(s["lg_done"], r * B + B)
                    for i in range(TI):
                        last = turn_small(ps[0:WS_ROWS, 6, i * P:(i + 1) * P], lg[:, i, :], P)
                    last.then_inc(s["lt_ready"], 1)
                    pe.wait_ge(s["selw_ready"], r + 1)
                    for i in range(TI):
                        last = turn_small(ps[:, 4, i * WS_ROWS:(i + 1) * WS_ROWS], selw[:, i * P:(i + 1) * P], WS_ROWS)
                    last.then_inc(s["st_ready"], 1)
                    pe.wait_ge(s["selT_ready"], r + 1)
                    for c in range(DC):
                        for b in range(B):
                            for i in range(TI):
                                at = c * WS_ROWS + b * WS_S
                                last = pe.matmul(ps[:, 5, at:at + WS_S], xf[:, b * TI + i, c * P:(c + 1) * P],
                                                 selT[:, i, b * WS_S:(b + 1) * WS_S],
                                                 start=(i == 0), stop=(i == TI - 1))
                    last.then_inc(s["xsel_ready"], 1)
                    pe.wait_ge(s["xselT_ready"], r + 1)
                    for c in range(DC):
                        pe.matmul(ps[0:WS_ROWS, 2, 0:D], xselT[:, c, :], g["ws_write"][:, c, :], start=(c == 0),
                                  stop=False)
                    pe.matmul(ps[0:WS_ROWS, 2, 0:D], ones[:, 0:WS_ROWS], g["ws_write_b"][:, :], start=False,
                              stop=True).then_inc(s["written"], 1)
                    pe.wait_ge(s["ws_ready"], r + 1)
                    for c in range(DC):
                        last = turn_small(ps[:, 7, c * WS_ROWS:(c + 1) * WS_ROWS], ws[:, c * P:(c + 1) * P], WS_ROWS)
                    last.then_inc(s["wt_ready"], 1)
                    pe.wait_ge(s["wsT_ready"], r + 1)
                    for v, name in enumerate(("ws_wk", "ws_wv")):
                        for oc in range(2):
                            at = v * 2 * WS_ROWS + oc * WS_ROWS
                            for c in range(DC):
                                last = pe.matmul(ps[:, 3, at:at + WS_ROWS], g[name][:, c, oc * P:(oc + 1) * P],
                                                 wsT[:, c, :], start=(c == 0), stop=(c == DC - 1))
                    last.then_inc(s["kv_ready"], 1)
                    pe.wait_ge(s["bd_ready"], r + 1)
                    for c in range(DC):
                        for oc in range(2):
                            at = (c * 2 + oc) * P
                            last = pe.matmul(ps[:, 4, at:at + P], g["ws_wq"][:, oc, c * P:(c + 1) * P],
                                             kbd[:, oc, :, :, :].rearrange("p b h s -> p (b h s)"),
                                             start=True, stop=True)
                    last.then_inc(s["m_ready"], 1)
                    for oc in range(2):
                        last = pe.matmul(ps[0:1, 5, oc * P:(oc + 1) * P], bias[:, oc:oc + 1],
                                         kbd[:, oc, :, :, :].rearrange("p b h s -> p (b h s)"),
                                         start=True, stop=True)
                    last.then_inc(s["cb_ready"], 1)
                    for b in range(B):
                        for oc in range(2):
                            last = pe.matmul(ps[32 * oc:32 * oc + 32, 6 + b // 2, (b % 2) * D:(b % 2 + 1) * D],
                                             vbd[:, oc, b, :, :].rearrange("p h s -> p (h s)"),
                                             g["ws_out"][:, oc, :], start=True, stop=True)
                    last.then_inc(s["nb_ready"], 1)

                    def scores(b):
                        if b == 0:
                            pe.wait_ge(s["fold_v"], r + 1)
                        for i in range(TI):
                            out = ps[:, b % 2, i * 64:(i + 1) * 64].rearrange("p (o s) -> p o s", o=2)
                            for c in range(DC):
                                at = b * S + i * P
                                pe.matmul(out, xfT[:, c, at:at + P], m[:, c, :, b, :], start=(c == 0), stop=False)
                            last = pe.matmul(out, ones[:, :], cb[:, :, b, :], start=False, stop=True)
                        last.then_inc(s["a_ready"], 1)

                    def turn_probs(b):
                        pe.wait_ge(s["att_ready"], r * B + b + 1)
                        for i in range(TI):
                            last = turn_small(ps[0:64, 2 + b % 2, i * P:(i + 1) * P], att[:, b, i, :], P)
                        last.then_inc(s["at_ready"], 1)

                    def read(b):
                        if b == 0:
                            pe.wait_ge(s["fold_a"], r + 1)
                        pe.wait_ge(s["attT_ready"], r * B + b + 1)
                        if b >= 2:
                            pe.wait_ge(s["xsum_ready"], r * B + b - 1)
                        for i in range(TI):
                            last = pe.matmul(ps[:, 4 + 2 * (b % 2) + i // 2, (i % 2) * D:(i % 2 + 1) * D],
                                             attT[:, b, i * P:(i + 1) * P], nb_w[:, b, :], start=True, stop=True)
                        last.then_inc(s["xb_ready"], 1)

                    staggered(scores, turn_probs, read)
        k.clear_sems()


LORA_N, LORA_RANK = 4, 16
LORA_ROWS = LORA_N * LORA_RANK
LORA_H = 16
LORA_HD = D // LORA_H
LORA_SCALE = float(LORA_HD ** -0.5)
LORA_BLOCKS = P // LORA_HD
LORA_PART_1 = (slice(0, 3), slice(1, 6, 2))
LORA_PART_2 = (slice(3, 5), slice(2, 5, 2))
LORA_PART_3 = (5, 0)
LORA_BOTH_1, LORA_BOTH_2 = 1, 4


def lora_attention(nc, g):
    with ExitStack() as ctx:
        k = Kit(nc, ctx)
        x, ident, ident_b, mask_b, rope = (g[n] for n in ("x", "ident", "ident_b", "mask_b", "lora_rope"))
        ln = Normed(k, "lora")
        starts = k.sb("lora_startf", [LORA_ROWS, LORA_N])
        begun = k.sb("lora_begun", [LORA_ROWS, B, LORA_N])
        which = k.sb("lora_which", [LORA_ROWS, B])
        mine = k.sb("lora_mine", [LORA_ROWS, B])
        am = k.sb("lora_am", [LORA_ROWS, 4, D])
        w = k.sb("lora_w", [P, DC, 4, D])
        rot = k.sb("lora_rot", [P, 2, 2 * D])
        qk = k.sb("lora_qk", [P, TI, 2 * LORA_H, LORA_HD])
        rest = k.sb("lora_rest", [P, TI, 2 * LORA_H, LORA_HD])
        parts = k.sb("lora_parts", [P, TI, 2 * LORA_H, LORA_BLOCKS, LORA_HD], BF16)
        qkT = k.sb("lora_qkT", [P, 2, 2, S], BF16)
        v = k.sb("lora_v", [P, TI, D])
        nmax = k.sb("lora_nmax", [P, 2, TI])
        lsum = k.sb("lora_lsum", [P, LORA_H, TI])
        rl = k.sb("lora_rl", [P, 2, TI])
        probs = g["cos_wout"][:, :, :].rearrange("p h d -> p (h d)")[:, 0:2 * CAUSAL_COLS]\
            .rearrange("p (j c) -> p j c", j=2)
        probsT = k.sb("lora_probsT", [P, 2, CAUSAL_COLS])
        on = k.sb("lora_on", [P, TI, LORA_H, LORA_HD])
        onT = ln.xnT
        sc = k.ps("lora_sc", [P, 2, 3 * 512])
        po = k.ps("lora_po", [P, 512])
        tq = k.ps("lora_tq", [P, 2, S], BF16)
        out2 = po[:, 0:2 * TI * LORA_HD].rearrange("p (j q c) -> p j q c", j=2, q=TI)

        def bank(n):
            return sc[:, n // 3, (n % 3) * 512:(n % 3 + 1) * 512] if n < 6 else po[:, :]

        fold_bank = {"q": 4, "k": 5, "v": 6, "o": 6}
        row_banks = [bank(0), bank(1)]
        qk_bank = (4, 5, 0, 1)

        names = ("am_ready", "fold_ready", "w_ready", "wo_ready", "v_ready", "v_copied", "pj_ready", "pj_read", "part1_ready",
                 "rest_ready", "rest2_ready", "part2_ready", "part3_ready", "qk_rotated", "tq_ready", "tq_read",
                 "s_ready", "max_ready", "e_ready", "t_ready", "pt_a", "pt_b", "o_ready", "o_done", "ot_ready",
                 "onT_ready", "y_ready", "x_done")
        s = {n: k.sem("lora_" + n) for n in names}
        PAIRS = LORA_H // 2

        with nc.Block() as block:
            @block.vector
            def _(dve):
                dve.nop().then_inc(s["o_done"], 1)
                dve.tensor_copy(starts[:, :], g["lora_starts"][:, :])
                dve.tensor_scalar(g["lora_wq"][:, :, :], g["lora_wq"][:, :, :], LORA_SCALE, None, ALU.mult)
                dve.memset(parts[:, :, :, 6:LORA_BLOCKS, :], 0.0)
                dve.drain()
                dve.tensor_tensor(begun[:, :, :], starts[:, :].unsqueeze(1).to_broadcast([LORA_ROWS, B, LORA_N]),
                                  g["lora_batch"][:, :].unsqueeze(2).to_broadcast([LORA_ROWS, B, LORA_N]), ALU.is_le)
                dve.drain()
                dve.tensor_reduce(which[:, :], begun[:, :, :], AX.X, ALU.add)
                dve.drain()
                dve.tensor_scalar(mine[:, :], which[:, :], -1.0, 0.0, ALU.add, ALU.max)
                dve.drain()
                dve.tensor_scalar(which[:, :], mine[:, :], float(LORA_N - 1), None, ALU.min)
                dve.drain()
                dve.tensor_scalar(mine[:, :], which[:, :], g["lora_row"][:, 0:1], None, ALU.is_equal)
                dve.drain()

                def masked_adapters(b):
                    for n, name in enumerate("qkvo"):
                        last = dve.tensor_scalar(am[:, n, :], g["lora_a" + name][:, :], mine[:, bass.ds(b, 1)],
                                                 LORA_SCALE if name == "q" else 1.0, ALU.mult, ALU.mult)
                    last.then_inc(s["am_ready"], 1)
                    ln.norm(dve, x, b)

                def weights(names, b, ready):
                    for name in names:
                        n = "qkvo".index(name)
                        dve.wait_ge(s["fold_ready"], 4 * b + n + 1)
                        last = dve.tensor_tensor(w[:, :, n, :],
                                                 bank(fold_bank[name]).rearrange("p (c d) -> p c d", c=DC),
                                                 g["lora_w" + name][:, :, :], ALU.add)
                        last.then_inc(s[ready], 1)

                def batch(b, more):
                    for i in range(TI):
                        dve.wait_ge(s["pj_ready"], b * TI + i + 1)
                        values = bank(qk_bank[i]).rearrange("p (n e f) -> p n e f", e=2, f=LORA_HD // 2)
                        cos = rope[:, i, 0, 0, :].unsqueeze(1).to_broadcast([P, 4 * LORA_H, LORA_HD // 2])
                        dve.tensor_tensor(rot[:, 0, :].rearrange("p (n f) -> p n f", f=LORA_HD // 2),
                                          bank(qk_bank[i]).rearrange("p (n f) -> p n f", f=LORA_HD // 2), cos,
                                          ALU.mult)
                        for e in range(2):
                            sin = rope[:, i, 1, e, :].unsqueeze(1).to_broadcast([P, 2 * LORA_H, LORA_HD // 2])
                            last = dve.tensor_tensor(
                                rot[:, 1, :].rearrange("p (n e f) -> p n e f", e=2, f=LORA_HD // 2)[:, :, e, :],
                                values[:, :, 1 - e, :], sin, ALU.mult)
                        last.then_inc(s["pj_read"], 1)
                        dve.drain()
                        dve.tensor_tensor(qk[:, i, :, :].rearrange("p n c -> p (n c)"), rot[:, 0, :], rot[:, 1, :],
                                          ALU.add).then_inc(s["qk_rotated"], 1)
                        if i == 0:
                            dve.wait_ge(s["part1_ready"], b * TI + 1)
                            dve.tensor_tensor(rest[:, 0, :, :], qk[:, 0, :, :], parts[:, 0, :, LORA_BOTH_1, :],
                                              ALU.subtract).then_inc(s["rest_ready"], 1)
                        dve.drain()
                    for i in range(1, TI):
                        dve.wait_ge(s["part1_ready"], b * TI + i + 1)
                        dve.tensor_tensor(rest[:, i, :, :], qk[:, i, :, :], parts[:, i, :, LORA_BOTH_1, :],
                                          ALU.subtract).then_inc(s["rest_ready"], 1)
                    for i in range(TI):
                        dve.wait_ge(s["part2_ready"], b * TI + i + 1)
                        for n in range(2):
                            heads = slice(n * LORA_H, (n + 1) * LORA_H)
                            last = dve.tensor_tensor(parts[:, i, heads, LORA_PART_3[n], :], rest[:, i, heads, :],
                                                     parts[:, i, heads, LORA_BOTH_2, :], ALU.subtract)
                        last.then_inc(s["part3_ready"], 1)

                    def maxima(n, j):
                        for qi in CAUSAL_ORDER:
                            if qi != 0:
                                dve.wait_ge(s["s_ready"], 3 * n + CAUSAL_BANK[qi] + 1)
                            at = CAUSAL_COL[qi]
                            red = dve.tensor_reduce(nmax[:, j, qi:qi + 1], sc[:, j, at:at + (qi + 1) * P],
                                                    AX.X, ALU.max, negate=True)
                            if qi != 2:
                                red.then_inc(s["max_ready"], 1)

                    def head(p, j, normalise, more):
                        n = b * LORA_H + 2 * p + j
                        dve.wait_ge(s["t_ready"], 3 * n + 2)
                        dve.tensor_copy(probsT[:, j, S:2 * S], sc[:, j, S:2 * S])
                        dve.wait_ge(s["t_ready"], 3 * n + 3)
                        dve.tensor_copy(probsT[:, j, 2 * S:CAUSAL_COLS],
                                        sc[:, j, 2 * S:CAUSAL_COLS]).then_inc(s["pt_b"], 1)
                        if more:
                            maxima(n + 1, 1 - j)
                        if normalise:
                            weigh(p - 1)

                    def weigh(p):
                        dve.wait_ge(s["o_ready"], b * PAIRS + p + 1)
                        dve.reciprocal(rl[:, :, :], lsum[:, bass.ds(2 * p, 2), :])
                        dve.drain()
                        dve.tensor_tensor(on[:, :, bass.ds(2 * p, 2), :].rearrange("p q j r -> p j q r"),
                                          out2, rl[:, :, :].unsqueeze(3).to_broadcast([P, 2, TI, LORA_HD]),
                                          ALU.mult).then_inc(s["o_done"], 1)

                    maxima(b * LORA_H, 0)
                    head(0, 0, False, True)
                    head(0, 1, False, True)
                    with dve.Fori(1, PAIRS - 1) as p:
                        head(p, 0, True, True)
                        head(p, 1, False, True)
                    if more:
                        masked_adapters(b + 1)
                    head(PAIRS - 1, 0, True, True)
                    head(PAIRS - 1, 1, False, False)
                    weigh(PAIRS - 1)
                    if more:
                        weights("qkv", b + 1, "w_ready")
                    dve.wait_ge(s["y_ready"], b + 1)
                    for i in range(TI):
                        xi = x[:, b * TI + i, :]
                        last = dve.tensor_tensor(xi, bank(2 + i // 2)[:, (i % 2) * D:(i % 2 + 1) * D], xi, ALU.add)
                    last.then_inc(s["x_done"], 1)
                    if more:
                        weights("o", b + 1, "wo_ready")

                dve.nop().then_inc(s["x_done"], 1)
                masked_adapters(0)
                weights("qkv", 0, "w_ready")
                weights("o", 0, "wo_ready")
                with dve.Fori(0, B - 1) as b:
                    batch(b, True)
                batch(B - 1, False)

            @block.gpsimd
            def _(pool):
                with pool.Fori(0, B) as b:
                    ln.invert(pool, g, b)

            @block.scalar
            def _(act):
                act.nop().then_inc(s["tq_read"], 1)

                def batch(b, more):
                    def part_1(i):
                        act.wait_ge(s["qk_rotated"], b * TI + i + 1)
                        for n in range(2):
                            heads = slice(n * LORA_H, (n + 1) * LORA_H)
                            last = act.activation(parts[:, i, heads, LORA_PART_1[n], :],
                                                  qk[:, i, heads, :].unsqueeze(2)
                                                  .to_broadcast([P, LORA_H, 3, LORA_HD]), ACT.Copy)
                        last.then_inc(s["part1_ready"], 1)

                    def part_2(i):
                        act.wait_ge(s["rest_ready"], b * TI + i + 1)
                        for n in range(2):
                            heads = slice(n * LORA_H, (n + 1) * LORA_H)
                            last = act.activation(parts[:, i, heads, LORA_PART_2[n], :],
                                                  rest[:, i, heads, :].unsqueeze(2)
                                                  .to_broadcast([P, LORA_H, 2, LORA_HD]), ACT.Copy)
                        last.then_inc(s["part2_ready"], 1)

                    for i in range(TI):
                        part_1(i)
                        if i == 0:
                            act.wait_ge(s["v_ready"], b + 1)
                            for h in range(2):
                                last = act.activation(v[:, 2 * h:2 * h + 2, :].rearrange("p i d -> p (i d)"),
                                                      bank(2 + h), ACT.Copy)
                            last.then_inc(s["v_copied"], 1)
                    for i in range(TI):
                        part_2(i)

                    def turned(n, j):
                        act.wait_ge(s["tq_ready"], n + 1)
                        act.activation(qkT[:, j, :, :], tq[:, :, :], ACT.Copy).then_inc(s["tq_read"], 1)

                    def exponents(n, h, j):
                        for qi in CAUSAL_ORDER:
                            if qi != 0:
                                act.wait_ge(s["max_ready"], 3 * n + CAUSAL_BANK[qi] + 1)
                            at = CAUSAL_COL[qi]
                            ex = act.activation(probs[:, j, at:at + (qi + 1) * P], sc[:, j, at:at + (qi + 1) * P],
                                                ACT.Exp, bias=nmax[:, j, qi:qi + 1],
                                                accum_out=lsum[:, bass.ds(h, 1), qi])
                            if qi != 2:
                                ex.then_inc(s["e_ready"], 1)

                    def head(p, j, more, turns):
                        n = b * LORA_H + 2 * p + j
                        act.wait_ge(s["t_ready"], 3 * n + 1)
                        act.activation(probsT[:, j, 0:S], sc[:, j, 0:S], ACT.Copy).then_inc(s["pt_a"], 1)
                        if more:
                            exponents(n + 1, 2 * p + j + 1, 1 - j)
                        if turns:
                            turned(n + 2, j)

                    turned(b * LORA_H, 0)
                    turned(b * LORA_H + 1, 1)
                    exponents(b * LORA_H, 0, 0)
                    with act.Fori(0, PAIRS - 1) as p:
                        head(p, 0, True, True)
                        head(p, 1, True, True)
                    head(PAIRS - 1, 0, True, False)
                    head(PAIRS - 1, 1, False, False)
                    act.wait_ge(s["ot_ready"], b + 1)
                    for c in range(DC):
                        last = act.activation(onT[:, c, :], bank(c), ACT.Copy)
                    last.then_inc(s["onT_ready"], 1)
                    if more:
                        ln.copy(act, row_banks, b + 1)

                ln.copy(act, row_banks, 0)
                with act.Fori(0, B - 1) as b:
                    batch(b, True)
                batch(B - 1, False)

            @block.tensor
            def _(pe):
                ln.first_free(pe)

                def fold(names, b):
                    pe.wait_ge(s["am_ready"], b + 1)
                    for name in names:
                        n = "qkvo".index(name)
                        for c in range(DC):
                            last = pe.matmul(bank(fold_bank[name])[:, c * D:(c + 1) * D],
                                             am[:, n, c * P:(c + 1) * P], g["lora_b" + name][:, :],
                                             start=True, stop=True)
                        last.then_inc(s["fold_ready"], 1)

                def batch(b, more):
                    pe.wait_ge(s["w_ready"], 3 * b + 3)
                    fold("o", b)
                    pe.wait_ge(ln.xnT_ready, b + 1)
                    for i in range(TI):
                        for c in range(DC):
                            last = pe.matmul(bank(qk_bank[i]), ln.xnT[:, c, i * P:(i + 1) * P],
                                             w[:, c, 0:2, :].rearrange("p n d -> p (n d)"),
                                             start=(c == 0), stop=(c == DC - 1))
                        last.then_inc(s["pj_ready"], 1)
                    pe.wait_ge(s["x_done"], b + 1)
                    for i in range(TI):
                        for c in range(DC):
                            last = pe.matmul(bank(2 + i // 2)[:, (i % 2) * D:(i % 2 + 1) * D],
                                             ln.xnT[:, c, i * P:(i + 1) * P], w[:, c, 2, :],
                                             start=(c == 0), stop=(c == DC - 1))
                    last.then_inc(s["v_ready"], 1)

                    def turn(h):
                        n = b * LORA_H + h
                        pe.wait_ge(s["tq_read"], n + 1)
                        for kind in range(2):
                            for i in range(TI):
                                last = pe.transpose(tq[:, kind, i * P:(i + 1) * P],
                                                    parts[:, i, bass.ds(kind * LORA_H + h, 1), :, :]
                                                    .rearrange("p n u c -> p (n u c)"), ident_b[:, :])
                        last.then_inc(s["tq_ready"], 1)

                    def scores(n, j):
                        pe.wait_ge(s["tq_read"], n + 2)
                        for qi in CAUSAL_ORDER:
                            at = CAUSAL_COL[qi]
                            pe.matmul(sc[:, j, at:at + (qi + 1) * P], qkT[:, j, 0, qi * P:(qi + 1) * P],
                                      qkT[:, j, 1, 0:(qi + 1) * P], start=True, stop=False)
                            last = pe.matmul(sc[:, j, at + qi * P:at + (qi + 1) * P], ident_b[:, :], mask_b[:, :],
                                             start=False, stop=True)
                            if qi != 2:
                                last.then_inc(s["s_ready"], 1)

                    def turn_probs(n, j):
                        for qi in CAUSAL_ORDER:
                            if qi != 0:
                                pe.wait_ge(s["e_ready"], 3 * n + CAUSAL_BANK[qi] + 1)
                            for kj in range(qi + 1):
                                at = CAUSAL_COL[qi] + kj * P
                                last = pe.transpose(sc[:, j, at:at + P], probs[:, j, at:at + P], ident[:, :])
                            if qi != 2:
                                last.then_inc(s["t_ready"], 1)

                    def outputs(n, h, j, pairs_done):
                        for qi in range(TI):
                            for kj in range(qi + 1):
                                at = CAUSAL_COL[qi] + kj * P
                                last = pe.matmul(out2[:, j, qi, :], probsT[:, j, at:at + P],
                                                 v[:, kj, bass.ds(h * LORA_HD, LORA_HD)],
                                                 start=(kj == 0), stop=(kj == qi))
                        if j == 1:
                            last.then_inc(s["o_ready"], 1)

                    def head(p, j, before, after, turns):
                        h = 2 * p + j
                        n = b * LORA_H + h
                        turn_probs(n, j)
                        if before:
                            pe.wait_ge(s["pt_a"], n)
                            pe.wait_ge(s["pt_b"], n)
                        if after:
                            scores(n + 1, 1 - j)
                        if before:
                            if j == 1:
                                pe.wait_ge(s["o_done"], b * PAIRS + p + 1)
                            outputs(n - 1, h - 1, 1 - j, p)
                        if turns:
                            turn(h + 2)

                    pe.wait_ge(s["part3_ready"], b * TI + TI)
                    turn(0)
                    turn(1)
                    pe.wait_ge(s["v_copied"], b + 1)
                    scores(b * LORA_H, 0)
                    head(0, 0, False, True, True)
                    head(0, 1, True, True, True)
                    with pe.Fori(1, PAIRS - 1) as p:
                        head(p, 0, True, True, True)
                        head(p, 1, True, True, True)
                    head(PAIRS - 1, 0, True, True, False)
                    head(PAIRS - 1, 1, True, False, False)
                    pe.wait_ge(s["pt_a"], (b + 1) * LORA_H)
                    pe.wait_ge(s["pt_b"], (b + 1) * LORA_H)
                    outputs(b * LORA_H + LORA_H - 1, LORA_H - 1, 1, PAIRS)

                    pe.wait_ge(s["o_done"], b * PAIRS + PAIRS + 1)
                    for c in range(DC):
                        for i in range(TI):
                            last = pe.transpose(bank(c)[:, i * P:(i + 1) * P],
                                                on[:, i, 8 * c:8 * c + 8, :].rearrange("p h e -> p (h e)"), ident[:, :])
                    last.then_inc(s["ot_ready"], 1)
                    if more:
                        fold("qkv", b + 1)
                    pe.wait_ge(s["onT_ready"], b + 1)
                    pe.wait_ge(s["wo_ready"], b + 1)
                    for i in range(TI):
                        for c in range(DC):
                            last = pe.matmul(bank(2 + i // 2)[:, (i % 2) * D:(i % 2 + 1) * D],
                                             onT[:, c, i * P:(i + 1) * P], w[:, c, 3, :],
                                             start=(c == 0), stop=(c == DC - 1))
                    last.then_inc(s["y_ready"], 1)
                    if more:
                        ln.turn(pe, g, row_banks, b + 1)

                fold("qkv", 0)
                ln.turn(pe, g, row_banks, 0)
                with pe.Fori(0, B - 1) as b:
                    batch(b, True)
                batch(B - 1, False)
        k.clear_sems()


def rope_tables(length, dim, theta=10000.0):
    inv = (1.0 / theta ** (np.arange(0, dim, 2, dtype=np.float32) / np.float32(dim))).astype(np.float32)
    ang = np.arange(length, dtype=np.float32)[:, None] * inv
    return np.cos(ang).astype(np.float32), np.sin(ang).astype(np.float32)


def shape_constants():
    c = {}
    c["ident"] = np.eye(P, dtype=np.float32)
    causal = np.where(np.arange(P)[None, :] <= np.arange(P)[:, None], 0.0, NEG).astype(np.float32)
    c["mask"] = causal
    cos, sin = rope_tables(S, MLA_DR)
    q = np.arange(2)[:, None, None]
    e = np.arange(2)[None, :, None]
    r = np.arange(16)[None, None, :]
    freq = (16 * q + r + 0 * e).reshape(-1)
    sign = np.where(e + 0 * (q + r) == 0, -1.0, 1.0).reshape(-1).astype(np.float32)
    cn, sn = cos[:, freq], sin[:, freq] * sign
    t = np.stack([cn, sn], 1)
    c["ropeN"] = t.reshape(TI, P, 2, MLA_DR).transpose(1, 0, 2, 3)
    c["ropeT"] = np.concatenate([t, t], 2).transpose(2, 1, 0)
    hj, hk = np.arange(P) // 8, np.arange(P) // 8
    same = (hj[:, None] == hk[None, :])
    c["gla_sel"] = np.stack([same & (np.arange(P)[:, None] % 8 == j) for j in range(8)], 1).astype(np.float32)
    edge = np.zeros((P, P - GLA_H), bool)
    c["gla_hsum"] = np.concatenate([edge, hk[:, None] == np.arange(GLA_H)[None, :], edge], 1).astype(np.float32)
    c["gla_same"] = (np.arange(P)[:, None] % GLA_H == np.arange(P)[None, :] % GLA_H).astype(np.float32)
    cos, sin = rope_tables(S, LORA_HD)
    t = np.stack([np.stack([cos, cos], 1), np.stack([-sin, sin], 1)], 1)
    c["lora_rope"] = t.reshape(TI, P, 2, 2, LORA_HD // 2).transpose(1, 0, 2, 3, 4)
    c["lora_row"] = (np.arange(LORA_ROWS)[:, None] // LORA_RANK).astype(np.float32)
    c["lora_batch"] = np.tile(np.arange(B, dtype=np.float32), (LORA_ROWS, 1))
    return {n: np.ascontiguousarray(a) for n, a in c.items()}


MLA_PE = np.array([2 * (16 * q + r) + e for q in range(2) for e in range(2) for r in range(16)])


def chunked(a):
    return a.reshape(-1, P, *a.shape[1:]).swapaxes(0, 1)


def lay_out(i):
    w = {}
    w["x"] = i["L0_attn_a_x"].reshape(NT, P, D).transpose(1, 0, 2)
    wq = i["L0_attn_a_wq"].reshape(D, MLA_H, MLA_DN + MLA_DR)
    w["mla_wqT"] = wq[:, :, :MLA_DN].transpose(2, 1, 0)
    pe = wq[:, :, MLA_DN:][:, :, MLA_PE].reshape(D, MLA_PAIRS, 2, MLA_DR)[:, :, ::-1]
    w["mla_wq_pe"] = chunked(pe.reshape(D, MLA_PAIRS, P))
    wkvb = i["L0_attn_a_wkv_b"].reshape(MLA_R, MLA_H, 2 * P)
    w["mla_wkT"] = wkvb[:, :, :P].transpose(2, 1, 0)
    w["mla_wvT"] = wkvb[:, :, P:].transpose(2, 1, 0)
    w["mla_wo"] = i["L0_attn_a_wo"].reshape(MLA_H, P, D).transpose(1, 0, 2)
    kva = i["L0_attn_a_wkv_a"]
    w["wkva"] = chunked(np.concatenate([kva[:, :MLA_R], kva[:, MLA_R:][:, MLA_PE]], 1))
    w["kvw"] = np.broadcast_to(i["L0_attn_a_kv_norm_w"], (P, MLA_R))
    w["ffn_w"] = chunked(i["L0_ffn_weight"])
    w["ffn_scale"] = np.broadcast_to(i["L0_ffn_scale"], (P, D))
    w["cos_g"] = chunked(i["L0_attn_b_g_norm"])
    w["cos_wq"] = chunked(i["L0_attn_b_Wq"])
    w["cos_wkv"] = chunked(i["L0_attn_b_Wkv"])
    w["cos_wout"] = chunked(i["L0_attn_b_Wout"])
    w["cos_gout"] = np.broadcast_to(i["L0_attn_b_g_out"], (P, D))
    for n, name in (("gla_wq", "Wq"), ("gla_wk", "Wk"), ("gla_wgk1", "Wgk1")):
        w[n] = chunked(i["L1_attn_a_" + name])
    wv = i["L1_attn_a_Wv"].reshape(D, GLA_H, 2, 8)
    w["gla_wv"] = chunked(wv.transpose(0, 2, 1, 3).reshape(D, D))
    w["gla_wg"] = chunked(i["L1_attn_a_Wg"].reshape(D, GLA_H, GLA_DV).swapaxes(1, 2).reshape(D, D))
    w["gla_wgk2"] = i["L1_attn_a_Wgk2"]
    w["gla_bgk2"] = i["L1_attn_a_bgk2"].reshape(P, 1)
    w["gla_normw"] = np.repeat(i["L1_attn_a_norm_w"].reshape(2, GLA_HALF), GLA_H, axis=1).T
    w["gla_wo"] = chunked(i["L1_attn_a_Wo"].reshape(GLA_H, GLA_DV, D).swapaxes(0, 1).reshape(D, D))
    def f(name):
        return i["L1_ffn_" + name]

    def slots(a):
        return np.broadcast_to(a, (B, *a.shape)).reshape(B * WS_S, -1)

    w["ws_start"] = slots(f("workspace"))
    w["ws_cw"] = chunked(f("compete_w").T)
    w["ws_cb"] = slots(f("compete_b")[:, None])
    w["ws_write"] = chunked(f("write_w").T)
    w["ws_write_b"] = f("write_b")[None]
    wq, wk, wv = f("in_proj_w")[:D], f("in_proj_w")[D:2 * D], f("in_proj_w")[2 * D:]
    w["ws_wq"], w["ws_wk"], w["ws_wv"] = chunked(wq), chunked(wk.T), chunked(wv.T)
    w["ws_in_b"] = chunked(f("in_proj_b"))
    w["ws_out"] = chunked(f("out_proj_w").T)
    w["ws_out_b"] = np.broadcast_to(f("out_proj_b"), (1, B, D))
    w["ws_pre"] = chunked(f("norm_pre_w"))
    w["ws_post"] = np.broadcast_to(f("norm_post_w"), (P, D))
    eo = (np.arange(LORA_H)[:, None, None] * LORA_HD + 2 * np.arange(8)[None, None, :]
          + np.arange(2)[None, :, None]).reshape(-1)
    for n in "qkvo":
        wt, bt = i["L1_attn_b_W" + n].T, i["L1_attn_b_B" + n].transpose(0, 2, 1).reshape(LORA_ROWS, D)
        if n in ("q", "k"):
            wt, bt = wt[:, eo], bt[:, eo]
        w["lora_w" + n], w["lora_b" + n] = chunked(wt), bt
        w["lora_a" + n] = i["L1_attn_b_A" + n].reshape(LORA_ROWS, D)
    w["lora_starts"] = np.broadcast_to(i["L1_attn_b_lora_start_indices"], (LORA_ROWS, LORA_N))
    w.update(shape_constants())
    return {n: np.ascontiguousarray(a) for n, a in w.items()}


def build(nc, w, out, stages=None):
    with ExitStack() as ctx:
        k = Kit(nc, ctx)
        g = {"x": k.sb("x", [P, NT, D]), "ident": k.sb("ident", [P, P]),
             "ident_b": k.sb("ident_b", [P, P], BF16), "mask_b": k.sb("mask_b", [P, P], BF16),
             "neg_half": k.sb("neg_half", [P, 64]), "pos_half": k.sb("pos_half", [P, 64]),
             "ws_eps": k.sb("ws_eps", [P, TI])}
        for n in ("x_loaded", "weights_loaded", "late_loaded", "consts_loaded"):
            g[n] = k.sem(n)
        def hold(names, loaded):
            for n in names:
                g[n] = k.sb(n, list(w[n].shape), w[n].dtype)
            return [(g[n][tuple(slice(None) for _ in w[n].shape)], w[n], loaded) for n in names]

        early = ["ffn_w", "ffn_scale", "cos_g", "cos_wq", "cos_wkv", "cos_wout", "cos_gout"]
        g["early_loads"] = hold(early, g["weights_loaded"])
        with ExitStack() as mla_ctx:
            m = Kit(nc, mla_ctx)
            g["wap"] = m.sb("wap", [P, DC, MLA_PAIRS, 2, P])
            g["wvo"] = m.sb("wvo", [P, MLA_PAIRS, D])
            g["wq_pe"] = m.sb("wq_pe", [P, DC, MLA_PAIRS, P])
            first = ["mask", "wkva", "kvw", "ropeT", "ropeN"]
            for n in first:
                g[n] = m.sb(n, list(w[n].shape))
            g["first_loads"] = [(g[n][tuple(slice(None) for _ in w[n].shape)], n) for n in ["ident"] + first]
            mla_fold_weights(nc, g, w)
            small_constants(nc, g)
            mla_attention(nc, g)
        late = ["gla_wq", "gla_wk", "gla_wgk1", "gla_wv", "gla_wg", "gla_wgk2", "gla_bgk2", "gla_normw", "gla_wo",
                "gla_sel", "gla_hsum", "gla_same", "ws_start", "ws_cw", "ws_cb", "ws_write", "ws_write_b", "ws_wq", "ws_wk",
                "ws_wv", "ws_in_b", "ws_out", "ws_out_b", "ws_pre", "ws_post",
                "lora_wq", "lora_wk", "lora_wv", "lora_wo", "lora_aq", "lora_ak", "lora_av", "lora_ao",
                "lora_bq", "lora_bk", "lora_bv", "lora_bo", "lora_starts", "lora_rope", "lora_row", "lora_batch"]
        wait_for_loads(nc, g["weights_loaded"], len(early))
        ternary_ffn(nc, g, "ffa", hold(late, g["late_loaded"]))
        cosine_attention(nc, g)
        ternary_ffn(nc, g, "ffb", [])
        wait_for_loads(nc, g["late_loaded"], len(late))
        gated_linear_attention(nc, g)
        workspace_ffn(nc, g, "wsa")
        lora_attention(nc, g)
        workspace_ffn(nc, g, "wsb")
        store_output(nc, g, out)


def wait_for_loads(nc, loaded, count):
    with nc.Block() as block:
        @block.sync
        def _(sp):
            sp.wait_ge(loaded, 16 * count)


def small_constants(nc, g):
    with nc.Block() as block:
        @block.vector
        def _(dve):
            dve.memset(g["neg_half"][:, :], -0.5)
            dve.memset(g["pos_half"][:, :], 0.5)
            dve.memset(g["ws_eps"][:, :], WS_EPS)
            dve.wait_ge(g["consts_loaded"], 16 * len(g["first_loads"]))
            dve.tensor_copy(g["ident_b"][:, :], g["ident"][:, :])
            dve.tensor_copy(g["mask_b"][:, :], g["mask"][:, :])


def store_output(nc, g, out):
    with ExitStack() as ctx:
        stored = Kit(nc, ctx).sem("stored")
        with nc.Block() as block:
            @block.sync
            def _(sp):
                sp.dma_start(out.rearrange("b (i p) d -> p (b i) d", p=P), g["x"][:, :, :]).then_inc(stored, 16)
                sp.wait_ge(stored, 16)


def kernel(**inputs):
    import concourse.bacc as bacc
    from concourse.bass_utils import run_bass_kernel_spmd

    nc = bacc.Bacc("TRN2", target_bir_lowering=False, num_devices=1)
    arrays = lay_out({n: np.asarray(a) for n, a in inputs.items()})
    w = {n: nc.dram_tensor("in_" + n, a.shape, mybir.dt.from_np(a.dtype), kind="ExternalInput").ap()
         for n, a in arrays.items()}
    out = nc.dram_tensor("out_0", (B, S, D), F32, kind="ExternalOutput").ap()
    build(nc, w, out)
    r = run_bass_kernel_spmd(nc, [{"in_" + n: a for n, a in arrays.items()}], core_ids=[0])
    return r.results[0]["out_0"]
```
